# Optimizing a Trainium2 kernel written in Bass

```python
import numpy as np
import jax
import jax.numpy as jnp

def _softmax(x, axis=-1):
    return jax.nn.softmax(x, axis=axis)

def _gelu(x):
    return jax.nn.gelu(x, approximate=True)

def _silu(x):
    return jax.nn.silu(x)

def _sigmoid(x):
    return jax.nn.sigmoid(x)

def _layernorm(x, axis=-1, eps=1e-05):
    m = jnp.mean(x, axis=axis, keepdims=True)
    v = jnp.var(x, axis=axis, keepdims=True)
    return (x - m) / jnp.sqrt(v + eps)

def _scatter_add(tgt, idx, src, axis=0):
    return tgt.at[idx].add(src)

def _segment_sum(src, seg, n):
    return jax.ops.segment_sum(src, seg, n)
kernel_name = 'mk_vit_tower_d2_tok_img512_r4_d0b078'

def setup_inputs(seed: int=0):
    np.random.seed(seed)
    _w = jnp.asarray

    def _rec_inputs():
        import jax
        import jax.numpy as jnp
        _rk = jax.random.key(seed)
        x = -0.000356955 + 1 * jax.random.normal(jax.random.fold_in(_rk, 1), (64, 3, 96, 96), jnp.float32)
        return x
    x = _rec_inputs()

    def _L0_tok_setup():
        import jax, jax.numpy as jnp
        import numpy as np
        key = jax.random.key(seed)
        k1, k2, k3 = jax.random.split(key, 3)
        B, C, H, W = (128, 3, 224, 224)
        E, p = (128, 16)
        K = C * p * p
        img = jax.random.normal(k1, (B, C, H, W), dtype=jnp.float32)
        w = jax.random.normal(k2, (E, K), dtype=jnp.float32) * (1.0 / np.sqrt(K))
        b = jax.random.normal(k3, (E,), dtype=jnp.float32)
        return {'img': img, 'w': w, 'b': b, 'patch_size': p}
    _L0_tok_all = _L0_tok_setup()
    _L0_tok_in = {k: v for k, v in _L0_tok_all.items() if k in ('w', 'b')}
    del _L0_tok_all

    def _L0_attn_setup():
        import jax, jax.numpy as jnp
        import numpy as np

        def _rel_shift(x):
            T = x.shape[2]
            i = jnp.arange(T)[:, None]
            j = jnp.arange(T)[None, :]
            idx = j + (T - 1) - i
            return jnp.take_along_axis(x, idx[None, None, :, :], axis=-1)
        key = jax.random.key(seed)
        ks = jax.random.split(key, 8)
        L, B, E, H = (256, 8, 128, 8)
        hd = E // H
        s = 0.02
        return {'query': jax.random.normal(ks[0], (L, B, E), jnp.float32), 'pos_emb': jax.random.normal(ks[1], (1, 2 * L - 1, E), jnp.float32), 'in_proj_w': jax.random.normal(ks[2], (3 * E, E), jnp.float32) * s, 'in_proj_b': jnp.zeros((3 * E,), jnp.float32), 'out_proj_w': jax.random.normal(ks[3], (E, E), jnp.float32) * s, 'out_proj_b': jnp.zeros((E,), jnp.float32), 'pos_w': jax.random.normal(ks[4], (E, E), jnp.float32) * s, 'pos_bias_u': jax.random.normal(ks[5], (H, hd), jnp.float32) * s, 'pos_bias_v': jax.random.normal(ks[6], (H, hd), jnp.float32) * s}
    _L0_attn_all = _L0_attn_setup()
    _L0_attn_in = {k: v for k, v in _L0_attn_all.items() if k in ('pos_emb', 'in_proj_w', 'in_proj_b', 'out_proj_w', 'out_proj_b', 'pos_w', 'pos_bias_u', 'pos_bias_v')}
    del _L0_attn_all

    def _L0_ffn_setup():
        import jax, jax.numpy as jnp
        import numpy as np
        MARK_AX, OP_ADD, OP_SUB = (0, 1, 2)
        ALU_LO, ALU_HI = (16, 32)
        AX_CARRY_LO, AX_CARRY_HI = (48, 64)
        OPCODE_BASE = 80
        OUTPUT_LO, OUTPUT_HI, CARRY = (128, 144, 160)
        NIB_A, NIB_B, OP_START = (0, 1, 10)
        RESULT, CARRY_OUT = (100, 101)
        GE_POS, GE_DIM = (8, 160)
        OPC_ADD, OPC_SUB = (25, 26)
        B, S, D = (8, 1024, 128)

        def _decode_nibble(x, base):
            return jnp.argmax(x[..., base:base + 16] > 0.5, axis=-1).astype(x.dtype)

        def _pipeline(h, W, b):
            for i in range(3):
                h = jnp.einsum('bspd,od->bspo', h, W[i]) + b[i]
                if i < 2:
                    h = jax.nn.relu(h)
            return h
        key = jax.random.key(seed)
        kx, k1, k2, k3, k4 = jax.random.split(key, 5)
        x_bd = jax.random.uniform(kx, (B, S, D), dtype=jnp.float32)
        Wa = jax.random.normal(k1, (3, GE_DIM, GE_DIM), dtype=jnp.float32) * 0.05
        ba = jax.random.normal(k2, (3, GE_DIM), dtype=jnp.float32) * 0.05
        Ws = jax.random.normal(k3, (3, GE_DIM, GE_DIM), dtype=jnp.float32) * 0.05
        bs = jax.random.normal(k4, (3, GE_DIM), dtype=jnp.float32) * 0.05
        return {'x_bd': x_bd, 'Wa': Wa, 'ba': ba, 'Ws': Ws, 'bs': bs}
    _L0_ffn_all = _L0_ffn_setup()
    _L0_ffn_in = {k: v for k, v in _L0_ffn_all.items() if k in ('Wa', 'ba', 'Ws', 'bs')}
    del _L0_ffn_all

    def _L1_attn_setup():
        import jax, jax.numpy as jnp
        import numpy as np
        B, L, U, H = (16, 256, 128, 2)
        key = jax.random.key(seed)
        ks = jax.random.split(key, 8)
        s = 0.02
        return {'inputs': jax.random.normal(ks[0], (B, L, U), dtype=jnp.float32), 'tW': jax.random.normal(ks[1], (H, U, U), dtype=jnp.float32) * s, 'tb': jnp.zeros((H, U), dtype=jnp.float32), 'cW': jax.random.normal(ks[2], (H, U, U), dtype=jnp.float32) * s, 'cb': jnp.zeros((H, U), dtype=jnp.float32), 'aW': jax.random.normal(ks[3], (3 * U,), dtype=jnp.float32) * s, 'ab': jnp.zeros((1,), dtype=jnp.float32), 'frW': jax.random.normal(ks[4], (2 * U, U), dtype=jnp.float32) * s, 'frb': jnp.zeros((U,), dtype=jnp.float32), 'ffW': jax.random.normal(ks[5], (2 * U, U), dtype=jnp.float32) * s, 'ffb': jnp.zeros((U,), dtype=jnp.float32)}
    _L1_attn_all = _L1_attn_setup()
    _L1_attn_in = {k: v for k, v in _L1_attn_all.items() if k in ('tW', 'tb', 'cW', 'cb', 'aW', 'ab', 'frW', 'frb', 'ffW', 'ffb')}
    del _L1_attn_all

    def _L1_ffn_setup():
        import jax, jax.numpy as jnp
        import numpy as np
        B, S, D, H, E = (4, 512, 128, 8, 8)
        FF = 4 * D
        HD = D // H
        EPS = 1e-05

        def _layernorm(x, g, b):
            mu = jnp.mean(x, axis=-1, keepdims=True)
            var = jnp.mean((x - mu) ** 2, axis=-1, keepdims=True)
            return (x - mu) * jax.lax.rsqrt(var + EPS) * g + b
        key = jax.random.key(seed)
        ks = jax.random.split(key, 16)
        s = 0.02
        return {'x': jax.random.normal(ks[0], (B, S, D), dtype=jnp.float32), 'ln1_g': jnp.ones((D,), jnp.float32), 'ln1_b': jnp.zeros((D,), jnp.float32), 'Wq': jax.random.normal(ks[1], (D, D), jnp.float32) * s, 'bq': jnp.zeros((D,), jnp.float32), 'Wk': jax.random.normal(ks[2], (D, D), jnp.float32) * s, 'bk': jnp.zeros((D,), jnp.float32), 'Wv': jax.random.normal(ks[3], (D, D), jnp.float32) * s, 'bv': jnp.zeros((D,), jnp.float32), 'Wo': jax.random.normal(ks[4], (D, D), jnp.float32) * s, 'bo': jnp.zeros((D,), jnp.float32), 'gate_W': jax.random.normal(ks[5], (D, E), jnp.float32) * s, 'gate_b': jnp.zeros((E,), jnp.float32), 'W1': jax.random.normal(ks[6], (E, D, FF), jnp.float32) * s, 'b1': jnp.zeros((E, FF), jnp.float32), 'W2': jax.random.normal(ks[7], (E, FF, D), jnp.float32) * s, 'b2': jnp.zeros((E, D), jnp.float32)}
    _L1_ffn_all = _L1_ffn_setup()
    _L1_ffn_in = {k: v for k, v in _L1_ffn_all.items() if k in ('ln1_g', 'ln1_b', 'Wq', 'bq', 'Wk', 'bk', 'Wv', 'bv', 'Wo', 'bo', 'gate_W', 'gate_b', 'W1', 'b1', 'W2', 'b2')}
    del _L1_ffn_all
    return {'x': x, 'L0_tok_w': _L0_tok_in['w'], 'L0_tok_b': _L0_tok_in['b'], 'L0_attn_pos_emb': _L0_attn_in['pos_emb'], 'L0_attn_in_proj_w': _L0_attn_in['in_proj_w'], 'L0_attn_in_proj_b': _L0_attn_in['in_proj_b'], 'L0_attn_out_proj_w': _L0_attn_in['out_proj_w'], 'L0_attn_out_proj_b': _L0_attn_in['out_proj_b'], 'L0_attn_pos_w': _L0_attn_in['pos_w'], 'L0_attn_pos_bias_u': _L0_attn_in['pos_bias_u'], 'L0_attn_pos_bias_v': _L0_attn_in['pos_bias_v'], 'L0_ffn_Wa': _L0_ffn_in['Wa'], 'L0_ffn_ba': _L0_ffn_in['ba'], 'L0_ffn_Ws': _L0_ffn_in['Ws'], 'L0_ffn_bs': _L0_ffn_in['bs'], 'L1_attn_tW': _L1_attn_in['tW'], 'L1_attn_tb': _L1_attn_in['tb'], 'L1_attn_cW': _L1_attn_in['cW'], 'L1_attn_cb': _L1_attn_in['cb'], 'L1_attn_aW': _L1_attn_in['aW'], 'L1_attn_ab': _L1_attn_in['ab'], 'L1_attn_frW': _L1_attn_in['frW'], 'L1_attn_frb': _L1_attn_in['frb'], 'L1_attn_ffW': _L1_attn_in['ffW'], 'L1_attn_ffb': _L1_attn_in['ffb'], 'L1_ffn_ln1_g': _L1_ffn_in['ln1_g'], 'L1_ffn_ln1_b': _L1_ffn_in['ln1_b'], 'L1_ffn_Wq': _L1_ffn_in['Wq'], 'L1_ffn_bq': _L1_ffn_in['bq'], 'L1_ffn_Wk': _L1_ffn_in['Wk'], 'L1_ffn_bk': _L1_ffn_in['bk'], 'L1_ffn_Wv': _L1_ffn_in['Wv'], 'L1_ffn_bv': _L1_ffn_in['bv'], 'L1_ffn_Wo': _L1_ffn_in['Wo'], 'L1_ffn_bo': _L1_ffn_in['bo'], 'L1_ffn_gate_W': _L1_ffn_in['gate_W'], 'L1_ffn_gate_b': _L1_ffn_in['gate_b'], 'L1_ffn_W1': _L1_ffn_in['W1'], 'L1_ffn_b1': _L1_ffn_in['b1'], 'L1_ffn_W2': _L1_ffn_in['W2'], 'L1_ffn_b2': _L1_ffn_in['b2']}

def reference(x, L0_tok_w, L0_tok_b, L0_attn_pos_emb, L0_attn_in_proj_w, L0_attn_in_proj_b, L0_attn_out_proj_w, L0_attn_out_proj_b, L0_attn_pos_w, L0_attn_pos_bias_u, L0_attn_pos_bias_v, L0_ffn_Wa, L0_ffn_ba, L0_ffn_Ws, L0_ffn_bs, L1_attn_tW, L1_attn_tb, L1_attn_cW, L1_attn_cb, L1_attn_aW, L1_attn_ab, L1_attn_frW, L1_attn_frb, L1_attn_ffW, L1_attn_ffb, L1_ffn_ln1_g, L1_ffn_ln1_b, L1_ffn_Wq, L1_ffn_bq, L1_ffn_Wk, L1_ffn_bk, L1_ffn_Wv, L1_ffn_bv, L1_ffn_Wo, L1_ffn_bo, L1_ffn_gate_W, L1_ffn_gate_b, L1_ffn_W1, L1_ffn_b1, L1_ffn_W2, L1_ffn_b2):
    import jax
    import jax.numpy as jnp

    def _L0_tok_ref(img, w, b, patch_size):
        import jax, jax.numpy as jnp
        import numpy as np
        B, C, H, W = img.shape
        p = patch_size
        Hp, Wp = (H // p, W // p)
        S = Hp * Wp
        patches = img.reshape(B, C, Hp, p, Wp, p)
        patches = patches.transpose(0, 2, 4, 1, 3, 5).reshape(B, S, C * p * p)
        out = jnp.einsum('bsk,ek->bse', patches, w) + b
        return out

    def _L0_attn_ref(query, pos_emb, in_proj_w, in_proj_b, out_proj_w, out_proj_b, pos_w, pos_bias_u, pos_bias_v):
        import jax, jax.numpy as jnp
        import numpy as np

        def _rel_shift(x):
            T = x.shape[2]
            i = jnp.arange(T)[:, None]
            j = jnp.arange(T)[None, :]
            idx = j + (T - 1) - i
            return jnp.take_along_axis(x, idx[None, None, :, :], axis=-1)
        L, B, E = query.shape
        H, hd = pos_bias_u.shape
        scaling = float(hd) ** (-0.5)
        qkv = query @ in_proj_w.T + in_proj_b
        q, k, v = jnp.split(qkv, 3, axis=-1)
        q = q.reshape(L, B, H, hd).transpose(1, 2, 0, 3)
        k = k.reshape(L, B, H, hd).transpose(1, 2, 0, 3)
        v = v.reshape(L, B, H, hd).transpose(1, 2, 0, 3)
        p = (pos_emb @ pos_w.T).reshape(pos_emb.shape[0], -1, H, hd)
        p = p.transpose(0, 2, 1, 3)
        q_u = q + pos_bias_u[None, :, None, :]
        q_v = q + pos_bias_v[None, :, None, :]
        mat_ac = jnp.einsum('bhld,bhsd->bhls', q_u, k)
        mat_bd = jnp.einsum('bhld,xhnd->bhln', q_v, p)
        mat_bd = _rel_shift(mat_bd)
        score = (mat_ac + mat_bd) * scaling
        attn = jax.nn.softmax(score, axis=-1)
        out = jnp.einsum('bhls,bhsd->bhld', attn, v)
        out = out.transpose(2, 0, 1, 3).reshape(L, B, E)
        out = out @ out_proj_w.T + out_proj_b
        return out

    def _L0_ffn_ref(x_bd, Wa, ba, Ws, bs):
        import jax, jax.numpy as jnp
        import numpy as np
        MARK_AX, OP_ADD, OP_SUB = (0, 1, 2)
        ALU_LO, ALU_HI = (16, 32)
        AX_CARRY_LO, AX_CARRY_HI = (48, 64)
        OPCODE_BASE = 80
        OUTPUT_LO, OUTPUT_HI, CARRY = (128, 144, 160)
        NIB_A, NIB_B, OP_START = (0, 1, 10)
        RESULT, CARRY_OUT = (100, 101)
        GE_POS, GE_DIM = (8, 160)
        OPC_ADD, OPC_SUB = (25, 26)
        B, S, D = (8, 1024, 128)

        def _decode_nibble(x, base):
            return jnp.argmax(x[..., base:base + 16] > 0.5, axis=-1).astype(x.dtype)

        def _pipeline(h, W, b):
            for i in range(3):
                h = jnp.einsum('bspd,od->bspo', h, W[i]) + b[i]
                if i < 2:
                    h = jax.nn.relu(h)
            return h
        x = x_bd
        Bsz, seq, _ = x.shape
        x_ge = jnp.zeros((Bsz, seq, GE_POS, GE_DIM), dtype=x.dtype)
        x_ge = x_ge.at[..., 0, NIB_A].set(_decode_nibble(x, ALU_LO))
        x_ge = x_ge.at[..., 1, NIB_A].set(_decode_nibble(x, ALU_HI))
        x_ge = x_ge.at[..., 0, NIB_B].set(_decode_nibble(x, AX_CARRY_LO))
        x_ge = x_ge.at[..., 1, NIB_B].set(_decode_nibble(x, AX_CARRY_HI))
        x_ge = x_ge.at[..., :, OP_START + OPC_ADD].set(x[..., OPCODE_BASE + OPC_ADD][..., None])
        x_ge = x_ge.at[..., :, OP_START + OPC_SUB].set(x[..., OPCODE_BASE + OPC_SUB][..., None])
        mark = x[..., MARK_AX] > 0.5
        m_add = mark & (x[..., OP_ADD] > 0.5)
        m_sub = mark & ~(x[..., OP_ADD] > 0.5) & (x[..., OP_SUB] > 0.5)
        active = (m_add | m_sub).astype(x.dtype)
        y_add = _pipeline(x_ge, Wa, ba)
        y_sub = _pipeline(x_ge, Ws, bs)
        y = jnp.where(m_add[..., None, None], y_add, jnp.where(m_sub[..., None, None], y_sub, x_ge))
        res_lo = jnp.clip(jnp.round(y[..., 0, RESULT]), 0, 15).astype(jnp.int32)
        res_hi = jnp.clip(jnp.round(y[..., 1, RESULT]), 0, 15).astype(jnp.int32)
        oh_lo = jax.nn.one_hot(res_lo, 16, dtype=x.dtype) * active[..., None]
        oh_hi = jax.nn.one_hot(res_hi, 16, dtype=x.dtype) * active[..., None]
        carry = (jnp.round(y[..., 1, CARRY_OUT]) > 0.5).astype(x.dtype) * active
        out = x
        out = out.at[..., OUTPUT_LO:OUTPUT_LO + 16].add(2.0 * oh_lo)
        out = out.at[..., OUTPUT_HI:OUTPUT_HI + 16].add(2.0 * oh_hi)
        out = out.at[..., CARRY].add(carry)
        return out

    def _L1_attn_ref(inputs, tW, tb, cW, cb, aW, ab, frW, frb, ffW, ffb):
        import jax, jax.numpy as jnp
        import numpy as np
        B, L, U, H = (16, 256, 128, 2)
        x = inputs
        for i in range(tW.shape[0]):
            t = jax.nn.relu(x @ tW[i] + tb[i])
            c = jax.nn.sigmoid(x @ cW[i] + cb[i])
            x = t * c + x * (1.0 - c)
        u = x.shape[-1]
        w1, w2, w3 = (aW[:u], aW[u:2 * u], aW[2 * u:])
        s1 = x @ w1
        s2 = x @ w2
        s3 = jnp.einsum('bid,bjd->bij', x * w3, x)
        A = jax.nn.relu(s1[:, :, None] + s2[:, None, :] + s3 + ab[0])
        att = jnp.einsum('bij,bjd->bid', jax.nn.softmax(A, axis=-1), x)
        concat = jnp.concatenate([inputs, att], axis=-1)
        z = jax.nn.sigmoid(concat @ ffW + ffb)
        r = jax.nn.sigmoid(concat @ frW + frb)
        f = z
        return r * inputs + f * z

    def _L1_ffn_ref(x, ln1_g, ln1_b, Wq, bq, Wk, bk, Wv, bv, Wo, bo, gate_W, gate_b, W1, b1, W2, b2):
        import jax, jax.numpy as jnp
        import numpy as np
        B, S, D, H, E = (4, 512, 128, 8, 8)
        FF = 4 * D
        HD = D // H
        EPS = 1e-05

        def _layernorm(x, g, b):
            mu = jnp.mean(x, axis=-1, keepdims=True)
            var = jnp.mean((x - mu) ** 2, axis=-1, keepdims=True)
            return (x - mu) * jax.lax.rsqrt(var + EPS) * g + b
        b, s, d = x.shape
        q = (x @ Wq + bq).reshape(b, s, H, HD)
        k = (x @ Wk + bk).reshape(b, s, H, HD)
        v = (x @ Wv + bv).reshape(b, s, H, HD)
        scores = jnp.einsum('bqhd,bkhd->bhqk', q, k) / jnp.sqrt(jnp.float32(HD))
        attn = jax.nn.softmax(scores, axis=-1)
        o = jnp.einsum('bhqk,bkhd->bqhd', attn, v).reshape(b, s, d) @ Wo + bo
        h = _layernorm(x + o, ln1_g, ln1_b)
        t = h.reshape(b * s, d)
        probs = jax.nn.softmax(t @ gate_W + gate_b, axis=-1)
        idx = jnp.argmax(probs, axis=-1)
        gw = jnp.max(probs, axis=-1)
        hid = jax.nn.gelu(jnp.einsum('nd,edf->enf', t, W1) + b1[:, None, :])
        out_all = jnp.einsum('enf,efd->end', hid, W2) + b2[:, None, :]
        onehot = jax.nn.one_hot(idx, E, dtype=t.dtype)
        out = jnp.einsum('ne,end->nd', onehot, out_all)
        out = out * gw[:, None]
        return out.reshape(b, s, d)
    h = _L0_tok_ref(x, L0_tok_w, L0_tok_b, 16)
    h = h + _L0_attn_ref(_layernorm(h, axis=-1), L0_attn_pos_emb, L0_attn_in_proj_w, L0_attn_in_proj_b, L0_attn_out_proj_w, L0_attn_out_proj_b, L0_attn_pos_w, L0_attn_pos_bias_u, L0_attn_pos_bias_v)
    h = h + _L0_ffn_ref(_layernorm(h, axis=-1), L0_ffn_Wa, L0_ffn_ba, L0_ffn_Ws, L0_ffn_bs)
    h = h + _L1_attn_ref(_layernorm(h, axis=-1), L1_attn_tW, L1_attn_tb, L1_attn_cW, L1_attn_cb, L1_attn_aW, L1_attn_ab, L1_attn_frW, L1_attn_frb, L1_attn_ffW, L1_attn_ffb)
    h = h + _L1_ffn_ref(_layernorm(h, axis=-1), L1_ffn_ln1_g, L1_ffn_ln1_b, L1_ffn_Wq, L1_ffn_bq, L1_ffn_Wk, L1_ffn_bk, L1_ffn_Wv, L1_ffn_bv, L1_ffn_Wo, L1_ffn_bo, L1_ffn_gate_W, L1_ffn_gate_b, L1_ffn_W1, L1_ffn_b1, L1_ffn_W2, L1_ffn_b2)
    return h

_drawn_inputs = setup_inputs


def setup_inputs(seed=0):
    import zlib

    import numpy as np

    out = dict(_drawn_inputs(seed))
    spreads = {'L0_attn_in_proj_b': (0.0, 0.592),
     'L0_attn_out_proj_b': (0.0, 0.1),
     'L1_attn_tb': (0.0, 0.8),
     'L1_attn_cb': (0.0, 0.8),
     'L1_attn_frb': (0.0, 0.8),
     'L1_attn_ffb': (0.0, 0.8),
     'L1_ffn_ln1_g': (1.0, 0.6),
     'L1_ffn_ln1_b': (0.0, 0.8),
     'L1_ffn_bq': (0.0, 0.8),
     'L1_ffn_bk': (0.0, 2.0),
     'L1_ffn_bv': (0.0, 0.8),
     'L1_ffn_bo': (0.0, 0.8),
     'L1_ffn_gate_b': (0.0, 0.8),
     'L1_ffn_b1': (0.0, 0.8),
     'L1_ffn_b2': (0.0, 0.8)}
    factors = {'L0_attn_pos_emb': 8.0,
     'L0_attn_pos_w': 8.0,
     'L0_attn_pos_bias_u': 200.0,
     'L0_attn_pos_bias_v': 8.0,
     'L1_attn_tW': 8.0,
     'L1_attn_cW': 8.0,
     'L1_attn_aW': 8.0,
     'L1_attn_frW': 2.898,
     'L1_attn_ffW': 2.844,
     'L1_ffn_Wq': 8.0,
     'L1_ffn_Wk': 8.0,
     'L1_ffn_Wv': 8.0,
     'L1_ffn_Wo': 8.0,
     'L1_ffn_gate_W': 8.0,
     'L1_ffn_W1': 8.0,
     'L1_ffn_W2': 8.0}
    for name, (base, spread) in spreads.items():
        noise = np.random.default_rng([zlib.crc32(name.encode()), seed]).standard_normal(out[name].shape)
        drawn = base * np.exp(spread * noise) if base else spread * noise
        out[name] = jnp.asarray(drawn.astype(out[name].dtype))
    for name, factor in factors.items():
        out[name] = (out[name] * factor).astype(out[name].dtype)
    return out
```

```python
from contextlib import ExitStack

import numpy as np

import concourse.bass as bass
from concourse import mybir

F32 = mybir.dt.float32
BF16 = mybir.dt.bfloat16
I32 = mybir.dt.int32
U32 = mybir.dt.uint32
ALU = mybir.AluOpType
ACT = mybir.ActivationFunctionType
X = mybir.AxisListType.X

P = 128
IMAGES, POSITIONS = 64, 36
CHUNKS = 6
HEADS, HD = 8, 16
TOKENS = IMAGES * POSITIONS
TILES = TOKENS // P
REL = 2 * IMAGES - 1
IMG_G = 3
G = IMG_G * POSITIONS
GROUPS = -(-IMAGES // IMG_G)
EXPERTS, FF = 8, 512
FC = FF // P
SLOT_TILES = TOKENS // P + EXPERTS - 1
EPS = 1e-5
SCALE = float(HD) ** -0.5
FAR = -float(2 ** 100)

_WEIGHTS = [("tok", CHUNKS * P), ("in_proj", 3 * P), ("out_proj", P), ("pos_w", P), ("pos", REL),
            ("ident", P), ("head_mask", HEADS), ("half_mask", HEADS)]
_WEIGHTS1 = [("tW", 2 * P), ("cW", 2 * P), ("ff", 2 * P), ("fr", 2 * P), ("Wq", P), ("Wk", P), ("Wv", P),
             ("Wo", P), ("gate", EXPERTS), ("same", G), ("before", G), ("ones", G), ("member", G),
             ("apart", 4 * G), ("valid", GROUPS), ("rank_w", EXPERTS), ("tile_lo", TILES), ("tile_no", SLOT_TILES),
             ("lower", EXPERTS * EXPERTS)]
_COLUMNS = ["bq0", "bk0", "bv0", "u", "v", "tb0", "tb1", "cb0", "cb1", "a1", "a2", "a3", "frb", "ffb", "g", "b",
            "bq1", "bk1", "bv1", "ab"]
_ROWS = [("tok_b", P), ("out_b", P), ("bo", P), ("gate_b", EXPERTS)]


def places(items):
    at, out = 0, {}
    for name, width in items:
        out[name] = (at, width)
        at += width
    return out, at


AT_W, WIDTH_W = places(_WEIGHTS)
AT_W1, WIDTH_W1 = places(_WEIGHTS1)
AT_R, WIDTH_R = places(_ROWS)


class Tile:

    def __init__(self, u, c, lag, tiles):
        self.n = 2 * u + (c - lag)
        self.par = (c - lag) % 2
        self.half = u + (c - lag) // 2
        self.live = not isinstance(u, int) or 0 <= self.n < tiles


def after(eng, sem, count):
    if not isinstance(count, int) or count > 0:
        eng.wait_ge(sem, count)


def pipeline(eng, stages, tiles, loop_from, loop_to):
    last = tiles + max(lag for _, lag in stages)

    def step(u, c):
        for stage, lag in stages:
            t = Tile(u, c, lag, tiles)
            if t.live:
                stage(t)

    for i in range(2 * loop_from):
        step(i // 2, i % 2)
    with eng.Fori(loop_from, loop_to) as u:
        step(u, 0)
        step(u, 1)
    for i in range(2 * loop_to, last):
        step(i // 2, i % 2)


def over(ap, axis, count, shape):
    return ap.unsqueeze(axis).broadcast_to(shape)


def tower(nc, patches, weights, weights1, columns, rows, b1_rows, b2_rows, W1, W2, zeros, out,
          bd_dram, hs_dram, sorted_dram, expert_dram, upto="all"):
    with ExitStack() as ctx:
        def sb(name, shape, dt=F32):
            return ctx.enter_context(nc.sbuf_tensor(name, shape, dt))

        def sem(name):
            return ctx.enter_context(nc.semaphore(name))

        banks = [ctx.enter_context(nc.psum_tensor(f"bank{i}", [P, 512], F32)) for i in range(8)]

        w = sb("w", [P, WIDTH_W])
        w1 = sb("w1", [P, WIDTH_W1])
        cols = sb("cols", [P, len(_COLUMNS)])
        bias_rows = sb("bias_rows", [P, WIDTH_R])

        def W(name, a=0, b=None):
            at, width = AT_W[name]
            return w[:, at + a:at + (width if b is None else b)]

        def V(name, a=0, b=None, rows_=P):
            at, width = AT_W1[name]
            return w1[0:rows_, at + a:at + (width if b is None else b)]

        def col(name, rows_=P):
            c = _COLUMNS.index(name)
            return cols[0:rows_, c:c + 1]

        def row(name, rows_=P):
            at, width = AT_R[name]
            return bias_rows[0:rows_, at:at + width]

        weights_in = sem("weights_in")
        weights1_in = sem("weights1_in")
        stored = [sem("stored_even"), sem("stored_odd")]

        pads_zero = sem("pads_zero")
        kept = [sem("kept_even"), sem("kept_odd")]
        h_all = sb("h_all", [G, GROUPS, P])
        xb_all = sb("xb_all", [G, GROUPS, P])
        n_all = sb("n_all", [G, GROUPS, P])
        lg_all = sb("lg_all", [G, GROUPS, EXPERTS])
        slots_zero = sem("slots_zero")
        experts_in = sem("experts_in")
        W1_sb = sb("W1_sb", [P, EXPERTS * FF])
        W2_sb = sb("W2_sb", [P, EXPERTS * FF])
        b1_sb = sb("b1_sb", [P, EXPERTS * FF])
        b2_sb = sb("b2_sb", [P, EXPERTS * P])
        loads = ((W1_sb, W1), (W2_sb, W2), (b1_sb, b1_rows), (b2_sb, b2_rows))
        own = []

        def part_sem(name):
            own.append(nc.alloc_semaphore(name=name))
            return own[-1]

        with ExitStack() as ctx0:
            block0(nc, ctx0, part_sem, banks, W, col, row, w, w1, cols, bias_rows, patches, weights, weights1,
                   columns, rows, weights_in, weights1_in, stored, bd_dram, hs_dram, zeros, pads_zero)
        nc.clear_and_free_semaphores(own)
        nc.all_engine_barrier()
        own.clear()
        with ExitStack() as ctx1:
            block1(nc, ctx1, part_sem, banks, V, col, row, W("ident"), W("head_mask"), h_all, xb_all, n_all, lg_all, hs_dram,
                   stored, pads_zero, weights1_in, kept, loads, experts_in, sorted_dram, slots_zero, zeros)
        nc.clear_and_free_semaphores(own)
        nc.all_engine_barrier()
        own.clear()
        with ExitStack() as ctx2:
            block2(nc, ctx2, part_sem, banks, V, col, W("ident"), h_all, n_all, lg_all, W1_sb, W2_sb, b1_sb, b2_sb, experts_in,
                   sorted_dram, expert_dram, out, slots_zero, kept)


def block0(nc, ctx, sem, banks, W, col, row, w, w1, cols, bias_rows, patches, weights, weights1,
           columns, rows, weights_in, weights1_in, stored, bd_dram, hs_dram, zeros, pads_zero):
    def sb(name, shape, dt=F32):
        return ctx.enter_context(nc.sbuf_tensor(name, shape, dt))

    def pair(name, shape, dt=F32):
        return [sb(f"{name}{i}", shape, dt) for i in range(2)]

    TOK, XT, Q, KV, BD0, BD1, AC, PT = banks

    patch = pair("patch", [P, CHUNKS * P])
    h0 = sb("h0", [P, TILES, P])
    stats = pair("stats", [P, 6])
    mv = pair("mv", [P, 2])
    ve = pair("ve", [P, 1])
    rstd = pair("rstd", [P, 1])
    xn = pair("xn", [P, P])
    xT = pair("xT", [P, 2, 2, IMAGES])
    qu = pair("qu", [P, P])
    qv = pair("qv", [P, P])
    kb = pair("kb", [P, HEADS, P])
    vv = pair("vv", [P, 2, HEADS, HD + 1])
    pos_p = sb("pos_p", [P, REL])
    pb = sb("pb", [P, HEADS, REL])
    bias_u = sb("bias_u", [P, 1])
    bias_v = sb("bias_v", [P, 1])
    bd = pair("bd", [P, HEADS * REL])
    bs = pair("bs", [P, HEADS * IMAGES])
    s1 = pair("s1", [P, HEADS, IMAGES])
    mx = pair("mx", [P, HEADS])
    s2 = pair("s2", [P, HEADS, IMAGES])
    ex = pair("ex", [P, HEADS * IMAGES])
    pT = pair("pT", [P, 4 * P])
    rs = pair("rs", [P, HEADS])
    on = pair("on", [P, HEADS, HD])
    oT = pair("oT", [P, P])
    st2 = pair("st2", [P, 6])
    mv2 = pair("mv2", [P, 2])
    ve2 = pair("ve2", [P, 1])
    rstd2 = pair("rstd2", [P, 1])
    nrm = pair("nrm", [P, P])
    att = pair("att", [P, P])
    h2 = pair("h2", [P, P])
    half_pow = sb("half_pow", [P, 1])

    patch_in = [sem("patch_in_even"), sem("patch_in_odd")]
    half_pow_set = sem("half_pow_set")
    ones_set = sem("ones_set")
    biases_made = sem("biases_made")
    pos_projected = sem("pos_projected")
    pos_ready = sem("pos_ready")
    tok_done = sem("tok_done")
    h_ready = sem("h_ready")
    stats_done = sem("stats_done")
    mv_done = sem("mv_done")
    ve_done = sem("ve_done")
    rstd_done = sem("rstd_done")
    xn_done = sem("xn_done")
    xT_done = sem("xT_done")
    xT_copied = sem("xT_copied")
    q_done = sem("q_done")
    qv_copied = sem("qv_copied")
    qu_copied = sem("qu_copied")
    kv_done = sem("kv_done")
    kb_made = sem("kb_made")
    vv_made = sem("vv_made")
    bd_done = sem("bd_done")
    bd_copied = sem("bd_copied")
    bd_out = [sem("bd_out_even"), sem("bd_out_odd")]
    bd_back = [sem("bd_back_even"), sem("bd_back_odd")]
    ac_done = sem("ac_done")
    scores_added = sem("scores_added")
    max_found = sem("max_found")
    scores_less_max = sem("scores_less_max")
    exp_done = sem("exp_done")
    pT_done = sem("pT_done")
    pT_copied = sem("pT_copied")
    pv_done = sem("pv_done")
    sums_inverted = sem("sums_inverted")
    attn_normal = sem("attn_normal")
    oT_done = sem("oT_done")
    oT_copied = sem("oT_copied")
    proj_done = sem("proj_done")
    att_biased = sem("att_biased")
    h1_ready = sem("h1_ready")
    stats2_done = sem("stats2_done")
    mv2_done = sem("mv2_done")
    ve2_done = sem("ve2_done")
    rstd2_done = sem("rstd2_done")
    nrm_done = sem("nrm_done")
    h2_ready = sem("h2_ready")

    hs_rows = hs_dram[0:TOKENS, :].rearrange("(l s) e -> s l e", s=POSITIONS)
    block = ctx.enter_context(nc.Block())
    LOOP = (2, TILES // 2)

    @block.sync
    def _(sp):
        sp.dma_start(w[:, :], weights).then_inc(weights_in, 16)
        sp.dma_start(cols[:, :], columns).then_inc(weights_in, 16)
        sp.dma_start(bias_rows[:, :], rows).then_inc(weights_in, 16)

        def shift_back(t):
            sp.wait_ge(bd_copied, t.n + 1)
            sp.dma_start(bd_dram[t.par], bd[t.par][:, :]).then_inc(bd_out[t.par], 16)
            sp.wait_ge(bd_out[t.par], 16 * (t.half + 1))
            for s in range(2):
                src = bass.AP(tensor=bd_dram.tensor,
                              offset=(t.par * P + s * IMAGES) * HEADS * REL + IMAGES - 1,
                              ap=[[HEADS * REL - 1, IMAGES], [REL, HEADS], [1, IMAGES]])
                sp.dma_start(bs[t.par][s * IMAGES:(s + 1) * IMAGES, :].rearrange("p (h j) -> p h j", h=HEADS),
                             src).then_inc(bd_back[t.par], 16)

        def store(t):
            sp.wait_ge(h2_ready, t.n + 1)
            for s in range(2):
                sp.dma_start(hs_rows[2 * t.n + s], h2[t.par][s * IMAGES:(s + 1) * IMAGES, :])\
                  .then_inc(stored[t.par], 16)

        pipeline(sp, [(shift_back, 0), (store, 2)], TILES, *LOOP)
        sp.dma_start(w1[:, :], weights1).then_inc(weights1_in, 16)
        sp.dma_start(hs_dram[TOKENS:GROUPS * G, :], zeros[0:GROUPS * G - TOKENS, :]).then_inc(pads_zero, 16)
        sp.wait_ge(pads_zero, 16)
        for s in stored:
            sp.wait_ge(s, 16 * TILES)

    @block.tensor
    def _(pe):
        pe.wait_ge(weights_in, 48)
        nc.tensor.matmul(XT[:, 0:REL], W("pos_w"), W("pos"), start=True, stop=True).then_inc(pos_projected, 1)

        def embed(t):
            pe.wait_ge(patch_in[t.par], 16 * (t.half + 1))
            after(pe, h_ready, t.n)
            after(pe, att_biased, t.n - 2)
            for c in range(CHUNKS):
                mm = nc.tensor.matmul(TOK[:, 0:P], patch[t.par][:, c * P:(c + 1) * P], W("tok", c * P, (c + 1) * P),
                                      start=(c == 0), stop=(c == CHUNKS - 1))
            mm.then_inc(tok_done, 1)

        def content(s):
            def stage(t):
                if s == 0:
                    pe.wait_ge(qu_copied, t.n + 1)
                    pe.wait_ge(kb_made, t.n + 1)
                    after(pe, scores_added, t.n)
                mm = nc.tensor.matmul(AC[s * IMAGES:(s + 1) * IMAGES, :], qu[t.par][:, s * IMAGES:(s + 1) * IMAGES],
                                      kb[t.par][:, :, s * IMAGES:(s + 1) * IMAGES], start=True, stop=True)
                if s == 1:
                    mm.then_inc(ac_done, 1)
            return stage

        def turn_probs(t):
            pe.wait_ge(exp_done, t.n + 1)
            after(pe, attn_normal, t.n)
            for g in range(4):
                mm = nc.tensor.transpose(PT[:, g * P:(g + 1) * P], ex[t.par][:, g * P:(g + 1) * P], W("ident"))
            mm.then_inc(pT_done, 1)

        def turn_x(t):
            pe.wait_ge(xn_done, t.n + 1)
            after(pe, oT_copied, t.n - 2)
            nc.tensor.transpose(XT[:, 0:P], xn[t.par][:, :], W("ident")).then_inc(xT_done, 1)

        def attend(t):
            pe.wait_ge(pT_copied, t.n + 1)
            pe.wait_ge(vv_made, t.n + 1)
            for s in range(2):
                for g in range(4):
                    mm = nc.tensor.matmul(
                        PT[s * IMAGES:(s + 1) * IMAGES, g * 34:(g + 1) * 34],
                        pT[t.par][:, g * P + s * IMAGES:g * P + (s + 1) * IMAGES],
                        vv[t.par][:, s, 2 * g:2 * g + 2, :].rearrange("p h d -> p (h d)"), start=True, stop=True)
            mm.then_inc(pv_done, 1)

        def project(t):
            pe.wait_ge(xT_copied, t.n + 1)
            after(pe, qu_copied, t.n)
            after(pe, qv_copied, t.n)
            nc.tensor.matmul(Q[:, 0:P], W("in_proj", 0, P), xT[t.par][:, :, 0, :], start=True, stop=True).then_inc(q_done, 1)
            after(pe, kb_made, t.n)
            after(pe, vv_made, t.n)
            nc.tensor.matmul(KV[:, 0:P], W("in_proj", P, 2 * P), xT[t.par][:, :, 0, :], start=True, stop=True)
            for s in range(2):
                twice = xT[t.par][:, s, :, :].rearrange("p r l -> p (r l)")
                mm = nc.tensor.matmul(KV[:, (s + 1) * P:(s + 2) * P], twice, W("in_proj", 2 * P, 3 * P),
                                      start=True, stop=True)
            mm.then_inc(kv_done, 1)

        def turn_o(t):
            pe.wait_ge(attn_normal, t.n + 1)
            after(pe, xT_copied, t.n + 3 if not isinstance(t.n, int) else min(t.n + 3, TILES))
            nc.tensor.transpose(XT[:, 0:P], on[t.par][:, :, :].rearrange("p h d -> p (h d)"), W("ident"))\
              .then_inc(oT_done, 1)

        def positions(b):
            def stage(t):
                if b == 0:
                    pe.wait_ge(qv_copied, t.n + 1)
                    if isinstance(t.n, int) and t.n == 0:
                        pe.wait_ge(pos_ready, 1)
                    after(pe, bd_copied, t.n)
                mm = nc.tensor.matmul((BD0, BD1)[b][:, 0:4 * REL], qv[t.par][:, :],
                                      pb[:, 4 * b:4 * b + 4, :].rearrange("p h n -> p (h n)"), start=True, stop=True)
                if b == 1:
                    mm.then_inc(bd_done, 1)
            return stage

        def project_out(t):
            pe.wait_ge(oT_copied, t.n + 1)
            after(pe, h_ready, t.n + 3 if not isinstance(t.n, int) else min(t.n + 3, TILES))
            nc.tensor.matmul(TOK[:, 0:P], oT[t.par][:, :], W("out_proj"), start=True, stop=True).then_inc(proj_done, 1)

        pipeline(pe, [(embed, 0), (content(0), 1), (turn_probs, 2), (content(1), 1), (turn_x, 0), (attend, 2),
                      (project, 0), (turn_o, 2), (positions(0), 0), (project_out, 2), (positions(1), 0)],
                 TILES, *LOOP)

    @block.scalar
    def _(act):
        act.wait_ge(pos_projected, 1)
        nc.scalar.activation(pos_p[:, :], XT[:, 0:REL], ACT.Identity).then_inc(pos_projected, 1)

        def keep_positions(t):
            act.wait_ge(bd_done, t.n + 1)
            after(act, bd_out[t.par], 16 * t.half)
            for b in range(2):
                a = nc.scalar.activation(bd[t.par][:, b * 4 * REL:(b + 1) * 4 * REL], (BD0, BD1)[b][:, 0:4 * REL],
                                         ACT.Identity)
            a.then_inc(bd_copied, 1)

        def exponentials(t):
            act.wait_ge(scores_less_max, t.n + 1)
            after(act, pT_done, t.n - 1)
            nc.scalar.activation(ex[t.par][:, :], s2[t.par][:, :, :].rearrange("p h j -> p (h j)"), ACT.Exp,
                                 scale=SCALE).then_inc(exp_done, 1)

        def copy_probs(t):
            act.wait_ge(pT_done, t.n + 1)
            after(act, pv_done, t.n - 1)
            nc.scalar.activation(pT[t.par][:, :], PT[:, :], ACT.Identity).then_inc(pT_copied, 1)

        def copy_x(t):
            act.wait_ge(xT_done, t.n + 1)
            after(act, kv_done, t.n - 1)
            nc.scalar.activation(xT[t.par][:, :, :, :],
                                 over(XT[:, 0:P].rearrange("p (s l) -> p s l", s=2), 2, 2, [P, 2, 2, IMAGES]),
                                 ACT.Identity).then_inc(xT_copied, 1)

        def queries(t):
            act.wait_ge(q_done, t.n + 1)
            if isinstance(t.n, int) and t.n == 0:
                act.wait_ge(biases_made, 2)
            after(act, bd_done, t.n - 1)
            nc.scalar.activation(qv[t.par][:, :], Q[:, 0:P], ACT.Identity, bias=bias_v[:, 0:1]).then_inc(qv_copied, 1)
            after(act, ac_done, t.n - 1)
            nc.scalar.activation(qu[t.par][:, :], Q[:, 0:P], ACT.Identity, bias=bias_u[:, 0:1]).then_inc(qu_copied, 1)

        def copy_o(t):
            act.wait_ge(oT_done, t.n + 1)
            after(act, proj_done, t.n - 1)
            nc.scalar.activation(oT[t.par][:, :], XT[:, 0:P], ACT.Identity, bias=col("bv0")).then_inc(oT_copied, 1)

        pipeline(act, [(keep_positions, 1), (exponentials, 2), (copy_probs, 2), (copy_x, 0), (queries, 0),
                       (copy_o, 2)], TILES, *LOOP)

    @block.gpsimd
    def _(pool):
        nc.gpsimd.memset(half_pow[:, :], -0.5).then_inc(half_pow_set, 1)
        for p in range(2):
            nc.gpsimd.memset(vv[p][:, :, :, :], 0.0).then_inc(ones_set, 1)
        pool.wait_ge(half_pow_set, 1)

        def load_patches(t):
            after(pool, tok_done, t.n - 1)
            pool.dma_start(patch[t.par][:, :], patches[t.n]).then_inc(patch_in[t.par], 16)

        def root(t):
            pool.wait_ge(ve_done, t.n + 1)
            after(pool, xn_done, t.n - 1)
            nc.gpsimd.tensor_tensor(rstd[t.par][:, :], ve[t.par][:, :], half_pow[:, :], ALU.pow).then_inc(rstd_done, 1)

        def root2(t):
            pool.wait_ge(ve2_done, t.n + 1)
            after(pool, nrm_done, t.n - 1)
            nc.gpsimd.tensor_tensor(rstd2[t.par][:, :], ve2[t.par][:, :], half_pow[:, :], ALU.pow)\
              .then_inc(rstd2_done, 1)

        pipeline(pool, [(load_patches, 0), (root, 1), (root2, 3)], TILES, *LOOP)

    @block.vector
    def _(dve):
        dve.wait_ge(weights_in, 48)
        dve.wait_ge(ones_set, 2)
        for p in range(2):
            for s in range(2):
                nc.vector.tensor_copy(vv[p][:, s, :, HD:HD + 1].rearrange("p h o -> p (h o)"), W("half_mask"))\
                  .then_inc(ones_set, 1)
        nc.vector.tensor_tensor(bias_u[:, :], col("bq0"), col("u"), ALU.add).then_inc(biases_made, 1)
        nc.vector.tensor_tensor(bias_v[:, :], col("bq0"), col("v"), ALU.add).then_inc(biases_made, 1)
        dve.wait_ge(pos_projected, 2)
        nc.vector.tensor_tensor(pb[:, :, :], over(pos_p[:, :], 1, HEADS, [P, HEADS, REL]),
                                over(W("head_mask"), 2, REL, [P, HEADS, REL]), ALU.mult).then_inc(pos_ready, 1)

        def embedded(t):
            after(dve, xn_done, t.n - 1)
            dve.wait_ge(tok_done, t.n + 1)
            nc.vector.tensor_tensor(h0[:, t.n, :], TOK[:, 0:P], row("tok_b"), ALU.add).then_inc(h_ready, 1)
            dve.drain()
            nc.vector.bn_stats(stats[t.par][:, :], h0[:, t.n, :])
            dve.drain()
            nc.vector.bn_aggr(mv[t.par][:, :], stats[t.par][:, :]).then_inc(mv_done, 1)
            dve.wait_ge(mv_done, t.n + 1)
            after(dve, rstd_done, t.n - 1)
            nc.vector.tensor_scalar(ve[t.par][:, :], mv[t.par][:, 1:2], EPS, None, ALU.add).then_inc(ve_done, 1)

        def normalise(t):
            dve.wait_ge(rstd_done, t.n + 1)
            after(dve, xT_done, t.n - 1)
            nc.vector.tensor_scalar(xn[t.par][:, :], h0[:, t.n, :], mv[t.par][:, 0:1], rstd[t.par][:, 0:1],
                                    ALU.subtract, ALU.mult).then_inc(xn_done, 1)

        def second_residual(t):
            dve.wait_ge(rstd2_done, t.n + 1)
            after(dve, h2_ready, t.n - 1)
            nc.vector.tensor_scalar(nrm[t.par][:, :], h0[:, t.n, :], mv2[t.par][:, 0:1], rstd2[t.par][:, 0:1],
                                    ALU.subtract, ALU.mult).then_inc(nrm_done, 1)
            dve.wait_ge(nrm_done, t.n + 1)
            after(dve, stored[t.par], 32 * t.half)
            nc.vector.tensor_tensor(h2[t.par][:, :], h0[:, t.n, :], nrm[t.par][:, :], ALU.add).then_inc(h2_ready, 1)

        def divide(t):
            o = PT[:, 0:HEADS * (HD + 1)].rearrange("p (h d) -> p h d", h=HEADS)
            dve.wait_ge(pv_done, t.n + 1)
            nc.vector.reciprocal(rs[t.par][:, :], o[:, :, HD]).then_inc(sums_inverted, 1)
            dve.wait_ge(sums_inverted, t.n + 1)
            after(dve, oT_done, t.n - 1)
            nc.vector.tensor_tensor(on[t.par][:, :, :], o[:, :, 0:HD], over(rs[t.par][:, :], 2, HD, [P, HEADS, HD]),
                                    ALU.mult).then_inc(attn_normal, 1)

        def keys_values(t):
            dve.wait_ge(kv_done, t.n + 1)
            after(dve, ac_done, t.n - 1)
            nc.vector.scalar_tensor_tensor(out=kb[t.par][:, :, :], in0=over(KV[:, 0:P], 1, HEADS, [P, HEADS, P]),
                                           scalar=col("bk0"), in1=over(W("head_mask"), 2, P, [P, HEADS, P]),
                                           op0=ALU.add, op1=ALU.mult).then_inc(kb_made, 1)
            after(dve, pv_done, t.n - 1)
            shape = [P, 2, HEADS, HD]
            v = KV[:, P:3 * P].rearrange("p (s h d) -> p s h d", s=2, h=HEADS)
            mask = W("half_mask").unsqueeze(1).unsqueeze(3).broadcast_to(shape)
            nc.vector.tensor_tensor(vv[t.par][:, :, :, 0:HD], v, mask, ALU.mult).then_inc(vv_made, 1)

        def scores(t):
            dve.wait_ge(bd_back[t.par], 32 * (t.half + 1))
            dve.wait_ge(ac_done, t.n + 1)
            after(dve, scores_less_max, t.n - 1)
            nc.vector.tensor_tensor(s1[t.par][:, :, :].rearrange("p h j -> p (h j)"), AC[:, :], bs[t.par][:, :],
                                    ALU.add).then_inc(scores_added, 1)
            dve.wait_ge(scores_added, t.n + 1)
            nc.vector.tensor_reduce(mx[t.par][:, :], s1[t.par][:, :, :], X, ALU.max).then_inc(max_found, 1)
            dve.wait_ge(max_found, t.n + 1)
            after(dve, exp_done, t.n - 1)
            nc.vector.tensor_tensor(s2[t.par][:, :, :], s1[t.par][:, :, :],
                                    over(mx[t.par][:, :], 2, IMAGES, [P, HEADS, IMAGES]), ALU.subtract)\
              .then_inc(scores_less_max, 1)

        def first_residual(t):
            dve.wait_ge(proj_done, t.n + 1)
            nc.vector.tensor_tensor(att[t.par][:, :], TOK[:, 0:P], row("out_b"), ALU.add).then_inc(att_biased, 1)
            dve.wait_ge(att_biased, t.n + 1)
            after(dve, nrm_done, t.n - 1)
            nc.vector.tensor_tensor(h0[:, t.n, :], h0[:, t.n, :], att[t.par][:, :], ALU.add)
            dve.drain()
            nc.vector.bn_stats(st2[t.par][:, :], h0[:, t.n, :])
            dve.drain()
            nc.vector.bn_aggr(mv2[t.par][:, :], st2[t.par][:, :]).then_inc(mv2_done, 1)
            dve.wait_ge(mv2_done, t.n + 1)
            after(dve, rstd2_done, t.n - 1)
            nc.vector.tensor_scalar(ve2[t.par][:, :], mv2[t.par][:, 1:2], EPS, None, ALU.add).then_inc(ve2_done, 1)

        pipeline(dve, [(embedded, 0), (second_residual, 3), (normalise, 0), (divide, 2), (keys_values, 0),
                       (first_residual, 2), (scores, 1)], TILES, *LOOP)


def block1(nc, ctx, sem, banks, V, col, row, Wident, w_head_mask, h_all, xb_all, n_all, lg_all, hs_dram, stored,
           pads_zero, weights1_in, kept, loads, experts_in, sorted_dram, slots_zero, zeros):
    def sb(name, shape, dt=F32):
        return ctx.enter_context(nc.sbuf_tensor(name, shape, dt))

    def pair(name, shape, dt=F32):
        return [sb(f"{name}{i}", shape, dt) for i in range(2)]

    U0, U1, MM, WD, S0, S1, T0, T1 = banks
    HALF = HEADS // 2

    member = sb("member", [IMG_G, G], BF16)
    apart = sb("apart", [IMG_G, HALF * G], BF16)
    half_col = sb("half_col", [P, 1])
    pow_col = sb("pow_col", [P, 1])
    half_bias = sb("half_bias", [P, 4])
    stats0, mv0, ve0, rstd0 = pair("stats0", [G, 6]), pair("mv0", [G, 2]), pair("ve0", [G, 1]), pair("rstd0", [G, 1])
    stats4, mv4, ve4, rstd4 = pair("stats4", [G, 6]), pair("mv4", [G, 2]), pair("ve4", [G, 1]), pair("rstd4", [G, 1])
    stats5, mv5, ve5, rstd5 = pair("stats5", [G, 6]), pair("mv5", [G, 2]), pair("ve5", [G, 1]), pair("rstd5", [G, 1])
    x0 = pair("x0", [G, P])
    x0T = pair("x0T", [P, G])
    relu1, gate1, x1T = pair("relu1", [P, G]), pair("gate1", [P, G]), pair("x1T", [P, G])
    relu2, gate2, x2T = pair("relu2", [P, G]), pair("gate2", [P, G]), pair("x2T", [P, G])
    mixa, mixb = sb("mixa", [P, G]), sb("mixb", [P, G])
    aT = pair("aT", [P, G])
    x2 = pair("x2", [G, P])
    g1b = sb("g1b", [G, 1])
    ga, gm, gneg = sb("ga", [G, G]), pair("gm", [G, G]), pair("gneg", [G, 1])
    gmax = sb("gmax", [G, 1])
    ge, gp = pair("ge", [G, G]), pair("gp", [G, G])
    gx, gsum, grec = sb("gx", [G, G]), sb("gsum", [G, 1]), sb("grec", [G, 1])
    gpT = pair("gpT", [G, G])
    attT = pair("attT", [P, G])
    tr, tz, zs, yT = pair("tr", [P, G]), pair("tz", [P, G]), pair("zs", [P, G]), pair("yT", [P, G])
    rx = sb("rx", [P, G])
    x4 = pair("x4", [G, P])
    x4T = pair("x4T", [P, G])
    qT = pair("qT", [P, G])
    kb = pair("kb_", [P, HEADS, G])
    v17 = pair("v17", [G, HEADS, HD + 1])
    mx = pair("mx_", [G, HEADS])
    s2 = pair("s2_", [G, HEADS, G])
    ex = pair("ex_", [G, HEADS, G])
    pT = pair("pT_", [G, HEADS, G])
    rs = pair("rs_", [G, HEADS])
    on = pair("on_", [G, HEADS, HD])
    oT = pair("oT_", [P, G])
    y5 = pair("y5", [G, P])
    nb = pair("nb", [G, P])
    tT = pair("tT", [P, G])

    names = ("consts halves x0_done x0T_done x0T_copied hw1_done gate1_done mixa_done mixb_done x1_done hw2_done "
             "gate2_done mix2a_done mix2b_done x2_done aT_done x2t_done x2_copied gram_done g1b_done ga_done gm_done "
             "gmax_done gneg_done ge_done gx_done grec_done gp_done gpT_done gpT_copied att_done att_copied rz_done "
             "tr_done tz_done rz_copied rx_done yT_done y_done h3_done mv0_done ve0_done rstd0_done mv4_done ve4_done "
             "rstd4_done mv5_done ve5_done rstd5_done x4_done xb_done x4T_done x4T_copied q_done_ q_copied k_done "
             "kb_done v_done v_copied s_done mx_done s2_done ex_done pT_done_ pT_copied_ pv_done_ rs_done on_done "
             "oT_done_ oT_copied_ wo_done y5_done nb_done nT_done tT_copied logits_done logits_kept").split()
    s = {n: sem(n) for n in names}
    loaded = sem("loaded")
    LOOP = (4, GROUPS // 2)
    USERS = {
        "U0": [("gather", 2, "att_copied"), ("x2", 1, "x2_copied"), ("x4", 2, "x4T_copied"), ("gp", 1, "gpT_copied")],
        "U1": [("n", 6, "tT_copied"), ("o", 5, "oT_copied_"), ("x0", 0, "x0T_copied")],
        "MM": [("highway1", 1, "gate1_done"), ("gates", 2, "rz_copied"), ("highway2", 1, "gate2_done"),
               ("q", 2, "q_copied")],
        "WD": [("logits", 6, "logits_kept"), ("y", 2, "h3_done"), ("gram", 1, "ga_done"), ("out", 5, "y5_done"),
               ("v", 4, "v_copied"), ("k", 2, "kb_done")],
        "S": [("s", 3, "s2_done")],
        "T": [("probs", 5, "on_done")],
    }

    def done(eng, name, t):
        eng.wait_ge(s[name], t.n + 1)

    def reused(eng, name, t):
        after(eng, s[name], t.n - 1)

    def bank_read(eng, bank, user, t):
        users = USERS[bank]
        at = [name for name, _, _ in users].index(user)
        step = t.n + users[at][1]
        for back in range(1, len(users) + 1):
            _, lag, read = users[(at - back) % len(users)]
            n = step - (back > at) - lag
            if not isinstance(n, int):
                return eng.wait_ge(s[read], n + 1)
            if 0 <= n < GROUPS:
                return eng.wait_ge(s[read], n + 1)

    block = ctx.enter_context(nc.Block())

    @block.sync
    def _(sp):
        sp.wait_ge(pads_zero, 16)
        for q in stored:
            sp.wait_ge(q, 16 * TILES)
        rows = hs_dram.rearrange("(g p) e -> p g e", p=G)
        sp.dma_start(h_all[:, 0:2, :], rows[:, 0:2, :]).then_inc(loaded, 16)
        sp.wait_ge(loaded, 16)
        sp.dma_start(h_all[:, 2:GROUPS, :], rows[:, 2:GROUPS, :]).then_inc(loaded, 16)

        sp.dma_start(sorted_dram.rearrange("(t p) e -> p t e", p=P), over(zeros, 1, SLOT_TILES, [P, SLOT_TILES, P]))\
          .then_inc(slots_zero, 16)
        for there, here in loads:
            sp.dma_start(there[:, :], here).then_inc(experts_in, 16)

        def keep(t):
            done(sp, "nb_done", t)
            sp.dma_start(n_all[:, t.n, :], nb[t.par][:, :]).then_inc(kept[t.par], 16)

        pipeline(sp, [(keep, 6)], GROUPS, *LOOP)
        for q in kept:
            sp.wait_ge(q, 16 * GROUPS // 2)

    @block.gpsimd
    def _(pool):
        nc.gpsimd.memset(half_col[:, :], 0.5).then_inc(s["consts"], 1)
        nc.gpsimd.memset(pow_col[:, :], -0.5).then_inc(s["consts"], 1)
        nc.gpsimd.memset(v17[0][:, :, :], 1.0).then_inc(s["consts"], 1)
        nc.gpsimd.memset(v17[1][:, :, :], 1.0).then_inc(s["consts"], 1)
        pool.wait_ge(s["consts"], 4)

        def root(k, ve, rstd, used):
            def stage(t):
                done(pool, f"ve{k}_done", t)
                reused(pool, used, t)
                nc.gpsimd.tensor_tensor(rstd[t.par][:, :], ve[t.par][:, :], pow_col[0:G, :], ALU.pow)\
                  .then_inc(s[f"rstd{k}_done"], 1)
            return stage

        pipeline(pool, [(root(0, ve0, rstd0, "x0_done"), 0), (root(4, ve4, rstd4, "x4_done"), 2),
                        (root(5, ve5, rstd5, "nb_done"), 5)], GROUPS, *LOOP)

    @block.tensor
    def _(pe):
        pe.wait_ge(weights1_in, 16)
        pe.wait_ge(s["consts"], 6)

        def highway(k, xin, x_name):
            def stage(t):
                done(pe, x_name, t)
                bank_read(pe, "MM", f"highway{k + 1}", t)
                nc.tensor.matmul(MM[:, 0:G], V("tW", k * P, (k + 1) * P), xin[t.par][:, :], start=True, stop=True)
                nc.tensor.matmul(MM[:, G:2 * G], V("cW", k * P, (k + 1) * P), xin[t.par][:, :], start=True, stop=True)\
                  .then_inc(s[f"hw{k + 1}_done"], 1)
            return stage

        def gather(t):
            done(pe, "gpT_copied", t)
            done(pe, "x2_copied", t)
            bank_read(pe, "U0", "gather", t)
            nc.tensor.matmul(U0[:, 0:G], x2[t.par][:, :], gpT[t.par][:, :], start=True, stop=True)\
              .then_inc(s["att_done"], 1)

        def turn_probs(t):
            done(pe, "ex_done", t)
            bank_read(pe, "T", "probs", t)
            for h in range(HEADS):
                mm = nc.tensor.transpose((T0, T1)[h // HALF][0:G, (h % HALF) * G:(h % HALF + 1) * G],
                                         ex[t.par][:, h, :], Wident[0:G, 0:G])
            mm.then_inc(s["pT_done_"], 1)

        def gates(t):
            done(pe, "att_copied", t)
            bank_read(pe, "MM", "gates", t)
            for j, name in enumerate(("fr", "ff")):
                nc.tensor.matmul(MM[:, j * G:(j + 1) * G], V(name, 0, P), x0T[t.par][:, :], start=True, stop=False)
                mm = nc.tensor.matmul(MM[:, j * G:(j + 1) * G], V(name, P, 2 * P), attT[t.par][:, :],
                                      start=False, stop=True)
            mm.then_inc(s["rz_done"], 1)

        def turn_n(t):
            done(pe, "nb_done", t)
            bank_read(pe, "U1", "n", t)
            nc.tensor.transpose(U1[:, 0:G], nb[t.par][:, :], Wident[0:G, 0:G]).then_inc(s["nT_done"], 1)

        def logits(t):
            done(pe, "tT_copied", t)
            bank_read(pe, "WD", "logits", t)
            nc.tensor.matmul(WD[0:G, 0:EXPERTS], tT[t.par][:, :], V("gate"), start=True, stop=True)\
              .then_inc(s["logits_done"], 1)

        def attend(t):
            done(pe, "pT_copied_", t)
            done(pe, "v_copied", t)
            for h in range(HEADS):
                mm = nc.tensor.matmul(T0[0:G, h * (HD + 1):(h + 1) * (HD + 1)], pT[t.par][:, h, :],
                                      v17[t.par][:, h, :], start=True, stop=True)
            mm.then_inc(s["pv_done_"], 1)

        def turn_y(t):
            done(pe, "yT_done", t)
            bank_read(pe, "WD", "y", t)
            nc.tensor.transpose(WD[0:G, 0:P], yT[t.par][:, :], Wident).then_inc(s["y_done"], 1)

        def gram(t):
            done(pe, "x2_done", t)
            bank_read(pe, "U0", "x2", t)
            nc.tensor.transpose(U0[0:G, 0:P], x2T[t.par][:, :], Wident).then_inc(s["x2t_done"], 1)
            done(pe, "aT_done", t)
            bank_read(pe, "WD", "gram", t)
            nc.tensor.matmul(WD[0:G, G:G + 1], x2T[t.par][:, :], col("a1"), start=True, stop=True)
            nc.tensor.matmul(WD[0:G, 0:G], aT[t.par][:, :], x2T[t.par][:, :], start=True, stop=True)\
              .then_inc(s["gram_done"], 1)

        def scores(b):
            def stage(t):
                if b == 0:
                    done(pe, "q_copied", t)
                    done(pe, "kb_done", t)
                    bank_read(pe, "S", "s", t)
                S = (S0, S1)[b]
                nc.tensor.matmul(S[0:G, 0:HALF * G], member[:, :], apart[:, :], start=True, stop=False)
                mm = nc.tensor.matmul(S[0:G, 0:HALF * G], qT[t.par][:, :],
                                      kb[t.par][:, b * HALF:(b + 1) * HALF, :].rearrange("p h j -> p (h j)"),
                                      start=False, stop=True)
                if b == 1:
                    mm.then_inc(s["s_done"], 1)
            return stage

        def turn_o(t):
            done(pe, "on_done", t)
            bank_read(pe, "U1", "o", t)
            nc.tensor.transpose(U1[:, 0:G], on[t.par][:, :, :].rearrange("p h d -> p (h d)"), Wident[0:G, 0:G])\
              .then_inc(s["oT_done_"], 1)

        def project_out(t):
            done(pe, "oT_copied_", t)
            bank_read(pe, "WD", "out", t)
            nc.tensor.matmul(WD[0:G, 0:P], oT[t.par][:, :], V("Wo"), start=True, stop=True).then_inc(s["wo_done"], 1)

        def values(t):
            bank_read(pe, "WD", "v", t)
            done(pe, "x4T_copied", t)
            nc.tensor.matmul(WD[0:G, 0:P], x4T[t.par][:, :], V("Wv"), start=True, stop=True).then_inc(s["v_done"], 1)

        def turn_x4(t):
            done(pe, "x4_done", t)
            bank_read(pe, "U0", "x4", t)
            nc.tensor.transpose(U0[:, 0:G], x4[t.par][:, :], Wident[0:G, 0:G]).then_inc(s["x4T_done"], 1)

        def turn_x0(t):
            done(pe, "x0_done", t)
            bank_read(pe, "U1", "x0", t)
            nc.tensor.transpose(U1[:, 0:G], x0[t.par][:, :], Wident[0:G, 0:G]).then_inc(s["x0T_done"], 1)

        def turn_gp(t):
            done(pe, "gp_done", t)
            bank_read(pe, "U0", "gp", t)
            nc.tensor.transpose(U0[0:G, 0:G], gp[t.par][:, :], Wident[0:G, 0:G]).then_inc(s["gpT_done"], 1)

        def queries_keys(t):
            done(pe, "x4T_copied", t)
            bank_read(pe, "MM", "q", t)
            nc.tensor.matmul(MM[:, 0:G], V("Wq"), x4T[t.par][:, :], start=True, stop=True).then_inc(s["q_done_"], 1)
            bank_read(pe, "WD", "k", t)
            nc.tensor.matmul(WD[:, 0:G], V("Wk"), x4T[t.par][:, :], start=True, stop=True).then_inc(s["k_done"], 1)

        pipeline(pe, [(highway(0, x0T, "x0T_copied"), 1), (gather, 2), (turn_probs, 5),
                      (gates, 2), (turn_n, 6), (highway(1, x1T, "x1_done"), 1),
                      (logits, 6), (attend, 5), (turn_y, 2), (gram, 1), (scores(0), 3), (turn_o, 5),
                      (scores(1), 3), (project_out, 5), (values, 4), (turn_x4, 2), (turn_x0, 0), (turn_gp, 1),
                      (queries_keys, 2)], GROUPS, *LOOP)

    @block.scalar
    def _(act):
        act.wait_ge(s["halves"], 4)
        act.wait_ge(s["consts"], 6)

        def exponentials(t):
            done(act, "s2_done", t)
            reused(act, "pT_done_", t)
            nc.scalar.activation(ex[t.par][:, :, :], s2[t.par][:, :, :], ACT.Exp, scale=SCALE).then_inc(s["ex_done"], 1)

        def highway(k, relu, gate, used):
            def stage(t):
                done(act, f"hw{k + 1}_done", t)
                reused(act, used, t)
                nc.scalar.activation(relu[t.par][:, :], MM[:, 0:G], ACT.Relu, bias=col(f"tb{k}"))
                nc.scalar.activation(gate[t.par][:, :], MM[:, G:2 * G], ACT.Tanh, scale=0.5,
                                     bias=half_bias[:, k:k + 1]).then_inc(s[f"gate{k + 1}_done"], 1)
            return stage

        def copy(out, src, ready, used, now, **how):
            def stage(t):
                done(act, ready, t)
                reused(act, used, t)
                nc.scalar.activation(out(t), src, ACT.Identity, **how).then_inc(s[now], 1)
            return stage

        def copy_probs(t):
            done(act, "pT_done_", t)
            reused(act, "pv_done_", t)
            for b, T in enumerate((T0, T1)):
                a = nc.scalar.activation(pT[t.par][:, b * HALF:(b + 1) * HALF, :].rearrange("p h j -> p (h j)"),
                                         T[0:G, 0:HALF * G], ACT.Identity)
            a.then_inc(s["pT_copied_"], 1)

        def gates(t):
            done(act, "rz_done", t)
            reused(act, "yT_done", t)
            nc.scalar.activation(tr[t.par][:, :], MM[:, 0:G], ACT.Tanh, scale=0.5, bias=half_bias[:, 2:3])\
              .then_inc(s["tr_done"], 1)
            nc.scalar.activation(tz[t.par][:, :], MM[:, G:2 * G], ACT.Tanh, scale=0.5, bias=half_bias[:, 3:4])\
              .then_inc(s["rz_copied"], 1)
            done(act, "rz_copied", t)
            nc.scalar.activation(zs[t.par][:, :], tz[t.par][:, :], ACT.Square, scale=0.5, bias=half_col[:, 0:1])\
              .then_inc(s["tz_done"], 1)

        def weigh(t):
            done(act, "x2_done", t)
            reused(act, "gram_done", t)
            nc.scalar.activation(aT[t.par][:, :], x2T[t.par][:, :], ACT.Identity, scale=col("a3"), bias=col("a2"))\
              .then_inc(s["aT_done"], 1)

        def gate_exp(t):
            done(act, "gneg_done", t)
            reused(act, "gx_done", t)
            nc.scalar.activation(ge[t.par][:, :], gm[t.par][:, :], ACT.Exp, bias=gneg[t.par][:, 0:1])\
              .then_inc(s["ge_done"], 1)

        pipeline(act, [
            (exponentials, 4), (highway(0, relu1, gate1, "x1_done"), 1),
            (copy(lambda t: attT[t.par][:, :], U0[:, 0:G], "att_done", "rz_done", "att_copied"), 2),
            (copy_probs, 5), (gates, 2),
            (copy(lambda t: tT[t.par][:, :], U1[:, 0:G], "nT_done", "logits_done", "tT_copied",
                  scale=col("g"), bias=col("b")), 6),
            (highway(1, relu2, gate2, "x2_done"), 1), (weigh, 1),
            (copy(lambda t: x2[t.par][:, :], U0[0:G, 0:P], "x2t_done", "att_done", "x2_copied"), 1),
            (copy(lambda t: oT[t.par][:, :], U1[:, 0:G], "oT_done_", "wo_done", "oT_copied_", bias=col("bv1")), 5),
            (gate_exp, 1),
            (copy(lambda t: x4T[t.par][:, :], U0[:, 0:G], "x4T_done", "v_done", "x4T_copied"), 2),
            (copy(lambda t: x0T[t.par][:, :], U1[:, 0:G], "x0T_done", "yT_done", "x0T_copied"), 0),
            (copy(lambda t: gpT[t.par][:, :], U0[0:G, 0:G], "gpT_done", "att_done", "gpT_copied"), 1),
            (copy(lambda t: qT[t.par][:, :], MM[:, 0:G], "q_done_", "s_done", "q_copied", bias=col("bq1")), 2)],
            GROUPS, *LOOP)

    @block.vector
    def _(dve):
        dve.wait_ge(weights1_in, 16)
        for i, name in enumerate(("cb0", "cb1", "frb", "ffb")):
            nc.vector.tensor_scalar(half_bias[:, i:i + 1], col(name), 0.5, None, ALU.mult).then_inc(s["halves"], 1)
        nc.vector.tensor_copy(member[:, :], V("member", rows_=IMG_G)).then_inc(s["consts"], 1)
        nc.vector.tensor_copy(apart[:, :], V("apart", rows_=IMG_G)).then_inc(s["consts"], 1)
        dve.wait_ge(s["consts"], 6)

        def moments(k, src, stats, mv, ve):
            def run(t):
                dve.drain()
                nc.vector.bn_stats(stats[t.par][:, :], src)
                dve.drain()
                nc.vector.bn_aggr(mv[t.par][:, :], stats[t.par][:, :]).then_inc(s[f"mv{k}_done"], 1)
                done(dve, f"mv{k}_done", t)
                reused(dve, f"rstd{k}_done", t)
                nc.vector.tensor_scalar(ve[t.par][:, :], mv[t.par][:, 1:2], EPS, None, ALU.add)\
                  .then_inc(s[f"ve{k}_done"], 1)
            return run

        def scale(out, src, k, mv, rstd, used, now):
            def stage(t):
                done(dve, f"rstd{k}_done", t)
                reused(dve, used, t)
                nc.vector.tensor_scalar(out[t.par][:, :], src(t), mv[t.par][:, 0:1], rstd[t.par][:, 0:1],
                                        ALU.subtract, ALU.mult).then_inc(s[now], 1)
            return stage

        def norm5(t):
            reused(dve, "nT_done", t)
            after(dve, kept[t.par], 16 * t.half)
            scale(nb, lambda t: y5[t.par][:, :], 5, mv5, rstd5, "nT_done", "nb_done")(t)

        def highway(k, x, relu, gate, out, used, a_done, b_done, now):
            def stage(t):
                done(dve, f"gate{k + 1}_done", t)
                after(dve, s[b_done], t.n)
                nc.vector.tensor_tensor(mixa[:, :], relu[t.par][:, :], x[t.par][:, :], ALU.subtract)\
                  .then_inc(s[a_done], 1)
                done(dve, a_done, t)
                after(dve, s[now], t.n)
                nc.vector.scalar_tensor_tensor(out=mixb[:, :], in0=gate[t.par][:, :], scalar=1.0, in1=mixa[:, :],
                                               op0=ALU.add, op1=ALU.mult).then_inc(s[b_done], 1)
                done(dve, b_done, t)
                reused(dve, used, t)
                nc.vector.scalar_tensor_tensor(out=out[t.par][:, :], in0=mixb[:, :], scalar=0.5, in1=x[t.par][:, :],
                                               op0=ALU.mult, op1=ALU.add).then_inc(s[now], 1)
            return stage

        def first_moments(t):
            dve.wait_ge(loaded, 16)
            if not isinstance(t.n, int) or t.n >= 2:
                dve.wait_ge(loaded, 32)
            reused(dve, "x0_done", t)
            moments(0, h_all[:, t.n, :], stats0, mv0, ve0)(t)

        def mix(t):
            done(dve, "tz_done", t)
            after(dve, s["yT_done"], t.n)
            nc.vector.scalar_tensor_tensor(out=rx[:, :], in0=tr[t.par][:, :], scalar=1.0, in1=x0T[t.par][:, :],
                                           op0=ALU.add, op1=ALU.mult).then_inc(s["rx_done"], 1)
            done(dve, "rx_done", t)
            reused(dve, "y_done", t)
            nc.vector.scalar_tensor_tensor(out=yT[t.par][:, :], in0=rx[:, :], scalar=0.5, in1=zs[t.par][:, :],
                                           op0=ALU.mult, op1=ALU.add).then_inc(s["yT_done"], 1)

        def keep_logits(t):
            done(dve, "logits_done", t)
            nc.vector.tensor_tensor(lg_all[:, t.n, :], WD[0:G, 0:EXPERTS], row("gate_b", G), ALU.add)\
              .then_inc(s["logits_kept"], 1)

        def divide(t):
            o = T0[0:G, 0:HEADS * (HD + 1)].rearrange("p (h d) -> p h d", h=HEADS)
            done(dve, "pv_done_", t)
            nc.vector.reciprocal(rs[t.par][:, :], o[:, :, HD]).then_inc(s["rs_done"], 1)
            done(dve, "rs_done", t)
            reused(dve, "oT_done_", t)
            nc.vector.tensor_tensor(on[t.par][:, :, :], o[:, :, 0:HD], over(rs[t.par][:, :], 2, HD, [G, HEADS, HD]),
                                    ALU.mult).then_inc(s["on_done"], 1)

        def third_residual(t):
            reused(dve, "x4_done", t)
            done(dve, "y_done", t)
            nc.vector.tensor_tensor(h_all[:, t.n, :], h_all[:, t.n, :], WD[0:G, 0:P], ALU.add)\
              .then_inc(s["h3_done"], 1)
            moments(4, h_all[:, t.n, :], stats4, mv4, ve4)(t)

        def gate_scores(t):
            done(dve, "gram_done", t)
            after(dve, s["gm_done"], t.n)
            nc.vector.tensor_tensor(g1b[:, :], WD[0:G, G:G + 1], col("ab", G), ALU.add).then_inc(s["g1b_done"], 1)
            done(dve, "g1b_done", t)
            nc.vector.tensor_scalar(ga[:, :], WD[0:G, 0:G], g1b[:, 0:1], 0.0, ALU.add, ALU.max)\
              .then_inc(s["ga_done"], 1)
            done(dve, "ga_done", t)
            reused(dve, "ge_done", t)
            nc.vector.tensor_tensor(gm[t.par][:, :], ga[:, :], V("same", rows_=G), ALU.mult).then_inc(s["gm_done"], 1)
            done(dve, "gm_done", t)
            nc.vector.tensor_reduce(gmax[:, :], gm[t.par][:, :], X, ALU.max).then_inc(s["gmax_done"], 1)
            done(dve, "gmax_done", t)
            nc.vector.tensor_scalar(gneg[t.par][:, :], gmax[:, :], -1.0, None, ALU.mult).then_inc(s["gneg_done"], 1)

        def gate_probs(t):
            done(dve, "ge_done", t)
            after(dve, s["gp_done"], t.n)
            nc.vector.tensor_tensor(gx[:, :], ge[t.par][:, :], V("same", rows_=G), ALU.mult).then_inc(s["gx_done"], 1)
            done(dve, "gx_done", t)
            nc.vector.tensor_reduce(gsum[:, :], gx[:, :], X, ALU.add).then_inc(s["grec_done"], 1)
            dve.wait_ge(s["grec_done"], 2 * t.n + 1)
            nc.vector.reciprocal(grec[:, :], gsum[:, :]).then_inc(s["grec_done"], 1)
            dve.wait_ge(s["grec_done"], 2 * t.n + 2)
            reused(dve, "gpT_done", t)
            nc.vector.tensor_scalar(gp[t.par][:, :], gx[:, :], grec[:, 0:1], None, ALU.mult).then_inc(s["gp_done"], 1)

        def scale4(t):
            scale(x4, lambda t: h_all[:, t.n, :], 4, mv4, rstd4, "x4T_done", "x4_done")(t)
            done(dve, "x4_done", t)
            nc.vector.tensor_tensor(xb_all[:, t.n, :], x4[t.par][:, :], row("bo", G), ALU.add).then_inc(s["xb_done"], 1)

        def fourth_residual(t):
            done(dve, "wo_done", t)
            reused(dve, "nb_done", t)
            nc.vector.tensor_tensor(y5[t.par][:, :], WD[0:G, 0:P], xb_all[:, t.n, :], ALU.add).then_inc(s["y5_done"], 1)
            moments(5, y5[t.par][:, :], stats5, mv5, ve5)(t)

        def values(t):
            done(dve, "v_done", t)
            reused(dve, "pv_done_", t)
            nc.vector.tensor_copy(v17[t.par][:, :, 0:HD], WD[0:G, 0:P].rearrange("p (h d) -> p h d", h=HEADS))\
              .then_inc(s["v_copied"], 1)

        def less_max(t):
            done(dve, "s_done", t)
            for b, S in enumerate((S0, S1)):
                nc.vector.tensor_reduce(mx[t.par][:, b * HALF:(b + 1) * HALF],
                                        S[0:G, 0:HALF * G].rearrange("p (h j) -> p h j", h=HALF), X, ALU.max)\
                  .then_inc(s["mx_done"], 1)
            reused(dve, "ex_done", t)
            dve.wait_ge(s["mx_done"], 2 * t.n + 2)
            for b, S in enumerate((S0, S1)):
                hs = slice(b * HALF, (b + 1) * HALF)
                ins = nc.vector.tensor_tensor(s2[t.par][:, hs, :], S[0:G, 0:HALF * G].rearrange("p (h j) -> p h j", h=HALF),
                                              over(mx[t.par][:, hs], 2, G, [G, HALF, G]), ALU.subtract)
            ins.then_inc(s["s2_done"], 1)

        def keys(t):
            done(dve, "k_done", t)
            reused(dve, "s_done", t)
            nc.vector.scalar_tensor_tensor(out=kb[t.par][:, :, :], in0=over(WD[:, 0:G], 1, HEADS, [P, HEADS, G]),
                                           scalar=col("bk1"), in1=over(w_head_mask, 2, G, [P, HEADS, G]),
                                           op0=ALU.add, op1=ALU.mult).then_inc(s["kb_done"], 1)

        pipeline(dve, [
            (norm5, 6), (highway(0, x0T, relu1, gate1, x1T, "hw2_done", "mixa_done", "mixb_done", "x1_done"), 1),
            (first_moments, 0), (mix, 2),
            (highway(1, x1T, relu2, gate2, x2T, "gram_done", "mix2a_done", "mix2b_done", "x2_done"), 1),
            (keep_logits, 6), (divide, 5), (third_residual, 2),
            (scale(x0, lambda t: h_all[:, t.n, :], 0, mv0, rstd0, "x0T_done", "x0_done"), 0),
            (gate_scores, 1), (scale4, 2), (gate_probs, 1), (fourth_residual, 5), (values, 4), (less_max, 3),
            (keys, 2)], GROUPS, *LOOP)


def block2(nc, ctx, sem, banks, V, col, Wident, h_all, n_all, lg_all, W1_sb, W2_sb, b1_sb, b2_sb, experts_in,
           sorted_dram, expert_dram, out, slots_zero, kept):
    def sb(name, shape, dt=F32):
        return ctx.enter_context(nc.sbuf_tensor(name, shape, dt))

    def pair(name, shape, dt=F32):
        return [sb(f"{name}{i}", shape, dt) for i in range(2)]

    NT, HB, HT, YB, RB = banks[0], banks[1], banks[2], banks[3], banks[4]
    GE = [G, GROUPS, EXPERTS]
    BATCH = 4
    LASTG = TOKENS - (GROUPS - 1) * G

    top = sb("top", [G, GROUPS])
    less = sb("less", GE)
    expo = sb("expo", GE)
    esum = sb("esum", [G, GROUPS])
    weight = sb("weight", [G, GROUPS])
    cand = sb("cand", GE)
    first = sb("first", [G, GROUPS])
    hot = sb("hot", GE)
    hotv = sb("hotv", GE)
    hotb = sb("hotb", GE, BF16)
    before_b, ones_b = sb("before_b", [G, G], BF16), sb("ones_b", [G, G], BF16)
    count = sb("count", [G, EXPERTS])
    over_t = sb("over_t", [G, EXPERTS, TILES])
    tiles_e = sb("tiles_e", [G, EXPERTS])
    sofar = sb("sofar", [G, EXPERTS, EXPERTS])
    start = sb("start", [G, EXPERTS])
    end = sb("end", [G, EXPERTS])
    slot_e = sb("slot_e", GE)
    slot_h = sb("slot_h", GE)
    slot_f = sb("slot_f", [G, GROUPS])
    slot = sb("slot", [G, GROUPS], I32)
    past = sb("past", [G, SLOT_TILES, EXPERTS])
    owner_f, owner_c = sb("owner_f", [G, SLOT_TILES]), sb("owner_c", [G, SLOT_TILES])
    owner = sb("owner", [G, SLOT_TILES], I32)
    nt = pair("nt", [P, P])
    tT = pair("t2T", [P, P])
    hb = pair("hb", [P, FF])
    hg = pair("hg", [P, FF])
    hT = pair("hT", [P, FF])
    ye = pair("ye", [P, P])
    back = sb("back", [G, GROUPS, P])
    res = sb("res", [G, GROUPS, P])

    names = ("routed expo_done hot_ready ranks_done slots_done owners_done exp_copied "
             "nT_done2 tT_done2 hid_done hb_done hg_done hT_done hT_copied y_done2 ye_done").split()
    s = {n: sem(n) for n in names}
    sorted_in = sem("sorted_in")
    nt_in = [sem("nt_in_even"), sem("nt_in_odd")]
    y_out = [sem("y_out_even"), sem("y_out_odd")]
    gathered = [sem(f"gathered{i}") for i in range(-(-GROUPS // BATCH))]
    finished = sem("finished")
    back_clear = sem("back_clear")
    out_done = sem("out_done")
    LOOP = (3, (SLOT_TILES - 1) // 2)

    def done(eng, name, t):
        eng.wait_ge(s[name], t.n + 1)

    def reused(eng, name, t):
        after(eng, s[name], t.n - 1)

    block = ctx.enter_context(nc.Block())

    @block.gpsimd
    def _(pool):
        for q in kept:
            pool.wait_ge(q, 16 * GROUPS // 2)
        pool.wait_ge(slots_zero, 16)
        pool.wait_ge(s["slots_done"], 1)
        for g in range(GROUPS):
            rows = G if g < GROUPS - 1 else LASTG
            pool.indirect_dma_start(out=sorted_dram, out_offset=bass.IndirectOffsetOnAxis(ap=slot[0:rows, g:g + 1], axis=0),
                                    in_=n_all[0:rows, g, :], in_offset=None).then_inc(sorted_in, 16)
        nc.gpsimd.memset(back[:, :, :], 0.0).then_inc(back_clear, 1)
        pool.wait_ge(back_clear, 1)
        for i, q in enumerate(y_out):
            pool.wait_ge(q, 16 * ((SLOT_TILES + 1 - i) // 2))
        for g in range(GROUPS):
            rows = G if g < GROUPS - 1 else LASTG
            pool.indirect_dma_start(out=back[0:rows, g, :], out_offset=None, in_=expert_dram,
                                    in_offset=bass.IndirectOffsetOnAxis(ap=slot[0:rows, g:g + 1], axis=0))\
                .then_inc(gathered[g // BATCH], 16)

    @block.sync
    def _(sp):
        sp.wait_ge(sorted_in, 16 * GROUPS)

        def load(t):
            after(sp, s["nT_done2"], t.n - 1)
            sp.dma_start(nt[t.par][:, :], sorted_dram.rearrange("(t p) e -> t p e", p=P)[t.n])\
              .then_inc(nt_in[t.par], 16)

        def store(t):
            done(sp, "ye_done", t)
            sp.dma_start(expert_dram.rearrange("(t p) e -> t p e", p=P)[t.n], ye[t.par][:, :])\
              .then_inc(y_out[t.par], 16)

        pipeline(sp, [(load, 0), (store, 4)], SLOT_TILES, *LOOP)
        for g in range(GROUPS):
            rows = G if g < GROUPS - 1 else LASTG
            sp.wait_ge(finished, g + 1)
            sp.dma_start(out[g * G:g * G + rows, :], res[0:rows, g, :]).then_inc(out_done, 16)
        sp.wait_ge(out_done, 16 * GROUPS)

    @block.tensor
    def _(pe):
        pe.wait_ge(s["hot_ready"], 3)
        R = RB[0:G, 0:GROUPS * EXPERTS]
        nc.tensor.matmul(R, before_b[:, :], hotb[:, :, :].rearrange("p g e -> p (g e)"), start=True, stop=False)
        for g in range(GROUPS - 1):
            later = GROUPS - 1 - g
            nc.tensor.matmul(R[:, (g + 1) * EXPERTS:], ones_b[:, :], over(hotb[:, g, :], 1, later, [G, later, EXPERTS]),
                             start=False, stop=(g == GROUPS - 2))
        for g in range(GROUPS):
            mm = nc.tensor.matmul(RB[0:G, GROUPS * EXPERTS:(GROUPS + 1) * EXPERTS], ones_b[:, :], hotb[:, g, :],
                                  start=(g == 0), stop=(g == GROUPS - 1))
        mm.then_inc(s["ranks_done"], 1)
        pe.wait_ge(s["owners_done"], 1)
        pe.wait_ge(experts_in, 64)

        def turn_n(t):
            pe.wait_ge(nt_in[t.par], 16 * (t.half + 1))
            after(pe, s["tT_done2"], t.n)
            nc.tensor.transpose(NT[:, 0:P], nt[t.par][:, :], Wident).then_inc(s["nT_done2"], 1)

        def hidden(t):
            e = pe.value_load(owner[0:1, bass.ds(t.n, 1)], min_val=0, max_val=EXPERTS - 1)
            done(pe, "tT_done2", t)
            after(pe, s["hb_done"], t.n)
            nc.tensor.matmul(HB[:, :], tT[t.par][:, :], W1_sb[:, bass.ds(e * FF, FF)], start=True, stop=True)\
              .then_inc(s["hid_done"], 1)

        def turn_h(t):
            done(pe, "hg_done", t)
            after(pe, s["hT_copied"], t.n)
            for c in range(FC):
                mm = nc.tensor.transpose(HT[:, c * P:(c + 1) * P], hg[t.par][:, c * P:(c + 1) * P], Wident)
            mm.then_inc(s["hT_done"], 1)

        def expert_out(t):
            e = pe.value_load(owner[0:1, bass.ds(t.n, 1)], min_val=0, max_val=EXPERTS - 1)
            done(pe, "hT_copied", t)
            after(pe, s["ye_done"], t.n)
            for c in range(FC):
                mm = nc.tensor.matmul(YB[:, 0:P], hT[t.par][:, c * P:(c + 1) * P],
                                      W2_sb[:, bass.ds(e * FF + c * P, P)], start=(c == 0), stop=(c == FC - 1))
            mm.then_inc(s["y_done2"], 1)

        pipeline(pe, [(hidden, 1), (turn_n, 0), (expert_out, 3), (turn_h, 2)], SLOT_TILES, *LOOP)

    @block.scalar
    def _(act):
        act.wait_ge(s["routed"], 2)
        nc.scalar.activation(expo[:, :, :], less[:, :, :], ACT.Exp).then_inc(s["expo_done"], 1)

        def gain(t):
            done(act, "nT_done2", t)
            reused(act, "hid_done", t)
            nc.scalar.activation(tT[t.par][:, :], NT[:, 0:P], ACT.Identity, scale=col("g"), bias=col("b"))\
              .then_inc(s["tT_done2"], 1)

        def gelu(t):
            done(act, "hb_done", t)
            reused(act, "hT_done", t)
            nc.scalar.activation(hg[t.par][:, :], hb[t.par][:, :], ACT.Gelu_apprx_tanh).then_inc(s["hg_done"], 1)

        def copy_h(t):
            done(act, "hT_done", t)
            reused(act, "y_done2", t)
            nc.scalar.activation(hT[t.par][:, :], HT[:, :], ACT.Identity).then_inc(s["hT_copied"], 1)

        pipeline(act, [(gain, 0), (gelu, 1), (copy_h, 2)], SLOT_TILES, *LOOP)

    @block.vector
    def _(dve):
        k = [0]

        def chain(ins):
            k[0] += 1
            ins.then_inc(s["routed"], 1)
            dve.wait_ge(s["routed"], k[0])

        chain(nc.vector.tensor_reduce(top[:, :], lg_all[:, :, :], X, ALU.max))
        chain(nc.vector.tensor_tensor(less[:, :, :], lg_all[:, :, :], over(top[:, :], 2, EXPERTS, GE), ALU.subtract))
        chain(nc.vector.scalar_tensor_tensor(out=cand[:, :, :], in0=less[:, :, :], scalar=0.0,
                                             in1=over(V("rank_w", rows_=G), 1, GROUPS, GE), op0=ALU.is_ge, op1=ALU.mult))
        chain(nc.vector.tensor_reduce(first[:, :], cand[:, :, :], X, ALU.max))
        chain(nc.vector.tensor_tensor(hot[:, :, :], cand[:, :, :], over(first[:, :], 2, EXPERTS, GE), ALU.is_equal))
        chain(nc.vector.tensor_tensor(hotv[:, :, :], hot[:, :, :], over(V("valid", rows_=G), 2, EXPERTS, GE), ALU.mult))
        nc.vector.tensor_copy(hotb[:, :, :], hotv[:, :, :]).then_inc(s["hot_ready"], 1)
        nc.vector.tensor_copy(before_b[:, :], V("before", rows_=G)).then_inc(s["hot_ready"], 1)
        nc.vector.tensor_copy(ones_b[:, :], V("ones", rows_=G)).then_inc(s["hot_ready"], 1)
        dve.wait_ge(s["expo_done"], 1)
        chain(nc.vector.tensor_reduce(esum[:, :], expo[:, :, :], X, ALU.add))
        chain(nc.vector.reciprocal(weight[:, :], esum[:, :]))
        dve.wait_ge(s["ranks_done"], 1)
        chain(nc.vector.tensor_copy(count[:, :], RB[0:G, GROUPS * EXPERTS:(GROUPS + 1) * EXPERTS]))
        chain(nc.vector.tensor_tensor(over_t[:, :, :], over(count[:, :], 2, TILES, [G, EXPERTS, TILES]),
                                      over(V("tile_lo", rows_=G), 1, EXPERTS, [G, EXPERTS, TILES]), ALU.is_gt))
        chain(nc.vector.tensor_reduce(tiles_e[:, :], over_t[:, :, :], X, ALU.add))
        chain(nc.vector.tensor_tensor(sofar[:, :, :], over(tiles_e[:, :], 1, EXPERTS, [G, EXPERTS, EXPERTS]),
                                      V("lower", rows_=G).rearrange("p (a b) -> p a b", a=EXPERTS), ALU.mult))
        chain(nc.vector.tensor_reduce(start[:, :], sofar[:, :, :], X, ALU.add))
        chain(nc.vector.scalar_tensor_tensor(out=slot_e[:, :, :], in0=over(start[:, :], 1, GROUPS, GE), scalar=float(P),
                                             in1=RB[0:G, 0:GROUPS * EXPERTS].rearrange("p (g e) -> p g e", g=GROUPS),
                                             op0=ALU.mult, op1=ALU.add))
        chain(nc.vector.tensor_tensor(slot_h[:, :, :], slot_e[:, :, :], hotv[:, :, :], ALU.mult))
        chain(nc.vector.tensor_reduce(slot_f[:, :], slot_h[:, :, :], X, ALU.add))
        nc.vector.tensor_copy(slot[:, :], slot_f[:, :]).then_inc(s["slots_done"], 1)
        chain(nc.vector.tensor_tensor(end[:, :], start[:, :], tiles_e[:, :], ALU.add))
        chain(nc.vector.tensor_tensor(past[:, :, :], over(V("tile_no", rows_=G), 2, EXPERTS, [G, SLOT_TILES, EXPERTS]),
                                      over(end[:, :], 1, SLOT_TILES, [G, SLOT_TILES, EXPERTS]), ALU.is_ge))
        chain(nc.vector.tensor_reduce(owner_f[:, :], past[:, :, :], X, ALU.add))
        chain(nc.vector.tensor_scalar(owner_c[:, :], owner_f[:, :], float(EXPERTS - 1), None, ALU.min))
        nc.vector.tensor_copy(owner[:, :], owner_c[:, :]).then_inc(s["owners_done"], 1)
        dve.wait_ge(s["owners_done"], 1)
        dve.wait_ge(experts_in, 64)

        def bias1(t):
            e = dve.value_load(owner[0:1, bass.ds(t.n, 1)], min_val=0, max_val=EXPERTS - 1)
            done(dve, "hid_done", t)
            reused(dve, "hg_done", t)
            nc.vector.tensor_tensor(hb[t.par][:, :], HB[:, :], b1_sb[:, bass.ds(e * FF, FF)], ALU.add)\
              .then_inc(s["hb_done"], 1)

        def bias2(t):
            e = dve.value_load(owner[0:1, bass.ds(t.n, 1)], min_val=0, max_val=EXPERTS - 1)
            done(dve, "y_done2", t)
            after(dve, y_out[t.par], 16 * t.half)
            nc.vector.tensor_tensor(ye[t.par][:, :], YB[:, 0:P], b2_sb[:, bass.ds(e * P, P)], ALU.add)\
              .then_inc(s["ye_done"], 1)

        pipeline(dve, [(bias1, 1), (bias2, 3)], SLOT_TILES, *LOOP)
        for g in range(GROUPS):
            rows = G if g < GROUPS - 1 else LASTG
            if g % BATCH == 0:
                dve.wait_ge(gathered[g // BATCH], 16 * min(BATCH, GROUPS - g))
            nc.vector.scalar_tensor_tensor(out=res[0:rows, g, :], in0=back[0:rows, g, :], scalar=weight[0:rows, g:g + 1],
                                           in1=h_all[0:rows, g, :], op0=ALU.mult, op1=ALU.add).then_inc(finished, 1)


def layout(x, w):
    f = np.float32
    a = {k: np.asarray(v) for k, v in w.items()}
    x = np.asarray(x)
    pt = x.reshape(IMAGES, 3, 6, 16, 6, 16).transpose(2, 4, 1, 3, 5, 0)
    pt = pt.reshape(TILES, 2, CHUNKS, P, IMAGES).transpose(0, 3, 2, 1, 4).reshape(TILES, P, CHUNKS * P)

    ident = np.eye(P, dtype=f)
    fh = np.arange(P)[:, None] // HD == np.arange(HEADS)[None, :]
    parity = np.arange(P)[:, None] // IMAGES == np.arange(HEADS)[None, :] % 2
    parts = {
        "tok": a["L0_tok_w"].T.reshape(CHUNKS, P, P).transpose(1, 0, 2).reshape(P, CHUNKS * P),
        "in_proj": a["L0_attn_in_proj_w"].T, "out_proj": a["L0_attn_out_proj_w"].T,
        "pos_w": a["L0_attn_pos_w"].T, "pos": a["L0_attn_pos_emb"][0, 0:REL].T,
        "ident": ident, "head_mask": fh.astype(f), "half_mask": parity.astype(f)}
    weights = np.concatenate([parts[n] for n, _ in _WEIGHTS], 1)

    g = np.arange(G)

    def pad(m):
        return np.concatenate([m, np.zeros((P - m.shape[0], m.shape[1]), f)], 0)

    same = (g[:, None] // POSITIONS == g[None, :] // POSITIONS).astype(f)
    member = (np.arange(IMG_G)[:, None] == g[None, :] // POSITIONS).astype(f)
    apart = np.where(member > 0, f(0), f(FAR))
    token = np.arange(GROUPS)[None, :] * G + np.arange(P)[:, None]
    parts = {
        "tW": a["L1_attn_tW"].transpose(1, 0, 2).reshape(P, 2 * P),
        "cW": a["L1_attn_cW"].transpose(1, 0, 2).reshape(P, 2 * P),
        "ff": a["L1_attn_ffW"].reshape(2, P, P).transpose(1, 0, 2).reshape(P, 2 * P),
        "fr": a["L1_attn_frW"].reshape(2, P, P).transpose(1, 0, 2).reshape(P, 2 * P),
        "Wq": a["L1_ffn_Wq"], "Wk": a["L1_ffn_Wk"], "Wv": a["L1_ffn_Wv"], "Wo": a["L1_ffn_Wo"],
        "gate": a["L1_ffn_gate_W"], "same": pad(same),
        "before": pad((g[:, None] < g[None, :]).astype(f)), "ones": np.ones((P, G), f),
        "member": pad(member), "apart": pad(np.tile(apart, (1, 4))),
        "valid": ((token < TOKENS) & (np.arange(P)[:, None] < G)).astype(f),
        "rank_w": np.tile(np.arange(EXPERTS, 0, -1, dtype=f), (P, 1)),
        "tile_lo": np.tile(np.arange(TILES, dtype=f) * P, (P, 1)),
        "tile_no": np.tile(np.arange(SLOT_TILES, dtype=f), (P, 1)),
        "lower": np.tile(np.tril(np.ones((EXPERTS, EXPERTS), f), -1).reshape(1, -1), (P, 1))}
    weights1 = np.concatenate([parts[n] for n, _ in _WEIGHTS1], 1)

    ipb, aw = a["L0_attn_in_proj_b"], a["L1_attn_aW"]
    columns = np.stack([
        ipb[0:P], ipb[P:2 * P], ipb[2 * P:], a["L0_attn_pos_bias_u"].reshape(P), a["L0_attn_pos_bias_v"].reshape(P),
        a["L1_attn_tb"][0], a["L1_attn_tb"][1], a["L1_attn_cb"][0], a["L1_attn_cb"][1], aw[0:P], aw[P:2 * P],
        aw[2 * P:], a["L1_attn_frb"], a["L1_attn_ffb"], a["L1_ffn_ln1_g"], a["L1_ffn_ln1_b"], a["L1_ffn_bq"],
        a["L1_ffn_bk"], a["L1_ffn_bv"], np.broadcast_to(a["L1_attn_ab"], (P,))], 1)
    rows = np.concatenate([a["L0_tok_b"], a["L0_attn_out_proj_b"], a["L1_ffn_bo"], a["L1_ffn_gate_b"]])
    rows = np.broadcast_to(rows[None, :], (P, WIDTH_R))
    return {
        "patches": pt, "weights": weights, "weights1": weights1, "columns": columns, "rows": rows,
        "b1_rows": np.broadcast_to(a["L1_ffn_b1"].reshape(1, EXPERTS * FF), (P, EXPERTS * FF)),
        "b2_rows": np.broadcast_to(a["L1_ffn_b2"].reshape(1, EXPERTS * P), (P, EXPERTS * P)),
        "W1": a["L1_ffn_W1"].transpose(1, 0, 2).reshape(P, EXPERTS * FF),
        "W2": a["L1_ffn_W2"].reshape(EXPERTS, FC, P, P).transpose(2, 0, 1, 3).reshape(P, EXPERTS * FC * P),
        "zeros": np.zeros((P, P), f)}


def kernel(x, **inputs):
    import concourse.bacc as _bacc
    from concourse.bass_utils import run_bass_kernel_spmd as _run

    nc = _bacc.Bacc("TRN2", target_bir_lowering=False, num_devices=1)
    arrays, args = {}, []
    for name, a in layout(x, inputs).items():
        a = np.ascontiguousarray(a)
        arrays[name] = a
        args.append(nc.dram_tensor(name, a.shape, mybir.dt.from_np(a.dtype), kind="ExternalInput").ap())
    args.append(nc.dram_tensor("out", (TOKENS, P), F32, kind="ExternalOutput").ap())
    for name, shape in (("bd_dram", (2, P, HEADS * REL)), ("hs_dram", (GROUPS * G, P)),
                        ("sorted_dram", (SLOT_TILES * P, P)), ("expert_dram", (SLOT_TILES * P, P))):
        args.append(nc.dram_tensor(name, shape, F32, kind="Internal").ap())
    tower(nc, *args)
    r = _run(nc, [arrays], core_ids=[0])
    return r.results[0]["out"].reshape(IMAGES, POSITIONS, P)
```

```python
from contextlib import ExitStack

import numpy as np

import concourse.bass as bass
from concourse import mybir

F32 = mybir.dt.float32
BF16 = mybir.dt.bfloat16
I32 = mybir.dt.int32
U32 = mybir.dt.uint32
ALU = mybir.AluOpType
ACT = mybir.ActivationFunctionType
X = mybir.AxisListType.X

P = 128
IMAGES, POSITIONS = 64, 36
CHUNKS = 6
HEADS, HD = 8, 16
TOKENS = IMAGES * POSITIONS
TILES = TOKENS // P
REL = 2 * IMAGES - 1
IMG_G = 3
G = IMG_G * POSITIONS
GROUPS = -(-IMAGES // IMG_G)
EXPERTS, FF = 8, 512
FC = FF // P
SLOT_TILES = TOKENS // P + EXPERTS - 1
SLOTS = SLOT_TILES * P
AT_H, AT_WEIGHT, AT_TOKEN = P, 2 * P, 2 * P + 1
ROW = 2 * P + 2
EPS = 1e-5
SCALE = float(HD) ** -0.5
FAR = -float(2 ** 100)

_WEIGHTS = [("tok", CHUNKS * P), ("in_proj", 3 * P), ("out_proj", P), ("pos_w", P), ("pos", REL),
            ("ident", P), ("head_mask", HEADS), ("half_mask", HEADS)]
_WEIGHTS1 = [("tW", 2 * P), ("cW", 2 * P), ("ff", 2 * P), ("fr", 2 * P), ("Wq", P), ("Wk", P), ("Wv", P),
             ("Wo", P), ("gate", EXPERTS), ("same", G), ("before", G), ("ones", G), ("member", G),
             ("apart", 4 * G), ("valid", GROUPS), ("rank_w", EXPERTS), ("tile_lo", TILES), ("tile_no", SLOT_TILES),
             ("lower", EXPERTS * EXPERTS), ("token", GROUPS)]
_COLUMNS = ["bq0", "bk0", "bv0", "u", "v", "tb0", "tb1", "cb0", "cb1", "a1", "a2", "a3", "frb", "ffb", "g", "b",
            "bq1", "bk1", "bv1", "ab"]
_ROWS = [("tok_b", P), ("out_b", P), ("bo", P), ("gate_b", EXPERTS)]


def places(items):
    at, out = 0, {}
    for name, width in items:
        out[name] = (at, width)
        at += width
    return out, at


AT_W, WIDTH_W = places(_WEIGHTS)
AT_W1, WIDTH_W1 = places(_WEIGHTS1)
AT_R, WIDTH_R = places(_ROWS)


class Tile:

    def __init__(self, u, c, lag, tiles):
        self.n = 2 * u + (c - lag)
        self.par = (c - lag) % 2
        self.half = u + (c - lag) // 2
        self.live = not isinstance(u, int) or 0 <= self.n < tiles


def after(eng, sem, count):
    if not isinstance(count, int) or count > 0:
        eng.wait_ge(sem, count)


def pipeline(eng, stages, tiles, loop_from, loop_to):
    last = tiles + max(lag for _, lag in stages)

    def step(u, c):
        for stage, lag in stages:
            t = Tile(u, c, lag, tiles)
            if t.live:
                stage(t)

    for i in range(2 * loop_from):
        step(i // 2, i % 2)
    with eng.Fori(loop_from, loop_to) as u:
        step(u, 0)
        step(u, 1)
    for i in range(2 * loop_to, last):
        step(i // 2, i % 2)


def over(ap, axis, count, shape):
    return ap.unsqueeze(axis).broadcast_to(shape)


def tower(nc, patches, weights, weights1, columns, rows, b1_rows, b2_rows, W1, W2, zeros, empty, out,
          bd_dram, hs_dram, sorted_dram):
    with ExitStack() as ctx:
        def sb(name, shape, dt=F32):
            return ctx.enter_context(nc.sbuf_tensor(name, shape, dt))

        def sem(name):
            return ctx.enter_context(nc.semaphore(name))

        def bank_pair(name):
            return ctx.enter_context(nc.psum_tensor(name, [P, 2, 512], F32))

        banks = [ctx.enter_context(nc.psum_tensor(f"bank{i}", [P, 512], F32)) for i in range(4)]
        banks += [bank_pair("bank45"), bank_pair("bank67")]

        w = sb("w", [P, WIDTH_W])
        w1 = sb("w1", [P, WIDTH_W1])
        cols = sb("cols", [P, len(_COLUMNS)])
        bias_rows = sb("bias_rows", [P, WIDTH_R])

        def W(name, a=0, b=None):
            at, width = AT_W[name]
            return w[:, at + a:at + (width if b is None else b)]

        def V(name, a=0, b=None, rows_=P):
            at, width = AT_W1[name]
            return w1[0:rows_, at + a:at + (width if b is None else b)]

        def col(name, rows_=P):
            c = _COLUMNS.index(name)
            return cols[0:rows_, c:c + 1]

        def row(name, rows_=P):
            at, width = AT_R[name]
            return bias_rows[0:rows_, at:at + width]

        weights_in = sem("weights_in")
        weights1_in = sem("weights1_in")
        stored = [sem("stored_even"), sem("stored_odd")]

        pads_zero = sem("pads_zero")
        kept = [sem("kept_even"), sem("kept_odd")]
        sent = sb("sent", [G, GROUPS, ROW])
        n_all = sent[:, :, 0:P]
        h_all = sent[:, :, AT_H:AT_H + P]
        xb_all = sb("xb_all", [G, GROUPS, P])
        lg_all = sb("lg_all", [G, GROUPS, EXPERTS])
        slots_empty = sem("slots_empty")
        experts_in = sem("experts_in")
        W1_sb = sb("W1_sb", [P, EXPERTS * FF])
        W2_sb = sb("W2_sb", [P, EXPERTS * FF])
        b1_sb = sb("b1_sb", [P, EXPERTS * FF])
        b2_sb = sb("b2_sb", [P, EXPERTS * P])
        loads = ((W1_sb, W1), (W2_sb, W2), (b1_sb, b1_rows), (b2_sb, b2_rows))
        own = []

        def part_sem(name):
            own.append(nc.alloc_semaphore(name=name))
            return own[-1]

        with ExitStack() as ctx0:
            block0(nc, ctx0, part_sem, banks, W, col, row, w, w1, cols, bias_rows, patches, weights, weights1,
                   columns, rows, weights_in, weights1_in, stored, bd_dram, hs_dram, zeros, pads_zero)
        nc.clear_and_free_semaphores(own)
        nc.all_engine_barrier()
        own.clear()
        with ExitStack() as ctx1:
            block1(nc, ctx1, part_sem, banks, V, col, row, W("ident"), W("head_mask"), sent, h_all, xb_all, n_all, lg_all, hs_dram,
                   stored, pads_zero, weights1_in, kept, loads, experts_in, sorted_dram, slots_empty, empty)
        nc.clear_and_free_semaphores(own)
        nc.all_engine_barrier()
        own.clear()
        with ExitStack() as ctx2:
            block2(nc, ctx2, part_sem, banks, V, col, W("ident"), sent, lg_all, W1_sb, W2_sb, b1_sb, b2_sb, experts_in,
                   sorted_dram, out, slots_empty, kept)


def block0(nc, ctx, sem, banks, W, col, row, w, w1, cols, bias_rows, patches, weights, weights1,
           columns, rows, weights_in, weights1_in, stored, bd_dram, hs_dram, zeros, pads_zero):
    def sb(name, shape, dt=F32):
        return ctx.enter_context(nc.sbuf_tensor(name, shape, dt))

    def pair(name, shape, dt=F32):
        return [sb(f"{name}{i}", shape, dt) for i in range(2)]

    TOK, XT, Q, KV, BD, ACPT = banks
    AC, PT = ACPT[:, 0, :], ACPT[:, 1, :]

    patch = pair("patch", [P, CHUNKS * P])
    h0 = sb("h0", [P, TILES, P])
    stats = pair("stats", [P, 6])
    mv = pair("mv", [P, 2])
    ve = pair("ve", [P, 1])
    rstd = pair("rstd", [P, 1])
    xn = pair("xn", [P, P])
    xT = pair("xT", [P, 2, 2, IMAGES])
    qu = pair("qu", [P, P])
    qv = pair("qv", [P, P])
    kb = pair("kb", [P, HEADS, P])
    vv = pair("vv", [P, 2, HEADS, HD + 1])
    pos_p = sb("pos_p", [P, REL])
    pb = sb("pb", [P, HEADS, REL])
    bias_u = sb("bias_u", [P, 1])
    bias_v = sb("bias_v", [P, 1])
    bd = pair("bd", [P, HEADS * REL])
    bs = pair("bs", [P, HEADS * IMAGES])
    s1 = pair("s1", [P, HEADS, IMAGES])
    mx = pair("mx", [P, HEADS])
    s2 = pair("s2", [P, HEADS, IMAGES])
    ex = pair("ex", [P, HEADS * IMAGES])
    pT = pair("pT", [P, 4 * P])
    rs = pair("rs", [P, HEADS])
    on = pair("on", [P, HEADS, HD])
    oT = pair("oT", [P, P])
    st2 = pair("st2", [P, 6])
    mv2 = pair("mv2", [P, 2])
    ve2 = pair("ve2", [P, 1])
    rstd2 = pair("rstd2", [P, 1])
    nrm = pair("nrm", [P, P])
    att = pair("att", [P, P])
    h2 = pair("h2", [P, P])
    half_pow = sb("half_pow", [P, 1])

    patch_in = [sem("patch_in_even"), sem("patch_in_odd")]
    half_pow_set = sem("half_pow_set")
    ones_set = sem("ones_set")
    biases_made = sem("biases_made")
    pos_projected = sem("pos_projected")
    pos_ready = sem("pos_ready")
    tok_done = sem("tok_done")
    h_ready = sem("h_ready")
    stats_done = sem("stats_done")
    mv_done = sem("mv_done")
    ve_done = sem("ve_done")
    rstd_done = sem("rstd_done")
    xn_done = sem("xn_done")
    xT_done = sem("xT_done")
    xT_copied = sem("xT_copied")
    q_done = sem("q_done")
    qv_copied = sem("qv_copied")
    qu_copied = sem("qu_copied")
    kv_done = sem("kv_done")
    kb_made = sem("kb_made")
    vv_made = sem("vv_made")
    bd_done = sem("bd_done")
    bd_copied = sem("bd_copied")
    bd_out = [sem("bd_out_even"), sem("bd_out_odd")]
    bd_back = [sem("bd_back_even"), sem("bd_back_odd")]
    ac_done = sem("ac_done")
    scores_added = sem("scores_added")
    max_found = sem("max_found")
    scores_less_max = sem("scores_less_max")
    exp_done = sem("exp_done")
    pT_done = sem("pT_done")
    pT_copied = sem("pT_copied")
    pv_done = sem("pv_done")
    sums_inverted = sem("sums_inverted")
    attn_normal = sem("attn_normal")
    oT_done = sem("oT_done")
    oT_copied = sem("oT_copied")
    proj_done = sem("proj_done")
    att_biased = sem("att_biased")
    h1_ready = sem("h1_ready")
    stats2_done = sem("stats2_done")
    mv2_done = sem("mv2_done")
    ve2_done = sem("ve2_done")
    rstd2_done = sem("rstd2_done")
    nrm_done = sem("nrm_done")
    h2_ready = sem("h2_ready")

    hs_rows = hs_dram[0:TOKENS, :].rearrange("(l s) e -> s l e", s=POSITIONS)
    block = ctx.enter_context(nc.Block())
    LOOP = (2, TILES // 2)

    @block.sync
    def _(sp):
        sp.dma_start(w[:, :], weights).then_inc(weights_in, 16)
        sp.dma_start(cols[:, :], columns).then_inc(weights_in, 16)
        sp.dma_start(bias_rows[:, :], rows).then_inc(weights_in, 16)

        def shift_back(t):
            sp.wait_ge(bd_copied, t.n + 1)
            sp.dma_start(bd_dram[t.par], bd[t.par][:, :]).then_inc(bd_out[t.par], 16)
            sp.wait_ge(bd_out[t.par], 16 * (t.half + 1))
            for s in range(2):
                src = bass.AP(tensor=bd_dram.tensor,
                              offset=(t.par * P + s * IMAGES) * HEADS * REL + IMAGES - 1,
                              ap=[[HEADS * REL - 1, IMAGES], [REL, HEADS], [1, IMAGES]])
                sp.dma_start(bs[t.par][s * IMAGES:(s + 1) * IMAGES, :].rearrange("p (h j) -> p h j", h=HEADS),
                             src).then_inc(bd_back[t.par], 16)

        def store(t):
            sp.wait_ge(h2_ready, t.n + 1)
            for s in range(2):
                sp.dma_start(hs_rows[2 * t.n + s], h2[t.par][s * IMAGES:(s + 1) * IMAGES, :])\
                  .then_inc(stored[t.par], 16)

        pipeline(sp, [(shift_back, 0), (store, 2)], TILES, *LOOP)
        sp.dma_start(w1[:, :], weights1).then_inc(weights1_in, 16)
        sp.dma_start(hs_dram[TOKENS:GROUPS * G, :], zeros[0:GROUPS * G - TOKENS, :]).then_inc(pads_zero, 16)
        sp.wait_ge(pads_zero, 16)
        for s in stored:
            sp.wait_ge(s, 16 * TILES)

    @block.tensor
    def _(pe):
        pe.wait_ge(weights_in, 48)
        nc.tensor.matmul(XT[:, 0:REL], W("pos_w"), W("pos"), start=True, stop=True).then_inc(pos_projected, 1)

        def embed(t):
            pe.wait_ge(patch_in[t.par], 16 * (t.half + 1))
            after(pe, h_ready, t.n)
            after(pe, att_biased, t.n - 2)
            for c in range(CHUNKS):
                mm = nc.tensor.matmul(TOK[:, 0:P], patch[t.par][:, c * P:(c + 1) * P], W("tok", c * P, (c + 1) * P),
                                      start=(c == 0), stop=(c == CHUNKS - 1))
            mm.then_inc(tok_done, 1)

        def content(s):
            def stage(t):
                if s == 0:
                    pe.wait_ge(qu_copied, t.n + 1)
                    pe.wait_ge(kb_made, t.n + 1)
                    after(pe, scores_added, t.n)
                mm = nc.tensor.matmul(AC[s * IMAGES:(s + 1) * IMAGES, :], qu[t.par][:, s * IMAGES:(s + 1) * IMAGES],
                                      kb[t.par][:, :, s * IMAGES:(s + 1) * IMAGES], start=True, stop=True)
                if s == 1:
                    mm.then_inc(ac_done, 1)
            return stage

        def turn_probs(t):
            pe.wait_ge(exp_done, t.n + 1)
            after(pe, attn_normal, t.n)
            for g in range(4):
                mm = nc.tensor.transpose(PT[:, g * P:(g + 1) * P], ex[t.par][:, g * P:(g + 1) * P], W("ident"))
            mm.then_inc(pT_done, 1)

        def turn_x(t):
            pe.wait_ge(xn_done, t.n + 1)
            after(pe, oT_copied, t.n - 2)
            nc.tensor.transpose(XT[:, 0:P], xn[t.par][:, :], W("ident")).then_inc(xT_done, 1)

        def attend(t):
            pe.wait_ge(pT_copied, t.n + 1)
            pe.wait_ge(vv_made, t.n + 1)
            for s in range(2):
                for g in range(4):
                    mm = nc.tensor.matmul(
                        PT[s * IMAGES:(s + 1) * IMAGES, g * 34:(g + 1) * 34],
                        pT[t.par][:, g * P + s * IMAGES:g * P + (s + 1) * IMAGES],
                        vv[t.par][:, s, 2 * g:2 * g + 2, :].rearrange("p h d -> p (h d)"), start=True, stop=True)
            mm.then_inc(pv_done, 1)

        def project(t):
            pe.wait_ge(xT_copied, t.n + 1)
            after(pe, qu_copied, t.n)
            after(pe, qv_copied, t.n)
            nc.tensor.matmul(Q[:, 0:P], W("in_proj", 0, P), xT[t.par][:, :, 0, :], start=True, stop=True).then_inc(q_done, 1)
            after(pe, kb_made, t.n)
            after(pe, vv_made, t.n)
            nc.tensor.matmul(KV[:, 0:P], W("in_proj", P, 2 * P), xT[t.par][:, :, 0, :], start=True, stop=True)
            for s in range(2):
                twice = xT[t.par][:, s, :, :].rearrange("p r l -> p (r l)")
                mm = nc.tensor.matmul(KV[:, (s + 1) * P:(s + 2) * P], twice, W("in_proj", 2 * P, 3 * P),
                                      start=True, stop=True)
            mm.then_inc(kv_done, 1)

        def turn_o(t):
            pe.wait_ge(attn_normal, t.n + 1)
            after(pe, xT_copied, t.n + 3 if not isinstance(t.n, int) else min(t.n + 3, TILES))
            nc.tensor.transpose(XT[:, 0:P], on[t.par][:, :, :].rearrange("p h d -> p (h d)"), W("ident"))\
              .then_inc(oT_done, 1)

        def positions(b):
            def stage(t):
                if b == 0:
                    pe.wait_ge(qv_copied, t.n + 1)
                    if isinstance(t.n, int) and t.n == 0:
                        pe.wait_ge(pos_ready, 1)
                    after(pe, bd_copied, t.n)
                mm = nc.tensor.matmul(BD[:, b, 0:4 * REL], qv[t.par][:, :],
                                      pb[:, 4 * b:4 * b + 4, :].rearrange("p h n -> p (h n)"), start=True, stop=True)
                if b == 1:
                    mm.then_inc(bd_done, 1)
            return stage

        def project_out(t):
            pe.wait_ge(oT_copied, t.n + 1)
            after(pe, h_ready, t.n + 3 if not isinstance(t.n, int) else min(t.n + 3, TILES))
            nc.tensor.matmul(TOK[:, 0:P], oT[t.par][:, :], W("out_proj"), start=True, stop=True).then_inc(proj_done, 1)

        pipeline(pe, [(embed, 0), (content(0), 1), (turn_probs, 2), (content(1), 1), (turn_x, 0), (attend, 2),
                      (project, 0), (turn_o, 2), (positions(0), 0), (project_out, 2), (positions(1), 0)],
                 TILES, *LOOP)

    @block.scalar
    def _(act):
        act.wait_ge(pos_projected, 1)
        nc.scalar.activation(pos_p[:, :], XT[:, 0:REL], ACT.Identity).then_inc(pos_projected, 1)

        def keep_positions(t):
            act.wait_ge(bd_done, t.n + 1)
            after(act, bd_out[t.par], 16 * t.half)
            nc.scalar.activation(bd[t.par][:, :].rearrange("p (b n) -> p b n", b=2), BD[:, :, 0:4 * REL],
                                 ACT.Identity).then_inc(bd_copied, 1)

        def exponentials(t):
            act.wait_ge(scores_less_max, t.n + 1)
            after(act, pT_done, t.n - 1)
            nc.scalar.activation(ex[t.par][:, :], s2[t.par][:, :, :].rearrange("p h j -> p (h j)"), ACT.Exp,
                                 scale=SCALE).then_inc(exp_done, 1)

        def copy_probs(t):
            act.wait_ge(pT_done, t.n + 1)
            after(act, pv_done, t.n - 1)
            nc.scalar.activation(pT[t.par][:, :], PT[:, :], ACT.Identity).then_inc(pT_copied, 1)

        def copy_x(t):
            act.wait_ge(xT_done, t.n + 1)
            after(act, kv_done, t.n - 1)
            nc.scalar.activation(xT[t.par][:, :, :, :],
                                 over(XT[:, 0:P].rearrange("p (s l) -> p s l", s=2), 2, 2, [P, 2, 2, IMAGES]),
                                 ACT.Identity).then_inc(xT_copied, 1)

        def queries(t):
            act.wait_ge(q_done, t.n + 1)
            if isinstance(t.n, int) and t.n == 0:
                act.wait_ge(biases_made, 2)
            after(act, bd_done, t.n - 1)
            nc.scalar.activation(qv[t.par][:, :], Q[:, 0:P], ACT.Identity, bias=bias_v[:, 0:1]).then_inc(qv_copied, 1)
            after(act, ac_done, t.n - 1)
            nc.scalar.activation(qu[t.par][:, :], Q[:, 0:P], ACT.Identity, bias=bias_u[:, 0:1]).then_inc(qu_copied, 1)

        def copy_o(t):
            act.wait_ge(oT_done, t.n + 1)
            after(act, proj_done, t.n - 1)
            nc.scalar.activation(oT[t.par][:, :], XT[:, 0:P], ACT.Identity, bias=col("bv0")).then_inc(oT_copied, 1)

        pipeline(act, [(keep_positions, 1), (exponentials, 2), (copy_probs, 2), (copy_x, 0), (queries, 0),
                       (copy_o, 2)], TILES, *LOOP)

    @block.gpsimd
    def _(pool):
        nc.gpsimd.memset(half_pow[:, :], -0.5).then_inc(half_pow_set, 1)
        for p in range(2):
            nc.gpsimd.memset(vv[p][:, :, :, :], 0.0).then_inc(ones_set, 1)
        pool.wait_ge(half_pow_set, 1)

        def load_patches(t):
            after(pool, tok_done, t.n - 1)
            pool.dma_start(patch[t.par][:, :], patches[t.n]).then_inc(patch_in[t.par], 16)

        def root(t):
            pool.wait_ge(ve_done, t.n + 1)
            after(pool, xn_done, t.n - 1)
            nc.gpsimd.tensor_tensor(rstd[t.par][:, :], ve[t.par][:, :], half_pow[:, :], ALU.pow).then_inc(rstd_done, 1)

        def root2(t):
            pool.wait_ge(ve2_done, t.n + 1)
            after(pool, nrm_done, t.n - 1)
            nc.gpsimd.tensor_tensor(rstd2[t.par][:, :], ve2[t.par][:, :], half_pow[:, :], ALU.pow)\
              .then_inc(rstd2_done, 1)

        pipeline(pool, [(load_patches, 0), (root, 1), (root2, 3)], TILES, *LOOP)

    @block.vector
    def _(dve):
        dve.wait_ge(weights_in, 48)
        dve.wait_ge(ones_set, 2)
        for p in range(2):
            for s in range(2):
                nc.vector.tensor_copy(vv[p][:, s, :, HD:HD + 1].rearrange("p h o -> p (h o)"), W("half_mask"))\
                  .then_inc(ones_set, 1)
        nc.vector.tensor_tensor(bias_u[:, :], col("bq0"), col("u"), ALU.add).then_inc(biases_made, 1)
        nc.vector.tensor_tensor(bias_v[:, :], col("bq0"), col("v"), ALU.add).then_inc(biases_made, 1)
        dve.wait_ge(pos_projected, 2)
        nc.vector.tensor_tensor(pb[:, :, :], over(pos_p[:, :], 1, HEADS, [P, HEADS, REL]),
                                over(W("head_mask"), 2, REL, [P, HEADS, REL]), ALU.mult).then_inc(pos_ready, 1)

        def embedded(t):
            after(dve, xn_done, t.n - 1)
            dve.wait_ge(tok_done, t.n + 1)
            nc.vector.tensor_tensor(h0[:, t.n, :], TOK[:, 0:P], row("tok_b"), ALU.add).then_inc(h_ready, 1)
            dve.drain()
            nc.vector.bn_stats(stats[t.par][:, :], h0[:, t.n, :])
            dve.drain()
            nc.vector.bn_aggr(mv[t.par][:, :], stats[t.par][:, :]).then_inc(mv_done, 1)
            dve.wait_ge(mv_done, t.n + 1)
            after(dve, rstd_done, t.n - 1)
            nc.vector.tensor_scalar(ve[t.par][:, :], mv[t.par][:, 1:2], EPS, None, ALU.add).then_inc(ve_done, 1)

        def normalise(t):
            dve.wait_ge(rstd_done, t.n + 1)
            after(dve, xT_done, t.n - 1)
            nc.vector.tensor_scalar(xn[t.par][:, :], h0[:, t.n, :], mv[t.par][:, 0:1], rstd[t.par][:, 0:1],
                                    ALU.subtract, ALU.mult).then_inc(xn_done, 1)

        def second_residual(t):
            dve.wait_ge(rstd2_done, t.n + 1)
            after(dve, h2_ready, t.n - 1)
            nc.vector.tensor_scalar(nrm[t.par][:, :], h0[:, t.n, :], mv2[t.par][:, 0:1], rstd2[t.par][:, 0:1],
                                    ALU.subtract, ALU.mult).then_inc(nrm_done, 1)
            dve.wait_ge(nrm_done, t.n + 1)
            after(dve, stored[t.par], 32 * t.half)
            nc.vector.tensor_tensor(h2[t.par][:, :], h0[:, t.n, :], nrm[t.par][:, :], ALU.add).then_inc(h2_ready, 1)

        def divide(t):
            o = PT[:, 0:HEADS * (HD + 1)].rearrange("p (h d) -> p h d", h=HEADS)
            dve.wait_ge(pv_done, t.n + 1)
            nc.vector.reciprocal(rs[t.par][:, :], o[:, :, HD]).then_inc(sums_inverted, 1)
            dve.wait_ge(sums_inverted, t.n + 1)
            after(dve, oT_done, t.n - 1)
            nc.vector.tensor_tensor(on[t.par][:, :, :], o[:, :, 0:HD], over(rs[t.par][:, :], 2, HD, [P, HEADS, HD]),
                                    ALU.mult).then_inc(attn_normal, 1)

        def keys_values(t):
            dve.wait_ge(kv_done, t.n + 1)
            after(dve, ac_done, t.n - 1)
            nc.vector.scalar_tensor_tensor(out=kb[t.par][:, :, :], in0=over(KV[:, 0:P], 1, HEADS, [P, HEADS, P]),
                                           scalar=col("bk0"), in1=over(W("head_mask"), 2, P, [P, HEADS, P]),
                                           op0=ALU.add, op1=ALU.mult).then_inc(kb_made, 1)
            after(dve, pv_done, t.n - 1)
            shape = [P, 2, HEADS, HD]
            v = KV[:, P:3 * P].rearrange("p (s h d) -> p s h d", s=2, h=HEADS)
            mask = W("half_mask").unsqueeze(1).unsqueeze(3).broadcast_to(shape)
            nc.vector.tensor_tensor(vv[t.par][:, :, :, 0:HD], v, mask, ALU.mult).then_inc(vv_made, 1)

        def scores(t):
            dve.wait_ge(bd_back[t.par], 32 * (t.half + 1))
            dve.wait_ge(ac_done, t.n + 1)
            after(dve, scores_less_max, t.n - 1)
            nc.vector.tensor_tensor(s1[t.par][:, :, :].rearrange("p h j -> p (h j)"), AC[:, :], bs[t.par][:, :],
                                    ALU.add).then_inc(scores_added, 1)
            dve.wait_ge(scores_added, t.n + 1)
            nc.vector.tensor_reduce(mx[t.par][:, :], s1[t.par][:, :, :], X, ALU.max).then_inc(max_found, 1)
            dve.wait_ge(max_found, t.n + 1)
            after(dve, exp_done, t.n - 1)
            nc.vector.tensor_tensor(s2[t.par][:, :, :], s1[t.par][:, :, :],
                                    over(mx[t.par][:, :], 2, IMAGES, [P, HEADS, IMAGES]), ALU.subtract)\
              .then_inc(scores_less_max, 1)

        def first_residual(t):
            dve.wait_ge(proj_done, t.n + 1)
            nc.vector.tensor_tensor(att[t.par][:, :], TOK[:, 0:P], row("out_b"), ALU.add).then_inc(att_biased, 1)
            dve.wait_ge(att_biased, t.n + 1)
            after(dve, nrm_done, t.n - 1)
            nc.vector.tensor_tensor(h0[:, t.n, :], h0[:, t.n, :], att[t.par][:, :], ALU.add)
            dve.drain()
            nc.vector.bn_stats(st2[t.par][:, :], h0[:, t.n, :])
            dve.drain()
            nc.vector.bn_aggr(mv2[t.par][:, :], st2[t.par][:, :]).then_inc(mv2_done, 1)
            dve.wait_ge(mv2_done, t.n + 1)
            after(dve, rstd2_done, t.n - 1)
            nc.vector.tensor_scalar(ve2[t.par][:, :], mv2[t.par][:, 1:2], EPS, None, ALU.add).then_inc(ve2_done, 1)

        pipeline(dve, [(embedded, 0), (second_residual, 3), (normalise, 0), (divide, 2), (keys_values, 0),
                       (first_residual, 2), (scores, 1)], TILES, *LOOP)


def block1(nc, ctx, sem, banks, V, col, row, Wident, w_head_mask, sent, h_all, xb_all, n_all, lg_all, hs_dram, stored,
           pads_zero, weights1_in, kept, loads, experts_in, sorted_dram, slots_empty, empty):
    def sb(name, shape, dt=F32):
        return ctx.enter_context(nc.sbuf_tensor(name, shape, dt))

    def pair(name, shape, dt=F32):
        return [sb(f"{name}{i}", shape, dt) for i in range(2)]

    U0, U1, MM, WD, S, T = banks
    HALF = HEADS // 2

    member = sb("member", [IMG_G, G], BF16)
    apart = sb("apart", [IMG_G, HALF * G], BF16)
    half_col = sb("half_col", [P, 1])
    pow_col = sb("pow_col", [P, 1])
    half_bias = sb("half_bias", [P, 4])
    bq_scaled = sb("bq_scaled", [P, 1])
    stats0, mv0, ve0, rstd0 = pair("stats0", [G, 6]), pair("mv0", [G, 2]), pair("ve0", [G, 1]), pair("rstd0", [G, 1])
    stats4, mv4, ve4, rstd4 = pair("stats4", [G, 6]), pair("mv4", [G, 2]), pair("ve4", [G, 1]), pair("rstd4", [G, 1])
    stats5, mv5, ve5, rstd5 = pair("stats5", [G, 6]), pair("mv5", [G, 2]), pair("ve5", [G, 1]), pair("rstd5", [G, 1])
    x0 = pair("x0", [G, P])
    x0T = pair("x0T", [P, G])
    relu1, gate1, x1T = pair("relu1", [P, G]), pair("gate1", [P, G]), pair("x1T", [P, G])
    relu2, gate2, x2T = pair("relu2", [P, G]), pair("gate2", [P, G]), pair("x2T", [P, G])
    mix1, mix2 = pair("mix1", [P, G]), pair("mix2", [P, G])
    mixb1, mixb2 = sb("mixb1", [P, G]), sb("mixb2", [P, G])
    aT = pair("aT", [P, G])
    x2 = pair("x2", [G, P])
    gm, gneg = pair("gm", [G, G]), pair("gneg", [G, 1])
    ge, gp = pair("ge", [G, G]), pair("gp", [G, G])
    gx, gsum, grec = sb("gx", [G, G]), sb("gsum", [G, 1]), sb("grec", [G, 1])
    gpT = pair("gpT", [G, G])
    attT = pair("attT", [P, G])
    tr, tz, zs, yT = pair("tr", [P, G]), pair("tz", [P, G]), pair("zs", [P, G]), pair("yT", [P, G])
    rx = sb("rx", [P, G])
    x4 = pair("x4", [G, P])
    x4T = pair("x4T", [P, G])
    qT = pair("qT", [P, G])
    kS = pair("kS", [P, G])
    kb = pair("kb_", [P, HEADS, G])
    xb = pair("xb", [G, P])
    v17 = pair("v17", [G, HEADS, HD + 1])
    less = pair("less_", [G, HEADS])
    ex = pair("ex_", [G, HEADS, G])
    pT = pair("pT_", [G, HEADS, G])
    rs = pair("rs_", [G, HEADS])
    on = pair("on_", [G, HEADS, HD])
    oT = pair("oT_", [P, G])
    y5 = pair("y5", [G, P])
    nb = pair("nb", [G, P])
    tT = pair("tT", [P, G])

    names = ("consts halves x0_done x0T_done x0T_copied hw1_done gate1_done mix1_done mixb1_done x1_done hw2_done "
             "gate2_done mix2_done mixb2_done x2_done aT_done x2t_done x2_copied gram_done gm_done "
             "gneg_done ge_done gx_done grec_done gp_done gpT_done gpT_copied att_done att_copied rz_done "
             "tr_done tz_done rz_copied rx_done yT_done y_done h3_done mv0_done ve0_done rstd0_done mv4_done ve4_done "
             "rstd4_done mv5_done ve5_done rstd5_done x4_done xb_done x4T_done x4T_copied q_done_ q_copied k_done k_copied "
             "kb_done v_done v_copied s_done less_done ex_done pT_done_ pT_copied_ pv_done_ rs_done on_done "
             "oT_done_ oT_copied_ wo_done y5_done nb_done nT_done tT_copied logits_done logits_kept").split()
    s = {n: sem(n) for n in names}
    loaded = sem("loaded")
    xb_kept = [sem("xb_kept_even"), sem("xb_kept_odd")]
    LOOP = (5, GROUPS // 2)
    USERS = {
        "U0": [("n", 7, "tT_copied"), ("q", 3, "q_copied"), ("gp", 1, "gpT_copied")],
        "U1": [("gather", 2, "att_copied"), ("gates", 2, "rz_copied"), ("y", 2, "h3_done"), ("x0", 0, "x0T_copied"),
               ("x2", 1, "x2_copied"), ("v", 4, "v_copied")],
        "MM": [("highway2", 1, "gate2_done"), ("pv", 5, "on_done"), ("o", 5, "oT_copied_"),
               ("highway1", 0, "gate1_done"), ("out", 5, "y5_done")],
        "WD": [("k", 3, "k_copied"), ("logits", 7, "logits_kept"), ("gram", 1, "gm_done"), ("x4", 2, "x4T_copied")],
        "S": [("s", 3, "ex_done")],
        "T": [("probs", 4, "pT_copied_")],
    }
    AT = {user: bank for name, bank in (("U0", U0), ("U1", U1), ("MM", MM), ("WD", WD)) for user, _, _ in USERS[name]}

    def done(eng, name, t):
        eng.wait_ge(s[name], t.n + 1)

    def reused(eng, name, t):
        after(eng, s[name], t.n - 1)

    def bank_read(eng, user, t):
        users = next(us for us in USERS.values() if user in [name for name, _, _ in us])
        at = [name for name, _, _ in users].index(user)
        step = t.n + users[at][1]
        for back in range(1, len(users) + 1):
            _, lag, read = users[(at - back) % len(users)]
            n = step - (back > at) - lag
            if not isinstance(n, int):
                return eng.wait_ge(s[read], n + 1)
            if 0 <= n < GROUPS:
                return eng.wait_ge(s[read], n + 1)

    block = ctx.enter_context(nc.Block())

    @block.sync
    def _(sp):
        sp.wait_ge(pads_zero, 16)
        for q in stored:
            sp.wait_ge(q, 16 * TILES)
        rows = hs_dram.rearrange("(g p) e -> p g e", p=G)
        sp.dma_start(h_all[:, 0:2, :], rows[:, 0:2, :]).then_inc(loaded, 16)
        sp.wait_ge(loaded, 16)
        sp.dma_start(h_all[:, 2:GROUPS, :], rows[:, 2:GROUPS, :]).then_inc(loaded, 16)

        sp.dma_start(sorted_dram, empty).then_inc(slots_empty, 16)
        for there, here in loads:
            sp.dma_start(there[:, :], here).then_inc(experts_in, 16)

        def keep(t):
            done(sp, "nb_done", t)
            sp.dma_start(n_all[:, t.n, :], nb[t.par][:, :]).then_inc(kept[t.par], 16)

        def keep_xb(t):
            done(sp, "xb_done", t)
            sp.dma_start(xb_all[:, t.n, :], xb[t.par][:, :]).then_inc(xb_kept[t.par], 16)

        pipeline(sp, [
            (keep_xb, 3), (keep, 8)],
            GROUPS, *LOOP)
        for q in kept:
            sp.wait_ge(q, 16 * GROUPS // 2)

    @block.gpsimd
    def _(pool):
        nc.gpsimd.memset(half_col[:, :], 0.5).then_inc(s["consts"], 1)
        nc.gpsimd.memset(pow_col[:, :], -0.5).then_inc(s["consts"], 1)
        nc.gpsimd.memset(v17[0][:, :, :], 1.0).then_inc(s["consts"], 1)
        nc.gpsimd.memset(v17[1][:, :, :], 1.0).then_inc(s["consts"], 1)
        pool.wait_ge(s["consts"], 4)

        def root(k, ve, rstd, used):
            def stage(t):
                done(pool, f"ve{k}_done", t)
                reused(pool, used, t)
                nc.gpsimd.tensor_tensor(rstd[t.par][:, :], ve[t.par][:, :], pow_col[0:G, :], ALU.pow)\
                  .then_inc(s[f"rstd{k}_done"], 1)
            return stage

        def differ(k, relu, x, mix, used):
            def stage(t):
                done(pool, f"gate{k}_done", t)
                reused(pool, used, t)
                nc.gpsimd.tensor_tensor(mix[t.par][:, :], relu[t.par][:, :], x[t.par][:, :], ALU.subtract)\
                  .then_inc(s[f"mix{k}_done"], 1)
            return stage

        def keys(t):
            done(pool, "k_copied", t)
            reused(pool, "s_done", t)
            nc.gpsimd.tensor_tensor(kb[t.par][:, :, :], over(kS[t.par][:, :], 1, HEADS, [P, HEADS, G]),
                                    over(w_head_mask, 2, G, [P, HEADS, G]), ALU.mult).then_inc(s["kb_done"], 1)

        def add_bo(t):
            done(pool, "x4_done", t)
            after(pool, xb_kept[t.par], 16 * t.half)
            nc.gpsimd.tensor_tensor(xb[t.par][:, :], x4[t.par][:, :], row("bo", G), ALU.add).then_inc(s["xb_done"], 1)

        pipeline(pool, [
            (root(5, ve5, rstd5, "nb_done"), 7), (differ(2, relu2, x1T, mix2, "x2_done"), 2), (keys, 4),
            (root(4, ve4, rstd4, "x4_done"), 3), (differ(1, relu1, x0T, mix1, "x1_done"), 1), (add_bo, 3),
            (root(0, ve0, rstd0, "x0_done"), 0)],
            GROUPS, *LOOP)
    @block.tensor
    def _(pe):
        pe.wait_ge(weights1_in, 16)
        pe.wait_ge(s["consts"], 6)

        def highway(k, xin, x_name):
            def stage(t):
                done(pe, x_name, t)
                bank_read(pe, f"highway{k + 1}", t)
                at = AT[f"highway{k + 1}"]
                nc.tensor.matmul(at[:, 0:G], V("tW", k * P, (k + 1) * P), xin[t.par][:, :], start=True, stop=True)
                nc.tensor.matmul(at[:, G:2 * G], V("cW", k * P, (k + 1) * P), xin[t.par][:, :], start=True, stop=True)\
                  .then_inc(s[f"hw{k + 1}_done"], 1)
            return stage

        def gather(t):
            done(pe, "gpT_copied", t)
            done(pe, "x2_copied", t)
            bank_read(pe, "gather", t)
            nc.tensor.matmul(AT["gather"][:, 0:G], x2[t.par][:, :], gpT[t.par][:, :], start=True, stop=True)\
              .then_inc(s["att_done"], 1)

        def turn_probs(t):
            done(pe, "ex_done", t)
            bank_read(pe, "probs", t)
            for h in range(HEADS):
                mm = nc.tensor.transpose(T[0:G, h // HALF, (h % HALF) * G:(h % HALF + 1) * G],
                                         ex[t.par][:, h, :], Wident[0:G, 0:G])
            mm.then_inc(s["pT_done_"], 1)

        def gates(t):
            done(pe, "att_copied", t)
            bank_read(pe, "gates", t)
            for j, name in enumerate(("fr", "ff")):
                out = AT["gates"][:, j * G:(j + 1) * G]
                nc.tensor.matmul(out, V(name, 0, P), x0T[t.par][:, :], start=True, stop=False)
                mm = nc.tensor.matmul(out, V(name, P, 2 * P), attT[t.par][:, :], start=False, stop=True)
            mm.then_inc(s["rz_done"], 1)

        def turn(user, src, ready, now, rows_=G):
            def stage(t):
                done(pe, ready, t)
                bank_read(pe, user, t)
                nc.tensor.transpose(AT[user][0:P + G - rows_, 0:rows_], src[t.par][:, :],
                                    Wident[0:rows_, 0:rows_]).then_inc(s[now], 1)
            return stage

        def turn_gp(t):
            done(pe, "gp_done", t)
            bank_read(pe, "gp", t)
            nc.tensor.transpose(AT["gp"][0:G, 0:G], gp[t.par][:, :], Wident[0:G, 0:G]).then_inc(s["gpT_done"], 1)

        def turn_o(t):
            done(pe, "on_done", t)
            bank_read(pe, "o", t)
            nc.tensor.transpose(AT["o"][:, 0:G], on[t.par][:, :, :].rearrange("p h d -> p (h d)"), Wident[0:G, 0:G])\
              .then_inc(s["oT_done_"], 1)

        def logits(t):
            done(pe, "tT_copied", t)
            bank_read(pe, "logits", t)
            nc.tensor.matmul(AT["logits"][0:G, 0:EXPERTS], tT[t.par][:, :], V("gate"), start=True, stop=True)\
              .then_inc(s["logits_done"], 1)

        def attend(t):
            done(pe, "pT_copied_", t)
            done(pe, "v_copied", t)
            bank_read(pe, "pv", t)
            for h in range(HEADS):
                mm = nc.tensor.matmul(T[0:G, 0, h * (HD + 1):(h + 1) * (HD + 1)], pT[t.par][:, h, :],
                                      v17[t.par][:, h, :], start=True, stop=True)
            mm.then_inc(s["pv_done_"], 1)

        def gram(t):
            done(pe, "aT_done", t)
            bank_read(pe, "gram", t)
            out = AT["gram"][0:G, 0:G]
            nc.tensor.matmul(out, member[:, :], apart[:, 0:G], start=True, stop=False)
            nc.tensor.matmul(out, x2T[t.par][:, :], col("a1").broadcast_to([P, G]), start=False, stop=False)
            nc.tensor.matmul(out, aT[t.par][:, :], x2T[t.par][:, :], start=False, stop=True)\
              .then_inc(s["gram_done"], 1)

        def scores(b):
            def stage(t):
                if b == 0:
                    done(pe, "q_copied", t)
                    done(pe, "kb_done", t)
                    bank_read(pe, "s", t)
                nc.tensor.matmul(S[0:G, b, 0:HALF * G], member[:, :], apart[:, :], start=True, stop=False)
                mm = nc.tensor.matmul(S[0:G, b, 0:HALF * G], qT[t.par][:, :],
                                      kb[t.par][:, b * HALF:(b + 1) * HALF, :].rearrange("p h j -> p (h j)"),
                                      start=False, stop=True)
                if b == 1:
                    mm.then_inc(s["s_done"], 1)
            return stage

        def project(user, lhsT, weights, ready, now):
            def stage(t):
                done(pe, ready, t)
                bank_read(pe, user, t)
                nc.tensor.matmul(AT[user][0:G, 0:P], lhsT[t.par][:, :], V(weights), start=True, stop=True)\
                  .then_inc(s[now], 1)
            return stage

        def project_turned(user, weights, now):
            def stage(t):
                done(pe, "x4T_copied", t)
                bank_read(pe, user, t)
                nc.tensor.matmul(AT[user][:, 0:G], V(weights), x4T[t.par][:, :], start=True, stop=True)\
                  .then_inc(s[now], 1)
            return stage

        pipeline(pe, [
            (scores(1), 4), (gather, 2), (highway(1, x1T, "x1_done"), 1), (project_turned("k", "Wk", "k_done"), 3),
            (turn("n", nb, "nb_done", "nT_done"), 7), (gates, 2), (attend, 5), (logits, 7),
            (project_turned("q", "Wq", "q_done_"), 3), (turn("y", yT, "yT_done", "y_done", P), 2), (gram, 1),
            (turn_o, 5), (turn("x0", x0, "x0_done", "x0T_done"), 0), (turn_probs, 4),
            (highway(0, x0T, "x0T_copied"), 0), (turn("x2", x2T, "x2_done", "x2t_done", P), 1), (scores(0), 3),
            (project("out", oT, "Wo", "oT_copied_", "wo_done"), 5), (turn("x4", x4, "x4_done", "x4T_done"), 2),
            (project("v", x4T, "Wv", "x4T_copied", "v_done"), 4), (turn_gp, 1)],
            GROUPS, *LOOP)
    @block.scalar
    def _(act):
        act.wait_ge(s["halves"], 6)
        act.wait_ge(s["consts"], 6)

        def exponentials(t):
            done(act, "less_done", t)
            reused(act, "pT_done_", t)
            for h in range(HEADS):
                e = nc.scalar.activation(ex[t.par][:, h, :], S[0:G, h // HALF, (h % HALF) * G:(h % HALF + 1) * G],
                                         ACT.Exp, bias=less[t.par][:, h:h + 1])
            e.then_inc(s["ex_done"], 1)

        def highway(k, relu, gate, used):
            def stage(t):
                done(act, f"hw{k + 1}_done", t)
                reused(act, used, t)
                at = AT[f"highway{k + 1}"]
                nc.scalar.activation(relu[t.par][:, :], at[:, 0:G], ACT.Relu, bias=col(f"tb{k}"))
                nc.scalar.activation(gate[t.par][:, :], at[:, G:2 * G], ACT.Tanh, scale=0.5,
                                     bias=half_bias[:, k:k + 1]).then_inc(s[f"gate{k + 1}_done"], 1)
            return stage

        def copy(out, src, ready, used, now, **how):
            def stage(t):
                done(act, ready, t)
                reused(act, used, t)
                nc.scalar.activation(out[t.par][:, :], src, ACT.Identity, **how).then_inc(s[now], 1)
            return stage

        def copy_probs(t):
            done(act, "pT_done_", t)
            reused(act, "pv_done_", t)
            nc.scalar.activation(pT[t.par][:, :, :].rearrange("p (b h) j -> p b (h j)", b=2), T[0:G, :, 0:HALF * G],
                                 ACT.Identity).then_inc(s["pT_copied_"], 1)

        def gates(t):
            done(act, "rz_done", t)
            reused(act, "yT_done", t)
            nc.scalar.activation(tr[t.par][:, :], AT["gates"][:, 0:G], ACT.Tanh, scale=0.5, bias=half_bias[:, 2:3])\
              .then_inc(s["tr_done"], 1)
            nc.scalar.activation(tz[t.par][:, :], AT["gates"][:, G:2 * G], ACT.Tanh, scale=0.5, bias=half_bias[:, 3:4])\
              .then_inc(s["rz_copied"], 1)
            done(act, "rz_copied", t)
            nc.scalar.activation(zs[t.par][:, :], tz[t.par][:, :], ACT.Square, scale=0.5, bias=half_col[:, 0:1])\
              .then_inc(s["tz_done"], 1)

        def gate_exp(t):
            done(act, "gneg_done", t)
            reused(act, "gx_done", t)
            nc.scalar.activation(ge[t.par][:, :], gm[t.par][:, :], ACT.Exp, bias=gneg[t.par][:, 0:1])\
              .then_inc(s["ge_done"], 1)

        def values(t):
            done(act, "v_done", t)
            reused(act, "pv_done_", t)
            nc.scalar.activation(v17[t.par][:, :, 0:HD], AT["v"][0:G, 0:P].rearrange("p (h d) -> p h d", h=HEADS),
                                 ACT.Identity).then_inc(s["v_copied"], 1)

        pipeline(act, [
            (copy(tT, AT["n"][:, 0:G], "nT_done", "logits_done", "tT_copied", scale=col("g"), bias=col("b")), 8),
            (copy(kS, AT["k"][:, 0:G], "k_done", "kb_done", "k_copied", bias=col("bk1")), 4), (gates, 3),
            (exponentials, 5), (copy(oT, AT["o"][:, 0:G], "oT_done_", "wo_done", "oT_copied_", bias=col("bv1")), 6),
            (copy(x0T, AT["x0"][:, 0:G], "x0T_done", "yT_done", "x0T_copied"), 1),
            (copy(qT, AT["q"][:, 0:G], "q_done_", "s_done", "q_copied", scale=SCALE, bias=bq_scaled[:, 0:1]), 4),
            (gate_exp, 2), (highway(0, relu1, gate1, "x1_done"), 1),
            (copy(x2, AT["x2"][0:G, 0:P], "x2t_done", "att_done", "x2_copied"), 2), (copy_probs, 5), (values, 5),
            (copy(gpT, AT["gp"][0:G, 0:G], "gpT_done", "att_done", "gpT_copied"), 2),
            (copy(x4T, AT["x4"][:, 0:G], "x4T_done", "v_done", "x4T_copied"), 3),
            (copy(attT, AT["gather"][:, 0:G], "att_done", "rz_done", "att_copied"), 2),
            (highway(1, relu2, gate2, "x2_done"), 1)],
            GROUPS, *LOOP)
    @block.vector
    def _(dve):
        dve.wait_ge(weights1_in, 16)
        for i, name in enumerate(("cb0", "cb1", "frb", "ffb")):
            nc.vector.tensor_scalar(half_bias[:, i:i + 1], col(name), 0.5, None, ALU.mult).then_inc(s["halves"], 1)
        nc.vector.tensor_copy(member[:, :], V("member", rows_=IMG_G)).then_inc(s["consts"], 1)
        nc.vector.tensor_copy(apart[:, :], V("apart", rows_=IMG_G)).then_inc(s["consts"], 1)
        nc.vector.tensor_copy(sent[:, :, AT_TOKEN], V("token", rows_=G)).then_inc(s["halves"], 1)
        nc.vector.tensor_scalar(bq_scaled[:, :], col("bq1"), SCALE, None, ALU.mult).then_inc(s["halves"], 1)
        dve.wait_ge(s["consts"], 6)

        def moments(k, src, stats, mv, ve):
            def run(t):
                dve.drain()
                nc.vector.bn_stats(stats[t.par][:, :], src)
                dve.drain()
                nc.vector.bn_aggr(mv[t.par][:, :], stats[t.par][:, :]).then_inc(s[f"mv{k}_done"], 1)
                done(dve, f"mv{k}_done", t)
                reused(dve, f"rstd{k}_done", t)
                nc.vector.tensor_scalar(ve[t.par][:, :], mv[t.par][:, 1:2], EPS, None, ALU.add)\
                  .then_inc(s[f"ve{k}_done"], 1)
            return run

        def scale(out, src, k, mv, rstd, used, now):
            def stage(t):
                done(dve, f"rstd{k}_done", t)
                reused(dve, used, t)
                nc.vector.tensor_scalar(out[t.par][:, :], src(t), mv[t.par][:, 0:1], rstd[t.par][:, 0:1],
                                        ALU.subtract, ALU.mult).then_inc(s[now], 1)
            return stage

        def norm5(t):
            reused(dve, "nT_done", t)
            after(dve, kept[t.par], 16 * t.half)
            scale(nb, lambda t: y5[t.par][:, :], 5, mv5, rstd5, "nT_done", "nb_done")(t)

        def blend(k, mix, gate, mixb):
            def stage(t):
                done(dve, f"gate{k}_done", t)
                done(dve, f"mix{k}_done", t)
                after(dve, s[f"x{k}_done"], t.n)
                nc.vector.scalar_tensor_tensor(out=mixb[:, :], in0=gate[t.par][:, :], scalar=1.0, in1=mix[t.par][:, :],
                                               op0=ALU.add, op1=ALU.mult).then_inc(s[f"mixb{k}_done"], 1)
            return stage

        def highway(k, x, mixb, out, *used):
            def stage(t):
                done(dve, f"mixb{k}_done", t)
                for name in used:
                    reused(dve, name, t)
                nc.vector.scalar_tensor_tensor(out=out[t.par][:, :], in0=mixb[:, :], scalar=0.5, in1=x[t.par][:, :],
                                               op0=ALU.mult, op1=ALU.add).then_inc(s[f"x{k}_done"], 1)
            return stage

        def weigh(t):
            done(dve, "x2_done", t)
            reused(dve, "gram_done", t)
            nc.vector.tensor_scalar(aT[t.par][:, :], x2T[t.par][:, :], col("a3"), col("a2"), ALU.mult, ALU.add)\
              .then_inc(s["aT_done"], 1)

        def first_moments(t):
            dve.wait_ge(loaded, 16)
            if not isinstance(t.n, int) or t.n >= 2:
                dve.wait_ge(loaded, 32)
            moments(0, h_all[:, t.n, :], stats0, mv0, ve0)(t)

        def first_part(t):
            done(dve, "tz_done", t)
            after(dve, s["yT_done"], t.n)
            nc.vector.scalar_tensor_tensor(out=rx[:, :], in0=tr[t.par][:, :], scalar=1.0, in1=x0T[t.par][:, :],
                                           op0=ALU.add, op1=ALU.mult).then_inc(s["rx_done"], 1)

        def mix(t):
            done(dve, "rx_done", t)
            reused(dve, "y_done", t)
            nc.vector.scalar_tensor_tensor(out=yT[t.par][:, :], in0=rx[:, :], scalar=0.5, in1=zs[t.par][:, :],
                                           op0=ALU.mult, op1=ALU.add).then_inc(s["yT_done"], 1)

        def keep_logits(t):
            done(dve, "logits_done", t)
            nc.vector.tensor_tensor(lg_all[:, t.n, :], AT["logits"][0:G, 0:EXPERTS], row("gate_b", G), ALU.add)\
              .then_inc(s["logits_kept"], 1)

        o = T[0:G, 0, 0:HEADS * (HD + 1)].rearrange("p (h d) -> p h d", h=HEADS)

        def reciprocals(t):
            done(dve, "pv_done_", t)
            nc.vector.reciprocal(rs[t.par][:, :], o[:, :, HD]).then_inc(s["rs_done"], 1)

        def divide(t):
            done(dve, "rs_done", t)
            reused(dve, "oT_done_", t)
            nc.vector.tensor_tensor(on[t.par][:, :, :], o[:, :, 0:HD], over(rs[t.par][:, :], 2, HD, [G, HEADS, HD]),
                                    ALU.mult).then_inc(s["on_done"], 1)

        def third_residual(t):
            reused(dve, "x4_done", t)
            done(dve, "y_done", t)
            nc.vector.tensor_tensor(h_all[:, t.n, :], h_all[:, t.n, :], AT["y"][0:G, 0:P], ALU.add)\
              .then_inc(s["h3_done"], 1)
            moments(4, h_all[:, t.n, :], stats4, mv4, ve4)(t)

        def gate_scores(t):
            done(dve, "gram_done", t)
            reused(dve, "ge_done", t)
            nc.vector.tensor_scalar(gm[t.par][:, :], AT["gram"][0:G, 0:G], col("ab", G), 0.0, ALU.add, ALU.max)\
              .then_inc(s["gm_done"], 1)

        def gate_maxima(t):
            done(dve, "gm_done", t)
            nc.vector.tensor_reduce(gneg[t.par][:, :], gm[t.par][:, :], X, ALU.max, negate=True)\
              .then_inc(s["gneg_done"], 1)

        def gate_sums(t):
            done(dve, "ge_done", t)
            after(dve, s["gp_done"], t.n)
            nc.vector.tensor_tensor_reduce(out=gx[:, :], in0=ge[t.par][:, :], in1=V("same", rows_=G), scale=1.0, scalar=0.0,
                                           op0=ALU.mult, op1=ALU.add, accum_out=gsum[:, :]).then_inc(s["gx_done"], 1)

        def gate_reciprocals(t):
            done(dve, "gx_done", t)
            nc.vector.reciprocal(grec[:, :], gsum[:, :]).then_inc(s["grec_done"], 1)

        def gate_probs(t):
            done(dve, "grec_done", t)
            reused(dve, "gpT_done", t)
            nc.vector.tensor_scalar(gp[t.par][:, :], gx[:, :], grec[:, 0:1], None, ALU.mult).then_inc(s["gp_done"], 1)

        def scale4(t):
            reused(dve, "xb_done", t)
            scale(x4, lambda t: h_all[:, t.n, :], 4, mv4, rstd4, "x4T_done", "x4_done")(t)

        def fourth_residual(t):
            done(dve, "wo_done", t)
            reused(dve, "nb_done", t)
            dve.wait_ge(xb_kept[t.par], 16 * (t.half + 1))
            nc.vector.tensor_tensor(y5[t.par][:, :], AT["out"][0:G, 0:P], xb_all[:, t.n, :], ALU.add).then_inc(s["y5_done"], 1)
            moments(5, y5[t.par][:, :], stats5, mv5, ve5)(t)

        def maxima(t):
            done(dve, "s_done", t)
            reused(dve, "ex_done", t)
            nc.vector.tensor_reduce(less[t.par][:, :].rearrange("p (b h) -> p b h", b=2),
                                    S[0:G, :, 0:HALF * G].rearrange("p b (h j) -> p b h j", h=HALF), X, ALU.max,
                                    negate=True).then_inc(s["less_done"], 1)

        pipeline(dve, [
            (first_moments, 0), (maxima, 5), (blend(2, mix2, gate2, mixb2), 2),
            (highway(2, x1T, mixb2, x2T, "gram_done", "x2t_done"), 2), (first_part, 3), (weigh, 2), (mix, 3),
            (reciprocals, 6), (keep_logits, 8), (divide, 6),
            (scale(x0, lambda t: h_all[:, t.n, :], 0, mv0, rstd0, "x0T_done", "x0_done"), 1), (third_residual, 3),
            (gate_scores, 2), (gate_maxima, 2), (gate_sums, 2), (scale4, 3), (gate_reciprocals, 2), (gate_probs, 2),
            (norm5, 7), (blend(1, mix1, gate1, mixb1), 1), (highway(1, x0T, mixb1, x1T, "hw2_done"), 1),
            (fourth_residual, 6)],
            GROUPS, *LOOP)

def block2(nc, ctx, sem, banks, V, col, Wident, sent, lg_all, W1_sb, W2_sb, b1_sb, b2_sb, experts_in,
           sorted_dram, out, slots_empty, kept):
    def sb(name, shape, dt=F32):
        return ctx.enter_context(nc.sbuf_tensor(name, shape, dt))

    def pair(name, shape, dt=F32):
        return [sb(f"{name}{i}", shape, dt) for i in range(2)]

    NT, YB = banks[0:2], banks[2:4]
    HB, HT = [[banks[i][:, p, :] for p in range(2)] for i in (4, 5)]
    RB = banks[4][:, 0, :]
    GE = [G, GROUPS, EXPERTS]
    LASTG = TOKENS - (GROUPS - 1) * G

    top = sb("top", [G, GROUPS])
    less = sb("less", GE)
    expo = sb("expo", GE)
    esum = sb("esum", [G, GROUPS])
    cand = sb("cand", GE)
    first = sb("first", [G, GROUPS])
    hot = sb("hot", GE)
    hotv = sb("hotv", GE)
    hotb = sb("hotb", GE, BF16)
    before_b, ones_b = sb("before_b", [G, G], BF16), sb("ones_b", [G, G], BF16)
    count = sb("count", [G, EXPERTS])
    over_t = sb("over_t", [G, EXPERTS, TILES])
    tiles_e = sb("tiles_e", [G, EXPERTS])
    sofar = sb("sofar", [G, EXPERTS, EXPERTS])
    start = sb("start", [G, EXPERTS])
    end = sb("end", [G, EXPERTS])
    slot_e = sb("slot_e", GE)
    slot_h = sb("slot_h", GE)
    slot_f = sb("slot_f", [G, GROUPS])
    slot = sb("slot", [G, GROUPS], I32)
    past = sb("past", [G, SLOT_TILES, EXPERTS])
    owner_f, owner_c = sb("owner_f", [G, SLOT_TILES]), sb("owner_c", [G, SLOT_TILES])
    owner = sb("owner", [G, SLOT_TILES], I32)
    nt = pair("nt", [P, P])
    tT = pair("t2T", [P, P])
    hb = pair("hb", [P, FF])
    hg = pair("hg", [P, FF])
    hT = pair("hT", [P, FF])
    ye = pair("ye", [P, P])
    rest = pair("rest", [P, ROW - P])
    to = pair("to", [P, 1], I32)
    res = pair("res", [P, P])

    names = ("routed expo_done hot_ready ranks_done slots_done owners_done "
             "nT_done2 tT_done2 hid_done hb_done hg_done hT_done hT_copied y_done2 ye_done to_made res_done sending").split()
    s = {n: sem(n) for n in names}
    sorted_in = sem("sorted_in")
    nt_in = [sem("nt_in_even"), sem("nt_in_odd")]
    rest_in = [sem("rest_in_even"), sem("rest_in_odd")]
    out_done = [sem("out_done_even"), sem("out_done_odd")]
    LOOP = (3, (SLOT_TILES - 1) // 2)

    def done(eng, name, t):
        eng.wait_ge(s[name], t.n + 1)

    def reused(eng, name, t):
        after(eng, s[name], t.n - 1)

    block = ctx.enter_context(nc.Block())

    @block.gpsimd
    def _(pool):
        for q in kept:
            pool.wait_ge(q, 16 * GROUPS // 2)
        pool.wait_ge(slots_empty, 16)
        pool.wait_ge(s["slots_done"], 1)
        for g in range(GROUPS):
            rows = G if g < GROUPS - 1 else LASTG
            pool.indirect_dma_start(out=sorted_dram, out_offset=bass.IndirectOffsetOnAxis(ap=slot[0:rows, g:g + 1], axis=0),
                                    in_=sent[0:rows, g, :], in_offset=None).then_inc(sorted_in, 16)

        def send(t):
            done(pool, "res_done", t)
            pool.sem_inc(s["sending"], 1)
            pool.indirect_dma_start(out=out, out_offset=bass.IndirectOffsetOnAxis(ap=to[t.par][:, 0:1], axis=0),
                                    in_=res[t.par][:, :], in_offset=None).then_inc(out_done[t.par], 16)

        pipeline(pool, [(send, 4)], SLOT_TILES, *LOOP)
        for i, q in enumerate(out_done):
            pool.wait_ge(q, 16 * ((SLOT_TILES + 1 - i) // 2))

    @block.sync
    def _(sp):
        sp.wait_ge(sorted_in, 16 * GROUPS)

        in_tiles = sorted_dram.rearrange("(t p) e -> t p e", p=P)

        def load(t):
            reused(sp, "nT_done2", t)
            sp.dma_start(nt[t.par][:, :], in_tiles[t.n, :, 0:P]).then_inc(nt_in[t.par], 16)

        def load_rest(t):
            reused(sp, "res_done", t)
            sp.dma_start(rest[t.par][:, :], in_tiles[t.n, :, P:ROW]).then_inc(rest_in[t.par], 16)

        pipeline(sp, [(load, 0), (load_rest, 3)], SLOT_TILES, *LOOP)

    @block.tensor
    def _(pe):
        pe.wait_ge(s["hot_ready"], 3)
        R = RB[0:G, 0:GROUPS * EXPERTS]
        nc.tensor.matmul(R, before_b[:, :], hotb[:, :, :].rearrange("p g e -> p (g e)"), start=True, stop=False)
        for g in range(GROUPS - 1):
            later = GROUPS - 1 - g
            nc.tensor.matmul(R[:, (g + 1) * EXPERTS:], ones_b[:, :], over(hotb[:, g, :], 1, later, [G, later, EXPERTS]),
                             start=False, stop=(g == GROUPS - 2))
        for g in range(GROUPS):
            mm = nc.tensor.matmul(RB[0:G, GROUPS * EXPERTS:(GROUPS + 1) * EXPERTS], ones_b[:, :], hotb[:, g, :],
                                  start=(g == 0), stop=(g == GROUPS - 1))
        mm.then_inc(s["ranks_done"], 1)
        pe.wait_ge(s["owners_done"], 1)
        pe.wait_ge(experts_in, 64)

        def turn_n(t):
            pe.wait_ge(nt_in[t.par], 16 * (t.half + 1))
            reused(pe, "tT_done2", t)
            nc.tensor.transpose(NT[t.par][:, 0:P], nt[t.par][:, :], Wident).then_inc(s["nT_done2"], 1)

        expert_hidden = [pe.alloc_register(f"expert_hidden{i}") for i in range(2)]
        expert_last = [pe.alloc_register(f"expert_last{i}") for i in range(2)]

        def read_expert(t):
            pe.reg_load(expert_hidden[t.par], owner[0:1, bass.ds(t.n, 1)])

        def hand_over_expert(t):
            pe.reg_mov(expert_last[t.par], expert_hidden[t.par])

        def hidden(t):
            e = pe.snap(expert_hidden[t.par], min_val=0, max_val=EXPERTS - 1)
            done(pe, "tT_done2", t)
            reused(pe, "hb_done", t)
            nc.tensor.matmul(HB[t.par], tT[t.par][:, :], W1_sb[:, bass.ds(e * FF, FF)], start=True, stop=True)\
              .then_inc(s["hid_done"], 1)

        def turn_h(t):
            done(pe, "hg_done", t)
            reused(pe, "hT_copied", t)
            for c in range(FC):
                mm = nc.tensor.transpose(HT[t.par][:, c * P:(c + 1) * P], hg[t.par][:, c * P:(c + 1) * P], Wident)
            mm.then_inc(s["hT_done"], 1)

        def expert_out(t):
            e = pe.snap(expert_last[t.par], min_val=0, max_val=EXPERTS - 1)
            done(pe, "hT_copied", t)
            reused(pe, "ye_done", t)
            for c in range(FC):
                mm = nc.tensor.matmul(YB[t.par][:, 0:P], hT[t.par][:, c * P:(c + 1) * P],
                                      W2_sb[:, bass.ds(e * FF + c * P, P)], start=(c == 0), stop=(c == FC - 1))
            mm.then_inc(s["y_done2"], 1)

        pipeline(pe, [(hidden, 1), (turn_n, 0), (expert_out, 3), (hand_over_expert, 1), (read_expert, 0), (turn_h, 2)],
                 SLOT_TILES, *LOOP)

    @block.scalar
    def _(act):
        act.wait_ge(s["routed"], 2)
        nc.scalar.activation(expo[:, :, :], less[:, :, :], ACT.Exp).then_inc(s["expo_done"], 1)

        def gain(t):
            done(act, "nT_done2", t)
            reused(act, "hid_done", t)
            nc.scalar.activation(tT[t.par][:, :], NT[t.par][:, 0:P], ACT.Identity, scale=col("g"), bias=col("b"))\
              .then_inc(s["tT_done2"], 1)

        def gelu(t):
            done(act, "hb_done", t)
            reused(act, "hT_done", t)
            nc.scalar.activation(hg[t.par][:, :], hb[t.par][:, :], ACT.Gelu_apprx_tanh).then_inc(s["hg_done"], 1)

        def copy_h(t):
            done(act, "hT_done", t)
            reused(act, "y_done2", t)
            nc.scalar.activation(hT[t.par][:, :], HT[t.par], ACT.Identity).then_inc(s["hT_copied"], 1)

        pipeline(act, [(copy_h, 3), (gain, 0), (gelu, 1)], SLOT_TILES, *LOOP)

    @block.vector
    def _(dve):
        k = [0]

        def chain(ins):
            k[0] += 1
            ins.then_inc(s["routed"], 1)
            dve.wait_ge(s["routed"], k[0])

        chain(nc.vector.tensor_reduce(top[:, :], lg_all[:, :, :], X, ALU.max))
        chain(nc.vector.tensor_tensor(less[:, :, :], lg_all[:, :, :], over(top[:, :], 2, EXPERTS, GE), ALU.subtract))
        chain(nc.vector.scalar_tensor_tensor(out=cand[:, :, :], in0=less[:, :, :], scalar=0.0,
                                             in1=over(V("rank_w", rows_=G), 1, GROUPS, GE), op0=ALU.is_ge, op1=ALU.mult))
        chain(nc.vector.tensor_reduce(first[:, :], cand[:, :, :], X, ALU.max))
        chain(nc.vector.tensor_tensor(hot[:, :, :], cand[:, :, :], over(first[:, :], 2, EXPERTS, GE), ALU.is_equal))
        chain(nc.vector.tensor_tensor(hotv[:, :, :], hot[:, :, :], over(V("valid", rows_=G), 2, EXPERTS, GE), ALU.mult))
        nc.vector.tensor_copy(hotb[:, :, :], hotv[:, :, :]).then_inc(s["hot_ready"], 1)
        nc.vector.tensor_copy(before_b[:, :], V("before", rows_=G)).then_inc(s["hot_ready"], 1)
        nc.vector.tensor_copy(ones_b[:, :], V("ones", rows_=G)).then_inc(s["hot_ready"], 1)
        dve.wait_ge(s["expo_done"], 1)
        chain(nc.vector.tensor_reduce(esum[:, :], expo[:, :, :], X, ALU.add))
        chain(nc.vector.reciprocal(sent[:, :, AT_WEIGHT], esum[:, :]))
        dve.wait_ge(s["ranks_done"], 1)
        chain(nc.vector.tensor_copy(count[:, :], RB[0:G, GROUPS * EXPERTS:(GROUPS + 1) * EXPERTS]))
        chain(nc.vector.tensor_tensor(over_t[:, :, :], over(count[:, :], 2, TILES, [G, EXPERTS, TILES]),
                                      over(V("tile_lo", rows_=G), 1, EXPERTS, [G, EXPERTS, TILES]), ALU.is_gt))
        chain(nc.vector.tensor_reduce(tiles_e[:, :], over_t[:, :, :], X, ALU.add))
        chain(nc.vector.tensor_tensor(sofar[:, :, :], over(tiles_e[:, :], 1, EXPERTS, [G, EXPERTS, EXPERTS]),
                                      V("lower", rows_=G).rearrange("p (a b) -> p a b", a=EXPERTS), ALU.mult))
        chain(nc.vector.tensor_reduce(start[:, :], sofar[:, :, :], X, ALU.add))
        chain(nc.vector.scalar_tensor_tensor(out=slot_e[:, :, :], in0=over(start[:, :], 1, GROUPS, GE), scalar=float(P),
                                             in1=RB[0:G, 0:GROUPS * EXPERTS].rearrange("p (g e) -> p g e", g=GROUPS),
                                             op0=ALU.mult, op1=ALU.add))
        chain(nc.vector.tensor_tensor(slot_h[:, :, :], slot_e[:, :, :], hotv[:, :, :], ALU.mult))
        chain(nc.vector.tensor_reduce(slot_f[:, :], slot_h[:, :, :], X, ALU.add))
        nc.vector.tensor_copy(slot[:, :], slot_f[:, :]).then_inc(s["slots_done"], 1)
        chain(nc.vector.tensor_tensor(end[:, :], start[:, :], tiles_e[:, :], ALU.add))
        chain(nc.vector.tensor_tensor(past[:, :, :], over(V("tile_no", rows_=G), 2, EXPERTS, [G, SLOT_TILES, EXPERTS]),
                                      over(end[:, :], 1, SLOT_TILES, [G, SLOT_TILES, EXPERTS]), ALU.is_ge))
        chain(nc.vector.tensor_reduce(owner_f[:, :], past[:, :, :], X, ALU.add))
        chain(nc.vector.tensor_scalar(owner_c[:, :], owner_f[:, :], float(EXPERTS - 1), None, ALU.min))
        nc.vector.tensor_copy(owner[:, :], owner_c[:, :]).then_inc(s["owners_done"], 1)
        dve.wait_ge(s["owners_done"], 1)
        dve.wait_ge(experts_in, 64)

        def bias1(t):
            e = dve.value_load(owner[0:1, bass.ds(t.n, 1)], min_val=0, max_val=EXPERTS - 1)
            done(dve, "hid_done", t)
            reused(dve, "hg_done", t)
            nc.vector.tensor_tensor(hb[t.par][:, :], HB[t.par], b1_sb[:, bass.ds(e * FF, FF)], ALU.add)\
              .then_inc(s["hb_done"], 1)

        def bias2(t):
            e = dve.value_load(owner[0:1, bass.ds(t.n, 1)], min_val=0, max_val=EXPERTS - 1)
            done(dve, "y_done2", t)
            nc.vector.tensor_tensor(ye[t.par][:, :], YB[t.par][:, 0:P], b2_sb[:, bass.ds(e * P, P)], ALU.add)\
              .then_inc(s["ye_done"], 1)

        def destinations(t):
            dve.wait_ge(rest_in[t.par], 16 * (t.half + 1))
            after(dve, out_done[t.par], 16 * t.half)
            nc.vector.tensor_copy(to[t.par][:, :], rest[t.par][:, AT_TOKEN - P:AT_TOKEN - P + 1])\
              .then_inc(s["to_made"], 1)

        def residual(t):
            done(dve, "ye_done", t)
            nc.vector.scalar_tensor_tensor(out=res[t.par][:, :], in0=ye[t.par][:, :],
                                           scalar=rest[t.par][:, AT_WEIGHT - P:AT_WEIGHT - P + 1],
                                           in1=rest[t.par][:, 0:P], op0=ALU.mult, op1=ALU.add)\
              .then_inc(s["res_done"], 1)

        pipeline(dve, [(bias1, 1), (bias2, 3), (destinations, 3), (residual, 3)], SLOT_TILES, *LOOP)


def layout(x, w):
    f = np.float32
    a = {k: np.asarray(v) for k, v in w.items()}
    x = np.asarray(x)
    pt = x.reshape(IMAGES, 3, 6, 16, 6, 16).transpose(2, 4, 1, 3, 5, 0)
    pt = pt.reshape(TILES, 2, CHUNKS, P, IMAGES).transpose(0, 3, 2, 1, 4).reshape(TILES, P, CHUNKS * P)

    ident = np.eye(P, dtype=f)
    fh = np.arange(P)[:, None] // HD == np.arange(HEADS)[None, :]
    parity = np.arange(P)[:, None] // IMAGES == np.arange(HEADS)[None, :] % 2
    parts = {
        "tok": a["L0_tok_w"].T.reshape(CHUNKS, P, P).transpose(1, 0, 2).reshape(P, CHUNKS * P),
        "in_proj": a["L0_attn_in_proj_w"].T, "out_proj": a["L0_attn_out_proj_w"].T,
        "pos_w": a["L0_attn_pos_w"].T, "pos": a["L0_attn_pos_emb"][0, 0:REL].T,
        "ident": ident, "head_mask": fh.astype(f), "half_mask": parity.astype(f)}
    weights = np.concatenate([parts[n] for n, _ in _WEIGHTS], 1)

    g = np.arange(G)

    def pad(m):
        return np.concatenate([m, np.zeros((P - m.shape[0], m.shape[1]), f)], 0)

    same = (g[:, None] // POSITIONS == g[None, :] // POSITIONS).astype(f)
    member = (np.arange(IMG_G)[:, None] == g[None, :] // POSITIONS).astype(f)
    apart = np.where(member > 0, f(0), f(FAR))
    token = np.arange(GROUPS)[None, :] * G + np.arange(P)[:, None]
    parts = {
        "tW": a["L1_attn_tW"].transpose(1, 0, 2).reshape(P, 2 * P),
        "cW": a["L1_attn_cW"].transpose(1, 0, 2).reshape(P, 2 * P),
        "ff": a["L1_attn_ffW"].reshape(2, P, P).transpose(1, 0, 2).reshape(P, 2 * P),
        "fr": a["L1_attn_frW"].reshape(2, P, P).transpose(1, 0, 2).reshape(P, 2 * P),
        "Wq": a["L1_ffn_Wq"], "Wk": a["L1_ffn_Wk"], "Wv": a["L1_ffn_Wv"], "Wo": a["L1_ffn_Wo"],
        "gate": a["L1_ffn_gate_W"], "same": pad(same),
        "before": pad((g[:, None] < g[None, :]).astype(f)), "ones": np.ones((P, G), f),
        "member": pad(member), "apart": pad(np.tile(apart, (1, 4))),
        "valid": ((token < TOKENS) & (np.arange(P)[:, None] < G)).astype(f),
        "rank_w": np.tile(np.arange(EXPERTS, 0, -1, dtype=f), (P, 1)),
        "tile_lo": np.tile(np.arange(TILES, dtype=f) * P, (P, 1)),
        "tile_no": np.tile(np.arange(SLOT_TILES, dtype=f), (P, 1)),
        "lower": np.tile(np.tril(np.ones((EXPERTS, EXPERTS), f), -1).reshape(1, -1), (P, 1)),
        "token": token.astype(f)}
    weights1 = np.concatenate([parts[n] for n, _ in _WEIGHTS1], 1)

    ipb, aw = a["L0_attn_in_proj_b"], a["L1_attn_aW"]
    columns = np.stack([
        ipb[0:P], ipb[P:2 * P], ipb[2 * P:], a["L0_attn_pos_bias_u"].reshape(P), a["L0_attn_pos_bias_v"].reshape(P),
        a["L1_attn_tb"][0], a["L1_attn_tb"][1], a["L1_attn_cb"][0], a["L1_attn_cb"][1], aw[0:P], aw[P:2 * P],
        aw[2 * P:], a["L1_attn_frb"], a["L1_attn_ffb"], a["L1_ffn_ln1_g"], a["L1_ffn_ln1_b"], a["L1_ffn_bq"],
        a["L1_ffn_bk"], a["L1_ffn_bv"], np.broadcast_to(a["L1_attn_ab"], (P,))], 1)
    rows = np.concatenate([a["L0_tok_b"], a["L0_attn_out_proj_b"], a["L1_ffn_bo"], a["L1_ffn_gate_b"]])
    rows = np.broadcast_to(rows[None, :], (P, WIDTH_R))
    empty = np.zeros((SLOTS, ROW), f)
    empty[:, AT_TOKEN] = TOKENS + np.arange(SLOTS)
    return {
        "patches": pt, "weights": weights, "weights1": weights1, "columns": columns, "rows": rows,
        "b1_rows": np.broadcast_to(a["L1_ffn_b1"].reshape(1, EXPERTS * FF), (P, EXPERTS * FF)),
        "b2_rows": np.broadcast_to(a["L1_ffn_b2"].reshape(1, EXPERTS * P), (P, EXPERTS * P)),
        "W1": a["L1_ffn_W1"].transpose(1, 0, 2).reshape(P, EXPERTS * FF),
        "W2": a["L1_ffn_W2"].reshape(EXPERTS, FC, P, P).transpose(2, 0, 1, 3).reshape(P, EXPERTS * FC * P),
        "zeros": np.zeros((P, P), f), "empty": empty}


def kernel(x, **inputs):
    import concourse.bacc as _bacc
    from concourse.bass_utils import run_bass_kernel_spmd as _run

    nc = _bacc.Bacc("TRN2", target_bir_lowering=False, num_devices=1)
    arrays, args = {}, []
    for name, a in layout(x, inputs).items():
        a = np.ascontiguousarray(a)
        arrays[name] = a
        args.append(nc.dram_tensor(name, a.shape, mybir.dt.from_np(a.dtype), kind="ExternalInput").ap())
    args.append(nc.dram_tensor("out", (TOKENS + SLOTS, P), F32, kind="ExternalOutput").ap())
    for name, shape in (("bd_dram", (2, P, HEADS * REL)), ("hs_dram", (GROUPS * G, P)),
                        ("sorted_dram", (SLOTS, ROW))):
        args.append(nc.dram_tensor(name, shape, F32, kind="Internal").ap())
    tower(nc, *args)
    r = _run(nc, [arrays], core_ids=[0])
    return r.results[0]["out"][0:TOKENS].reshape(IMAGES, POSITIONS, P)
```

```python
from contextlib import ExitStack

import numpy as np

import concourse.bass as bass
from concourse import mybir

F32 = mybir.dt.float32
BF16 = mybir.dt.bfloat16
I32 = mybir.dt.int32
U32 = mybir.dt.uint32
ALU = mybir.AluOpType
ACT = mybir.ActivationFunctionType
X = mybir.AxisListType.X

P = 128
IMAGES, POSITIONS = 64, 36
CHUNKS = 6
HEADS, HD = 8, 16
TOKENS = IMAGES * POSITIONS
TILES = TOKENS // P
REL = 2 * IMAGES - 1
IMG_G = 3
G = IMG_G * POSITIONS
GROUPS = -(-IMAGES // IMG_G)
EXPERTS, FF = 8, 512
FC = FF // P
FIRST = FF + FC
SLOT_TILES = TOKENS // P + EXPERTS - 1
SLOTS = SLOT_TILES * P
AT_H, AT_WEIGHT, AT_TOKEN = P, 2 * P, 2 * P + 1
ROW = 2 * P + 2
EPS = 1e-5
SCALE = float(HD) ** -0.5
FAR = -float(2 ** 100)

_WEIGHTS = [("tok", CHUNKS * P), ("in_proj", 3 * P), ("out_proj", P), ("pos_w", P), ("pos", REL),
            ("ident", P), ("head_mask", HEADS), ("half_mask", HEADS)]
_WEIGHTS1 = [("tW", 2 * P), ("cW", 2 * P), ("ff", 2 * P), ("fr", 2 * P), ("Wq", P), ("Wk", P), ("Wv", P),
             ("Wo", P), ("gate", EXPERTS), ("same", G), ("before", G), ("ones", G), ("member", G),
             ("apart", 4 * G), ("valid", GROUPS), ("rank_w", EXPERTS), ("tile_lo", TILES), ("tile_no", SLOT_TILES),
             ("lower", EXPERTS * EXPERTS), ("token", GROUPS)]
_COLUMNS = ["bq0", "bk0", "bv0", "u", "v", "tb0", "tb1", "cb0", "cb1", "a1", "a2", "a3", "frb", "ffb", "g", "b",
            "bq1", "bk1", "bv1", "ab"]
_ROWS = [("tok_b", P), ("out_b", P), ("bo", P), ("gate_b", EXPERTS)]


def places(items):
    at, out = 0, {}
    for name, width in items:
        out[name] = (at, width)
        at += width
    return out, at


AT_W, WIDTH_W = places(_WEIGHTS)
AT_W1, WIDTH_W1 = places(_WEIGHTS1)
AT_R, WIDTH_R = places(_ROWS)


class Tile:

    def __init__(self, u, c, lag, tiles):
        self.n = 2 * u + (c - lag)
        self.par = (c - lag) % 2
        self.half = u + (c - lag) // 2
        self.live = not isinstance(u, int) or 0 <= self.n < tiles


def after(eng, sem, count):
    if not isinstance(count, int) or count > 0:
        eng.wait_ge(sem, count)


def pipeline(eng, stages, tiles, loop_from, loop_to):
    last = tiles + max(lag for _, lag in stages)

    def step(u, c):
        for stage, lag in stages:
            t = Tile(u, c, lag, tiles)
            if t.live:
                stage(t)

    for i in range(2 * loop_from):
        step(i // 2, i % 2)
    with eng.Fori(loop_from, loop_to) as u:
        step(u, 0)
        step(u, 1)
    for i in range(2 * loop_to, last):
        step(i // 2, i % 2)


def last_read(eng, users_of, user, t, tiles):
    users = next(us for us in users_of.values() if user in [name for name, _, _ in us])
    at = [name for name, _, _ in users].index(user)
    step = t.n + users[at][1]
    for back in range(1, len(users) + 1):
        _, lag, read = users[(at - back) % len(users)]
        n = step - (back > at) - lag
        if not isinstance(n, int) or 0 <= n < tiles:
            return eng.wait_ge(read, n + 1)


def over(ap, axis, count, shape):
    return ap.unsqueeze(axis).broadcast_to(shape)


def tower(nc, patches, weights, weights1, columns, rows, b2_rows, W1, W2, zeros, empty, out,
          bd_dram, hs_dram, sorted_dram):
    with ExitStack() as ctx:
        def sb(name, shape, dt=F32):
            return ctx.enter_context(nc.sbuf_tensor(name, shape, dt))

        def sem(name):
            return ctx.enter_context(nc.semaphore(name))

        def bank_pair(name):
            return ctx.enter_context(nc.psum_tensor(name, [P, 2, 512], F32))

        banks = [ctx.enter_context(nc.psum_tensor(f"bank{i}", [P, 512], F32)) for i in range(4)]
        banks += [bank_pair("bank45"), bank_pair("bank67")]

        w = sb("w", [P, WIDTH_W])
        w1 = sb("w1", [P, WIDTH_W1])
        cols = sb("cols", [P, len(_COLUMNS)])
        bias_rows = sb("bias_rows", [P, WIDTH_R])

        def W(name, a=0, b=None):
            at, width = AT_W[name]
            return w[:, at + a:at + (width if b is None else b)]

        def V(name, a=0, b=None, rows_=P):
            at, width = AT_W1[name]
            return w1[0:rows_, at + a:at + (width if b is None else b)]

        def col(name, rows_=P):
            c = _COLUMNS.index(name)
            return cols[0:rows_, c:c + 1]

        def row(name, rows_=P):
            at, width = AT_R[name]
            return bias_rows[0:rows_, at:at + width]

        weights_in = sem("weights_in")
        weights1_in = sem("weights1_in")
        stored = [sem("stored_even"), sem("stored_odd")]

        pads_zero = sem("pads_zero")
        kept = [sem("kept_even"), sem("kept_odd")]
        sent = sb("sent", [G, GROUPS, ROW])
        n_all = sent[:, :, 0:P]
        h_all = sent[:, :, AT_H:AT_H + P]
        xb_all = sb("xb_all", [G, GROUPS, P])
        lg_all = sb("lg_all", [G, GROUPS, EXPERTS])
        slots_empty = sem("slots_empty")
        experts_in = sem("experts_in")
        W1_sb = sb("W1_sb", [P, EXPERTS * FIRST])
        W2_sb = sb("W2_sb", [P, EXPERTS * FF])
        b2_sb = sb("b2_sb", [P, EXPERTS * P])
        loads = ((W1_sb, W1), (W2_sb, W2), (b2_sb, b2_rows))
        own = []

        def part_sem(name):
            own.append(nc.alloc_semaphore(name=name))
            return own[-1]

        with ExitStack() as ctx0:
            block0(nc, ctx0, part_sem, banks, W, col, row, w, w1, cols, bias_rows, patches, weights, weights1,
                   columns, rows, weights_in, weights1_in, stored, bd_dram, hs_dram, zeros, pads_zero)
        nc.clear_and_free_semaphores(own)
        nc.all_engine_barrier()
        own.clear()
        with ExitStack() as ctx1:
            block1(nc, ctx1, part_sem, banks, V, col, row, W("ident"), W("head_mask"), sent, h_all, xb_all, n_all, lg_all, hs_dram,
                   stored, pads_zero, weights1_in, kept, loads, experts_in, sorted_dram, slots_empty, empty)
        nc.clear_and_free_semaphores(own)
        nc.all_engine_barrier()
        own.clear()
        with ExitStack() as ctx2:
            block2(nc, ctx2, part_sem, banks, V, col, W("ident"), sent, lg_all, W1_sb, W2_sb, b2_sb, experts_in,
                   sorted_dram, out, slots_empty, kept)


def block0(nc, ctx, sem, banks, W, col, row, w, w1, cols, bias_rows, patches, weights, weights1,
           columns, rows, weights_in, weights1_in, stored, bd_dram, hs_dram, zeros, pads_zero):
    def sb(name, shape, dt=F32):
        return ctx.enter_context(nc.sbuf_tensor(name, shape, dt))

    def pair(name, shape, dt=F32):
        return [sb(f"{name}{i}", shape, dt) for i in range(2)]

    BD = banks[4]

    patch = pair("patch", [P, CHUNKS * P])
    h0 = sb("h0", [P, TILES, P])
    stats = pair("stats", [P, 6])
    mv = pair("mv", [P, 2])
    ve = pair("ve", [P, 1])
    rstd = pair("rstd", [P, 1])
    xn = pair("xn", [P, P])
    xT = pair("xT", [P, 2, 2, IMAGES])
    qu = pair("qu", [P, P])
    qv = pair("qv", [P, P])
    kS0 = pair("kS0", [P, P])
    kb = pair("kb", [P, HEADS, P])
    vv = pair("vv", [P, 2, HEADS, HD + 1])
    pos_p = sb("pos_p", [P, REL])
    pb = sb("pb", [P, HEADS, REL])
    bias_u = sb("bias_u", [P, 1])
    bias_v = sb("bias_v", [P, 1])
    bd = pair("bd", [P, HEADS * REL])
    bs = pair("bs", [P, HEADS * IMAGES])
    s1 = pair("s1", [P, HEADS, IMAGES])
    less = pair("less", [P, HEADS])
    ex = pair("ex", [P, HEADS * IMAGES])
    pT = pair("pT", [P, 4 * P])
    rs = pair("rs", [P, HEADS])
    on = pair("on", [P, HEADS, HD])
    oT = pair("oT", [P, P])
    st2 = pair("st2", [P, 6])
    mv2 = pair("mv2", [P, 2])
    ve2 = pair("ve2", [P, 1])
    rstd2 = pair("rstd2", [P, 1])
    nrm = pair("nrm", [P, P])
    att = pair("att", [P, P])
    h2 = pair("h2", [P, P])
    half_pow = sb("half_pow", [P, 1])

    patch_in = [sem("patch_in_even"), sem("patch_in_odd")]
    tok_in = sem("tok_in")
    half_pow_set = sem("half_pow_set")
    ones_set = sem("ones_set")
    biases_made = sem("biases_made")
    pos_projected = sem("pos_projected")
    pos_ready = sem("pos_ready")
    tok_done = sem("tok_done")
    h_ready = sem("h_ready")
    mv_done = sem("mv_done")
    ve_done = sem("ve_done")
    rstd_done = sem("rstd_done")
    xn_done = sem("xn_done")
    xT_done = sem("xT_done")
    xT_copied = sem("xT_copied")
    q_done = sem("q_done")
    qv_copied = sem("qv_copied")
    qu_copied = sem("qu_copied")
    k_done = sem("k_done0")
    k_copied = sem("k_copied0")
    v_done = sem("v_done0")
    kb_made = sem("kb_made")
    vv_made = sem("vv_made")
    bd_done = sem("bd_done")
    bd_copied = sem("bd_copied")
    bd_out = [sem("bd_out_even"), sem("bd_out_odd")]
    bd_back = [sem("bd_back_even"), sem("bd_back_odd")]
    ac_done = sem("ac_done")
    scores_added = sem("scores_added")
    max_found = sem("max_found")
    exp_done = sem("exp_done")
    pT_done = sem("pT_done")
    pT_copied = sem("pT_copied")
    pv_done = sem("pv_done")
    sums_inverted = sem("sums_inverted")
    attn_normal = sem("attn_normal")
    oT_done = sem("oT_done")
    oT_copied = sem("oT_copied")
    proj_done = sem("proj_done")
    att_biased = sem("att_biased")
    mv2_done = sem("mv2_done")
    ve2_done = sem("ve2_done")
    rstd2_done = sem("rstd2_done")
    nrm_done = sem("nrm_done")
    h2_ready = sem("h2_ready")

    hs_rows = hs_dram[0:TOKENS, :].rearrange("(l s) e -> s l e", s=POSITIONS)
    LOOP = (4, TILES // 2)
    USERS = {
        "bank0": [("embed", 1, h_ready), ("out", 6, att_biased)],
        "bank1": [("v", 3, vv_made)],
        "bank2": [("k", 3, k_copied)],
        "bank3": [("content", 4, scores_added)],
        "bank6": [("attend", 6, attn_normal), ("probs", 5, pT_copied)],
        "bank7": [("q", 3, qu_copied), ("x", 2, xT_copied), ("o", 6, oT_copied)],
        "bank45": [("positions", 3, bd_copied)],
    }
    AT = {user: bank for name, bank in (("bank0", banks[0]), ("bank1", banks[1]), ("bank2", banks[2]), ("bank3", banks[3]), ("bank6", banks[5][:, 0, :]), ("bank7", banks[5][:, 1, :]))
          for user, _, _ in USERS[name]}

    def done(eng, sem_, t):
        eng.wait_ge(sem_, t.n + 1)

    def reused(eng, sem_, t):
        after(eng, sem_, t.n - 1)

    def bank_read(eng, user, t):
        last_read(eng, USERS, user, t, TILES)

    block = ctx.enter_context(nc.Block())

    @block.sync
    def _(sp):
        sp.dma_start(w[:, 0:CHUNKS * P], weights[:, 0:CHUNKS * P]).then_inc(tok_in, 16)

        def load_patches(t):
            reused(sp, tok_done, t)
            sp.dma_start(patch[t.par][:, :], patches[t.n]).then_inc(patch_in[t.par], 16)
            if isinstance(t.n, int) and t.n == 0:
                sp.dma_start(bias_rows[:, :], rows).then_inc(weights_in, 16)
                sp.dma_start(cols[:, :], columns).then_inc(weights_in, 16)
                sp.dma_start(w[:, CHUNKS * P:], weights[:, CHUNKS * P:]).then_inc(weights_in, 16)

        def shift_back(t):
            sp.wait_ge(bd_copied, t.n + 1)
            sp.dma_start(bd_dram[t.par], bd[t.par][:, :]).then_inc(bd_out[t.par], 16)
            sp.wait_ge(bd_out[t.par], 16 * (t.half + 1))
            for s in range(2):
                src = bass.AP(tensor=bd_dram.tensor,
                              offset=(t.par * P + s * IMAGES) * HEADS * REL + IMAGES - 1,
                              ap=[[HEADS * REL - 1, IMAGES], [REL, HEADS], [1, IMAGES]])
                sp.dma_start(bs[t.par][s * IMAGES:(s + 1) * IMAGES, :].rearrange("p (h j) -> p h j", h=HEADS),
                             src).then_inc(bd_back[t.par], 16)

        def store(t):
            sp.wait_ge(h2_ready, t.n + 1)
            for s in range(2):
                sp.dma_start(hs_rows[2 * t.n + s], h2[t.par][s * IMAGES:(s + 1) * IMAGES, :])\
                  .then_inc(stored[t.par], 16)

        pipeline(sp, [(load_patches, 0), (shift_back, 3), (store, 6)], TILES, *LOOP)

    @block.tensor
    def _(pe):
        pe.wait_ge(tok_in, 16)

        def embed(t):
            if isinstance(t.n, int) and t.n == 1:
                pe.wait_ge(weights_in, 48)
                nc.tensor.matmul(BD[:, 0, 0:REL], W("pos_w"), W("pos"), start=True, stop=True).then_inc(pos_projected, 1)
            pe.wait_ge(patch_in[t.par], 16 * (t.half + 1))
            bank_read(pe, "embed", t)
            for c in range(CHUNKS):
                mm = nc.tensor.matmul(AT["embed"][:, 0:P], patch[t.par][:, c * P:(c + 1) * P],
                                      W("tok", c * P, (c + 1) * P), start=(c == 0), stop=(c == CHUNKS - 1))
            mm.then_inc(tok_done, 1)

        def content(s):
            def stage(t):
                if s == 0:
                    done(pe, qu_copied, t)
                    done(pe, kb_made, t)
                    bank_read(pe, "content", t)
                mm = nc.tensor.matmul(AT["content"][s * IMAGES:(s + 1) * IMAGES, :],
                                      qu[t.par][:, s * IMAGES:(s + 1) * IMAGES],
                                      kb[t.par][:, :, s * IMAGES:(s + 1) * IMAGES], start=True, stop=True)
                if s == 1:
                    mm.then_inc(ac_done, 1)
            return stage

        def turn_probs(t):
            done(pe, exp_done, t)
            bank_read(pe, "probs", t)
            for g in range(4):
                mm = nc.tensor.transpose(AT["probs"][:, g * P:(g + 1) * P], ex[t.par][:, g * P:(g + 1) * P], W("ident"))
            mm.then_inc(pT_done, 1)

        def turn_x(t):
            done(pe, xn_done, t)
            bank_read(pe, "x", t)
            nc.tensor.transpose(AT["x"][:, 0:P], xn[t.par][:, :], W("ident")).then_inc(xT_done, 1)

        def attend(t):
            done(pe, pT_copied, t)
            done(pe, vv_made, t)
            bank_read(pe, "attend", t)
            for s in range(2):
                for g in range(4):
                    mm = nc.tensor.matmul(
                        AT["attend"][s * IMAGES:(s + 1) * IMAGES, g * 34:(g + 1) * 34],
                        pT[t.par][:, g * P + s * IMAGES:g * P + (s + 1) * IMAGES],
                        vv[t.par][:, s, 2 * g:2 * g + 2, :].rearrange("p h d -> p (h d)"), start=True, stop=True)
            mm.then_inc(pv_done, 1)

        def queries(t):
            done(pe, xT_copied, t)
            bank_read(pe, "q", t)
            nc.tensor.matmul(AT["q"][:, 0:P], W("in_proj", 0, P), xT[t.par][:, :, 0, :], start=True, stop=True)\
              .then_inc(q_done, 1)

        def keys(t):
            done(pe, xT_copied, t)
            bank_read(pe, "k", t)
            nc.tensor.matmul(AT["k"][:, 0:P], W("in_proj", P, 2 * P), xT[t.par][:, :, 0, :], start=True, stop=True)\
              .then_inc(k_done, 1)

        def values(t):
            done(pe, xT_copied, t)
            bank_read(pe, "v", t)
            for s in range(2):
                twice = xT[t.par][:, s, :, :].rearrange("p r l -> p (r l)")
                mm = nc.tensor.matmul(AT["v"][:, s * P:(s + 1) * P], twice, W("in_proj", 2 * P, 3 * P),
                                      start=True, stop=True)
            mm.then_inc(v_done, 1)

        def turn_o(t):
            done(pe, attn_normal, t)
            bank_read(pe, "o", t)
            nc.tensor.transpose(AT["o"][:, 0:P], on[t.par][:, :, :].rearrange("p h d -> p (h d)"), W("ident"))\
              .then_inc(oT_done, 1)

        def positions(b):
            def stage(t):
                if b == 0:
                    done(pe, qv_copied, t)
                    if isinstance(t.n, int) and t.n == 0:
                        pe.wait_ge(pos_ready, 1)
                    bank_read(pe, "positions", t)
                mm = nc.tensor.matmul(BD[:, b, 0:4 * REL], qv[t.par][:, :],
                                      pb[:, 4 * b:4 * b + 4, :].rearrange("p h n -> p (h n)"), start=True, stop=True)
                if b == 1:
                    mm.then_inc(bd_done, 1)
            return stage

        def project_out(t):
            done(pe, oT_copied, t)
            bank_read(pe, "out", t)
            nc.tensor.matmul(AT["out"][:, 0:P], oT[t.par][:, :], W("out_proj"), start=True, stop=True)\
              .then_inc(proj_done, 1)

        pipeline(pe, [(keys, 3), (queries, 3), (attend, 6), (embed, 1), (content(0), 4), (positions(0), 3),
                      (turn_x, 2), (positions(1), 3), (turn_o, 6), (turn_probs, 5), (content(1), 4), (values, 3),
                      (project_out, 6)], TILES, *LOOP)

    @block.scalar
    def _(act):
        act.wait_ge(pos_projected, 1)
        nc.scalar.activation(pos_p[:, :], BD[:, 0, 0:REL], ACT.Identity).then_inc(pos_projected, 1)

        def keep_positions(t):
            act.wait_ge(bd_done, t.n + 1)
            after(act, bd_out[t.par], 16 * t.half)
            nc.scalar.activation(bd[t.par][:, :].rearrange("p (b n) -> p b n", b=2), BD[:, :, 0:4 * REL],
                                 ACT.Identity).then_inc(bd_copied, 1)

        def exponentials(t):
            done(act, max_found, t)
            reused(act, pT_done, t)
            for h in range(HEADS):
                e = nc.scalar.activation(ex[t.par][:, h * IMAGES:(h + 1) * IMAGES], s1[t.par][:, h, :], ACT.Exp,
                                         bias=less[t.par][:, h:h + 1])
            e.then_inc(exp_done, 1)

        def copy_probs(t):
            done(act, pT_done, t)
            reused(act, pv_done, t)
            nc.scalar.activation(pT[t.par][:, :], AT["probs"][:, :], ACT.Identity).then_inc(pT_copied, 1)

        def copy_x(t):
            done(act, xT_done, t)
            reused(act, q_done, t)
            reused(act, k_done, t)
            reused(act, v_done, t)
            nc.scalar.activation(xT[t.par][:, :, :, :],
                                 over(AT["x"][:, 0:P].rearrange("p (s l) -> p s l", s=2), 2, 2, [P, 2, 2, IMAGES]),
                                 ACT.Identity).then_inc(xT_copied, 1)

        def queries(out, bias, used, now):
            def stage(t):
                done(act, q_done, t)
                if isinstance(t.n, int) and t.n == 0:
                    act.wait_ge(biases_made, 2)
                reused(act, used, t)
                nc.scalar.activation(out[t.par][:, :], AT["q"][:, 0:P], ACT.Identity, scale=SCALE, bias=bias[:, 0:1])\
                  .then_inc(now, 1)
            return stage

        def copy_keys(t):
            done(act, k_done, t)
            reused(act, kb_made, t)
            nc.scalar.activation(kS0[t.par][:, :], AT["k"][:, 0:P], ACT.Identity, bias=col("bk0")).then_inc(k_copied, 1)

        def copy_o(t):
            done(act, oT_done, t)
            reused(act, proj_done, t)
            nc.scalar.activation(oT[t.par][:, :], AT["o"][:, 0:P], ACT.Identity, bias=col("bv0")).then_inc(oT_copied, 1)

        pipeline(act, [(exponentials, 3), (copy_x, 0), (copy_keys, 1), (keep_positions, 1), (copy_o, 4),
                       (copy_probs, 3), (queries(qv, bias_v, bd_done, qv_copied), 0),
                       (queries(qu, bias_u, ac_done, qu_copied), 0)], TILES, *LOOP)

    @block.gpsimd
    def _(pool):
        nc.gpsimd.memset(half_pow[:, :], -0.5).then_inc(half_pow_set, 1)
        for p in range(2):
            nc.gpsimd.memset(vv[p][:, :, :, :], 0.0).then_inc(ones_set, 1)
        pool.wait_ge(half_pow_set, 1)

        def root(t):
            pool.wait_ge(ve_done, t.n + 1)
            after(pool, xn_done, t.n - 1)
            nc.gpsimd.tensor_tensor(rstd[t.par][:, :], ve[t.par][:, :], half_pow[:, :], ALU.pow).then_inc(rstd_done, 1)

        def root2(t):
            pool.wait_ge(ve2_done, t.n + 1)
            after(pool, nrm_done, t.n - 1)
            nc.gpsimd.tensor_tensor(rstd2[t.par][:, :], ve2[t.par][:, :], half_pow[:, :], ALU.pow)\
              .then_inc(rstd2_done, 1)

        def keys(t):
            if isinstance(t.n, int) and t.n == 2:
                pool.dma_start(w1[:, :], weights1).then_inc(weights1_in, 16)
                pool.dma_start(hs_dram[TOKENS:GROUPS * G, :], zeros[0:GROUPS * G - TOKENS, :]).then_inc(pads_zero, 16)
            done(pool, k_copied, t)
            reused(pool, ac_done, t)
            nc.gpsimd.tensor_tensor(kb[t.par][:, :, :], over(kS0[t.par][:, :], 1, HEADS, [P, HEADS, P]),
                                    over(W("head_mask"), 2, P, [P, HEADS, P]), ALU.mult).then_inc(kb_made, 1)

        pipeline(pool, [(root, 0), (keys, 2), (root2, 5)], TILES, *LOOP)

    @block.vector
    def _(dve):
        dve.wait_ge(weights_in, 48)
        dve.wait_ge(ones_set, 2)
        for p in range(2):
            for s in range(2):
                nc.vector.tensor_copy(vv[p][:, s, :, HD:HD + 1].rearrange("p h o -> p (h o)"), W("half_mask"))\
                  .then_inc(ones_set, 1)
        for bias, name in ((bias_u, "u"), (bias_v, "v")):
            nc.vector.tensor_scalar(bias[:, :], col("bq0"), col(name), SCALE, ALU.add, ALU.mult).then_inc(biases_made, 1)

        def embedded(t):
            after(dve, xn_done, t.n - 1)
            dve.wait_ge(tok_done, t.n + 1)
            nc.vector.tensor_tensor(h0[:, t.n, :], AT["embed"][:, 0:P], row("tok_b"), ALU.add).then_inc(h_ready, 1)
            dve.drain()
            nc.vector.bn_stats(stats[t.par][:, :], h0[:, t.n, :])
            dve.drain()
            nc.vector.bn_aggr(mv[t.par][:, :], stats[t.par][:, :]).then_inc(mv_done, 1)
            dve.wait_ge(mv_done, t.n + 1)
            after(dve, rstd_done, t.n - 1)
            nc.vector.tensor_scalar(ve[t.par][:, :], mv[t.par][:, 1:2], EPS, None, ALU.add).then_inc(ve_done, 1)

        def normalise(t):
            dve.wait_ge(rstd_done, t.n + 1)
            after(dve, xT_done, t.n - 1)
            nc.vector.tensor_scalar(xn[t.par][:, :], h0[:, t.n, :], mv[t.par][:, 0:1], rstd[t.par][:, 0:1],
                                    ALU.subtract, ALU.mult).then_inc(xn_done, 1)
            if isinstance(t.n, int) and t.n == 0:
                dve.wait_ge(pos_projected, 2)
                nc.vector.tensor_tensor(pb[:, :, :], over(pos_p[:, :], 1, HEADS, [P, HEADS, REL]),
                                        over(W("head_mask"), 2, REL, [P, HEADS, REL]), ALU.mult).then_inc(pos_ready, 1)

        def normalise2(t):
            done(dve, rstd2_done, t)
            reused(dve, h2_ready, t)
            nc.vector.tensor_scalar(nrm[t.par][:, :], h0[:, t.n, :], mv2[t.par][:, 0:1], rstd2[t.par][:, 0:1],
                                    ALU.subtract, ALU.mult).then_inc(nrm_done, 1)

        def second_residual(t):
            done(dve, nrm_done, t)
            after(dve, stored[t.par], 32 * t.half)
            nc.vector.tensor_tensor(h2[t.par][:, :], h0[:, t.n, :], nrm[t.par][:, :], ALU.add).then_inc(h2_ready, 1)

        o = AT["attend"][:, 0:HEADS * (HD + 1)].rearrange("p (h d) -> p h d", h=HEADS)

        def reciprocals(t):
            done(dve, pv_done, t)
            nc.vector.reciprocal(rs[t.par][:, :], o[:, :, HD]).then_inc(sums_inverted, 1)

        def divide(t):
            done(dve, sums_inverted, t)
            reused(dve, oT_done, t)
            nc.vector.tensor_tensor(on[t.par][:, :, :], o[:, :, 0:HD], over(rs[t.par][:, :], 2, HD, [P, HEADS, HD]),
                                    ALU.mult).then_inc(attn_normal, 1)

        def values(t):
            done(dve, v_done, t)
            reused(dve, pv_done, t)
            shape = [P, 2, HEADS, HD]
            v = AT["v"][:, 0:2 * P].rearrange("p (s h d) -> p s h d", s=2, h=HEADS)
            mask = W("half_mask").unsqueeze(1).unsqueeze(3).broadcast_to(shape)
            nc.vector.tensor_tensor(vv[t.par][:, :, :, 0:HD], v, mask, ALU.mult).then_inc(vv_made, 1)

        def scores(t):
            dve.wait_ge(bd_back[t.par], 32 * (t.half + 1))
            done(dve, ac_done, t)
            reused(dve, exp_done, t)
            nc.vector.tensor_tensor(s1[t.par][:, :, :].rearrange("p h j -> p (h j)"), AT["content"][:, :],
                                    bs[t.par][:, :], ALU.add).then_inc(scores_added, 1)

        def maxima(t):
            done(dve, scores_added, t)
            nc.vector.tensor_reduce(less[t.par][:, :], s1[t.par][:, :, :], X, ALU.max, negate=True)\
              .then_inc(max_found, 1)

        def bias_out(t):
            done(dve, proj_done, t)
            nc.vector.tensor_tensor(att[t.par][:, :], AT["out"][:, 0:P], row("out_b"), ALU.add).then_inc(att_biased, 1)

        def first_residual(t):
            done(dve, att_biased, t)
            reused(dve, nrm_done, t)
            nc.vector.tensor_tensor(h0[:, t.n, :], h0[:, t.n, :], att[t.par][:, :], ALU.add)
            dve.drain()
            nc.vector.bn_stats(st2[t.par][:, :], h0[:, t.n, :])
            dve.drain()
            nc.vector.bn_aggr(mv2[t.par][:, :], st2[t.par][:, :]).then_inc(mv2_done, 1)
            dve.wait_ge(mv2_done, t.n + 1)
            after(dve, rstd2_done, t.n - 1)
            nc.vector.tensor_scalar(ve2[t.par][:, :], mv2[t.par][:, 1:2], EPS, None, ALU.add).then_inc(ve2_done, 1)

        pipeline(dve, [(maxima, 4), (first_residual, 6), (reciprocals, 5), (divide, 5), (normalise2, 6), (values, 3),
                       (embedded, 0), (second_residual, 6), (scores, 3), (normalise, 0),
                       (bias_out, 5)], TILES, *LOOP)


def block1(nc, ctx, sem, banks, V, col, row, Wident, w_head_mask, sent, h_all, xb_all, n_all, lg_all, hs_dram, stored,
           pads_zero, weights1_in, kept, loads, experts_in, sorted_dram, slots_empty, empty):
    def sb(name, shape, dt=F32):
        return ctx.enter_context(nc.sbuf_tensor(name, shape, dt))

    def pair(name, shape, dt=F32):
        return [sb(f"{name}{i}", shape, dt) for i in range(2)]

    U0, U1, MM, WD, S, T = banks
    HALF = HEADS // 2

    member = sb("member", [IMG_G, G], BF16)
    apart = sb("apart", [IMG_G, HALF * G], BF16)
    half_col = sb("half_col", [P, 1])
    pow_col = sb("pow_col", [P, 1])
    half_bias = sb("half_bias", [P, 4])
    bq_scaled = sb("bq_scaled", [P, 1])
    stats0, mv0, ve0, rstd0 = pair("stats0", [G, 6]), pair("mv0", [G, 2]), pair("ve0", [G, 1]), pair("rstd0", [G, 1])
    stats4, mv4, ve4, rstd4 = pair("stats4", [G, 6]), pair("mv4", [G, 2]), pair("ve4", [G, 1]), pair("rstd4", [G, 1])
    stats5, mv5, ve5, rstd5 = pair("stats5", [G, 6]), pair("mv5", [G, 2]), pair("ve5", [G, 1]), pair("rstd5", [G, 1])
    x0 = pair("x0", [G, P])
    x0T = pair("x0T", [P, G])
    relu1, gate1, x1T = pair("relu1", [P, G]), pair("gate1", [P, G]), pair("x1T", [P, G])
    relu2, gate2, x2T = pair("relu2", [P, G]), pair("gate2", [P, G]), pair("x2T", [P, G])
    mix1, mix2 = pair("mix1", [P, G]), pair("mix2", [P, G])
    mixb1, mixb2 = sb("mixb1", [P, G]), sb("mixb2", [P, G])
    aT = pair("aT", [P, G])
    x2 = pair("x2", [G, P])
    gm, gneg = pair("gm", [G, G]), pair("gneg", [G, 1])
    ge, gp = pair("ge", [G, G]), pair("gp", [G, G])
    gx, gsum, grec = sb("gx", [G, G]), sb("gsum", [G, 1]), sb("grec", [G, 1])
    gpT = pair("gpT", [G, G])
    attT = pair("attT", [P, G])
    tr, tz, zs, yT = pair("tr", [P, G]), pair("tz", [P, G]), pair("zs", [P, G]), pair("yT", [P, G])
    rx = sb("rx", [P, G])
    x4 = pair("x4", [G, P])
    x4T = pair("x4T", [P, G])
    qT = pair("qT", [P, G])
    kS = pair("kS", [P, G])
    kb = pair("kb_", [P, HEADS, G])
    xb = pair("xb", [G, P])
    v17 = pair("v17", [G, HEADS, HD + 1])
    less = pair("less_", [G, HEADS])
    ex = pair("ex_", [G, HEADS, G])
    pT = pair("pT_", [G, HEADS, G])
    rs = pair("rs_", [G, HEADS])
    on = pair("on_", [G, HEADS, HD])
    oT = pair("oT_", [P, G])
    y5 = pair("y5", [G, P])
    nb = pair("nb", [G, P])
    tT = pair("tT", [P, G])

    names = ("consts halves x0_done x0T_done x0T_copied hw1_done gate1_done mix1_done mixb1_done x1_done hw2_done "
             "gate2_done mix2_done mixb2_done x2_done aT_done x2t_done x2_copied gram_done gm_done "
             "gneg_done ge_done gx_done grec_done gp_done gpT_done gpT_copied att_done att_copied rz_done "
             "tr_done tz_done rz_copied rx_done yT_done y_done h3_done mv0_done ve0_done rstd0_done mv4_done ve4_done "
             "rstd4_done mv5_done ve5_done rstd5_done x4_done xb_done x4T_done x4T_copied q_done_ q_copied k_done k_copied "
             "kb_done v_done v_copied s_done less_done ex_done pT_done_ pT_copied_ pv_done_ rs_done on_done "
             "oT_done_ oT_copied_ wo_done y5_done nb_done nT_done tT_copied logits_done logits_kept").split()
    s = {n: sem(n) for n in names}
    loaded = sem("loaded")
    xb_kept = [sem("xb_kept_even"), sem("xb_kept_odd")]
    LOOP = (5, GROUPS // 2)
    USERS = {
        "U0": [("gp", 2, "gpT_copied"), ("k", 3, "k_copied"), ("logits", 7, "logits_kept"), ("v", 4, "v_copied")],
        "U1": [("highway1", 1, "gate1_done"), ("x4", 3, "x4T_copied"), ("n", 7, "tT_copied"), ("gram", 1, "gm_done"),
               ("q", 3, "q_copied")],
        "MM": [("x2", 2, "x2_copied"), ("highway2", 1, "gate2_done"), ("pv", 5, "on_done"), ("y", 2, "h3_done"),
               ("o", 5, "oT_copied_")],
        "WD": [("out", 6, "y5_done"), ("gather", 2, "att_copied"), ("gates", 2, "rz_copied"),
               ("x0", 0, "x0T_copied")],
        "S": [("s", 4, "ex_done")],
        "T": [("probs", 4, "pT_copied_")],
    }
    AT = {user: bank for name, bank in (("U0", U0), ("U1", U1), ("MM", MM), ("WD", WD)) for user, _, _ in USERS[name]}

    def done(eng, name, t):
        eng.wait_ge(s[name], t.n + 1)

    def reused(eng, name, t):
        after(eng, s[name], t.n - 1)

    def bank_read(eng, user, t):
        last_read(eng, {name: [(u, lag, s[read]) for u, lag, read in us] for name, us in USERS.items()}, user, t, GROUPS)

    block = ctx.enter_context(nc.Block())

    @block.sync
    def _(sp):
        sp.wait_ge(pads_zero, 16)
        for q in stored:
            sp.wait_ge(q, 16 * TILES)
        rows = hs_dram.rearrange("(g p) e -> p g e", p=G)
        sp.dma_start(h_all[:, 0:2, :], rows[:, 0:2, :]).then_inc(loaded, 16)
        sp.wait_ge(loaded, 16)
        sp.dma_start(h_all[:, 2:GROUPS, :], rows[:, 2:GROUPS, :]).then_inc(loaded, 16)

        sp.dma_start(sorted_dram, empty).then_inc(slots_empty, 16)
        for there, here in loads:
            sp.dma_start(there[:, :], here).then_inc(experts_in, 16)

        def keep(t):
            done(sp, "nb_done", t)
            sp.dma_start(n_all[:, t.n, :], nb[t.par][:, :]).then_inc(kept[t.par], 16)

        def keep_xb(t):
            done(sp, "xb_done", t)
            sp.dma_start(xb_all[:, t.n, :], xb[t.par][:, :]).then_inc(xb_kept[t.par], 16)

        pipeline(sp, [
            (keep_xb, 2), (keep, 5)],
            GROUPS, *LOOP)
        for q in kept:
            sp.wait_ge(q, 16 * GROUPS // 2)

    @block.gpsimd
    def _(pool):
        nc.gpsimd.memset(half_col[:, :], 0.5).then_inc(s["consts"], 1)
        nc.gpsimd.memset(pow_col[:, :], -0.5).then_inc(s["consts"], 1)
        nc.gpsimd.memset(v17[0][:, :, :], 1.0).then_inc(s["consts"], 1)
        nc.gpsimd.memset(v17[1][:, :, :], 1.0).then_inc(s["consts"], 1)
        pool.wait_ge(s["consts"], 4)

        def root(k, ve, rstd, used):
            def stage(t):
                done(pool, f"ve{k}_done", t)
                reused(pool, used, t)
                nc.gpsimd.tensor_tensor(rstd[t.par][:, :], ve[t.par][:, :], pow_col[0:G, :], ALU.pow)\
                  .then_inc(s[f"rstd{k}_done"], 1)
            return stage

        def differ(k, relu, x, mix, used):
            def stage(t):
                done(pool, f"gate{k}_done", t)
                reused(pool, used, t)
                nc.gpsimd.tensor_tensor(mix[t.par][:, :], relu[t.par][:, :], x[t.par][:, :], ALU.subtract)\
                  .then_inc(s[f"mix{k}_done"], 1)
            return stage

        def keys(t):
            done(pool, "k_copied", t)
            reused(pool, "s_done", t)
            nc.gpsimd.tensor_tensor(kb[t.par][:, :, :], over(kS[t.par][:, :], 1, HEADS, [P, HEADS, G]),
                                    over(w_head_mask, 2, G, [P, HEADS, G]), ALU.mult).then_inc(s["kb_done"], 1)

        def add_bo(t):
            done(pool, "x4_done", t)
            after(pool, xb_kept[t.par], 16 * t.half)
            nc.gpsimd.tensor_tensor(xb[t.par][:, :], x4[t.par][:, :], row("bo", G), ALU.add).then_inc(s["xb_done"], 1)

        pipeline(pool, [
            (differ(2, relu2, x1T, mix2, "x2_done"), 3), (keys, 5), (root(5, ve5, rstd5, "nb_done"), 8),
            (root(4, ve4, rstd4, "x4_done"), 4), (differ(1, relu1, x0T, mix1, "x1_done"), 2), (add_bo, 5),
            (root(0, ve0, rstd0, "x0_done"), 0)],
            GROUPS, *LOOP)
    @block.tensor
    def _(pe):
        pe.wait_ge(weights1_in, 16)
        pe.wait_ge(s["consts"], 6)

        def highway(k, xin, x_name):
            def stage(t):
                done(pe, x_name, t)
                bank_read(pe, f"highway{k + 1}", t)
                at = AT[f"highway{k + 1}"]
                nc.tensor.matmul(at[:, 0:G], V("tW", k * P, (k + 1) * P), xin[t.par][:, :], start=True, stop=True)
                nc.tensor.matmul(at[:, G:2 * G], V("cW", k * P, (k + 1) * P), xin[t.par][:, :], start=True, stop=True)\
                  .then_inc(s[f"hw{k + 1}_done"], 1)
            return stage

        def gather(t):
            done(pe, "gpT_copied", t)
            done(pe, "x2_copied", t)
            bank_read(pe, "gather", t)
            nc.tensor.matmul(AT["gather"][:, 0:G], x2[t.par][:, :], gpT[t.par][:, :], start=True, stop=True)\
              .then_inc(s["att_done"], 1)

        def turn_probs(t):
            done(pe, "ex_done", t)
            bank_read(pe, "probs", t)
            for h in range(HEADS):
                mm = nc.tensor.transpose(T[0:G, h // HALF, (h % HALF) * G:(h % HALF + 1) * G],
                                         ex[t.par][:, h, :], Wident[0:G, 0:G])
            mm.then_inc(s["pT_done_"], 1)

        def gates(t):
            done(pe, "att_copied", t)
            bank_read(pe, "gates", t)
            for j, name in enumerate(("fr", "ff")):
                out = AT["gates"][:, j * G:(j + 1) * G]
                nc.tensor.matmul(out, V(name, 0, P), x0T[t.par][:, :], start=True, stop=False)
                mm = nc.tensor.matmul(out, V(name, P, 2 * P), attT[t.par][:, :], start=False, stop=True)
            mm.then_inc(s["rz_done"], 1)

        def turn(user, src, ready, now, rows_=G):
            def stage(t):
                done(pe, ready, t)
                bank_read(pe, user, t)
                nc.tensor.transpose(AT[user][0:P + G - rows_, 0:rows_], src[t.par][:, :],
                                    Wident[0:rows_, 0:rows_]).then_inc(s[now], 1)
            return stage

        def turn_gp(t):
            done(pe, "gp_done", t)
            bank_read(pe, "gp", t)
            nc.tensor.transpose(AT["gp"][0:G, 0:G], gp[t.par][:, :], Wident[0:G, 0:G]).then_inc(s["gpT_done"], 1)

        def turn_o(t):
            done(pe, "on_done", t)
            bank_read(pe, "o", t)
            nc.tensor.transpose(AT["o"][:, 0:G], on[t.par][:, :, :].rearrange("p h d -> p (h d)"), Wident[0:G, 0:G])\
              .then_inc(s["oT_done_"], 1)

        def logits(t):
            done(pe, "tT_copied", t)
            bank_read(pe, "logits", t)
            nc.tensor.matmul(AT["logits"][0:G, 0:EXPERTS], tT[t.par][:, :], V("gate"), start=True, stop=True)\
              .then_inc(s["logits_done"], 1)

        def attend(t):
            done(pe, "pT_copied_", t)
            done(pe, "v_copied", t)
            bank_read(pe, "pv", t)
            for h in range(HEADS):
                mm = nc.tensor.matmul(T[0:G, 0, h * (HD + 1):(h + 1) * (HD + 1)], pT[t.par][:, h, :],
                                      v17[t.par][:, h, :], start=True, stop=True)
            mm.then_inc(s["pv_done_"], 1)

        def gram(t):
            done(pe, "aT_done", t)
            bank_read(pe, "gram", t)
            out = AT["gram"][0:G, 0:G]
            nc.tensor.matmul(out, member[:, :], apart[:, 0:G], start=True, stop=False)
            nc.tensor.matmul(out, x2T[t.par][:, :], col("a1").broadcast_to([P, G]), start=False, stop=False)
            nc.tensor.matmul(out, aT[t.par][:, :], x2T[t.par][:, :], start=False, stop=True)\
              .then_inc(s["gram_done"], 1)

        def scores(b):
            def stage(t):
                if b == 0:
                    done(pe, "q_copied", t)
                    done(pe, "kb_done", t)
                    bank_read(pe, "s", t)
                nc.tensor.matmul(S[0:G, b, 0:HALF * G], member[:, :], apart[:, :], start=True, stop=False)
                mm = nc.tensor.matmul(S[0:G, b, 0:HALF * G], qT[t.par][:, :],
                                      kb[t.par][:, b * HALF:(b + 1) * HALF, :].rearrange("p h j -> p (h j)"),
                                      start=False, stop=True)
                if b == 1:
                    mm.then_inc(s["s_done"], 1)
            return stage

        def project(user, lhsT, weights, ready, now):
            def stage(t):
                done(pe, ready, t)
                bank_read(pe, user, t)
                nc.tensor.matmul(AT[user][0:G, 0:P], lhsT[t.par][:, :], V(weights), start=True, stop=True)\
                  .then_inc(s[now], 1)
            return stage

        def project_turned(user, weights, now):
            def stage(t):
                done(pe, "x4T_copied", t)
                bank_read(pe, user, t)
                nc.tensor.matmul(AT[user][:, 0:G], V(weights), x4T[t.par][:, :], start=True, stop=True)\
                  .then_inc(s[now], 1)
            return stage

        pipeline(pe, [
            (highway(0, x0T, "x0T_copied"), 1), (turn("x2", x2T, "x2_done", "x2t_done", P), 2),
            (project("out", oT, "Wo", "oT_copied_", "wo_done"), 6), (turn_gp, 2), (scores(0), 4),
            (turn("x4", x4, "x4_done", "x4T_done"), 3), (gather, 2), (scores(1), 4), (highway(1, x1T, "x1_done"), 1),
            (project_turned("k", "Wk", "k_done"), 3), (turn("n", nb, "nb_done", "nT_done"), 7), (gates, 2),
            (attend, 5), (gram, 1), (logits, 7), (turn("x0", x0, "x0_done", "x0T_done"), 0),
            (turn("y", yT, "yT_done", "y_done", P), 2), (project_turned("q", "Wq", "q_done_"), 3),
            (project("v", x4T, "Wv", "x4T_copied", "v_done"), 4), (turn_o, 5), (turn_probs, 4)],
            GROUPS, *LOOP)
    @block.scalar
    def _(act):
        act.wait_ge(s["halves"], 6)
        act.wait_ge(s["consts"], 6)

        def exponentials(t):
            done(act, "less_done", t)
            reused(act, "pT_done_", t)
            for h in range(HEADS):
                e = nc.scalar.activation(ex[t.par][:, h, :], S[0:G, h // HALF, (h % HALF) * G:(h % HALF + 1) * G],
                                         ACT.Exp, bias=less[t.par][:, h:h + 1])
            e.then_inc(s["ex_done"], 1)

        def highway(k, relu, gate, used):
            def stage(t):
                done(act, f"hw{k + 1}_done", t)
                reused(act, used, t)
                at = AT[f"highway{k + 1}"]
                nc.scalar.activation(relu[t.par][:, :], at[:, 0:G], ACT.Relu, bias=col(f"tb{k}"))
                nc.scalar.activation(gate[t.par][:, :], at[:, G:2 * G], ACT.Tanh, scale=0.5,
                                     bias=half_bias[:, k:k + 1]).then_inc(s[f"gate{k + 1}_done"], 1)
            return stage

        def copy(out, src, ready, used, now, **how):
            def stage(t):
                done(act, ready, t)
                reused(act, used, t)
                nc.scalar.activation(out[t.par][:, :], src, ACT.Identity, **how).then_inc(s[now], 1)
            return stage

        def copy_probs(t):
            done(act, "pT_done_", t)
            reused(act, "pv_done_", t)
            nc.scalar.activation(pT[t.par][:, :, :].rearrange("p (b h) j -> p b (h j)", b=2), T[0:G, :, 0:HALF * G],
                                 ACT.Identity).then_inc(s["pT_copied_"], 1)

        def gates(t):
            done(act, "rz_done", t)
            reused(act, "yT_done", t)
            nc.scalar.activation(tr[t.par][:, :], AT["gates"][:, 0:G], ACT.Tanh, scale=0.5, bias=half_bias[:, 2:3])\
              .then_inc(s["tr_done"], 1)
            nc.scalar.activation(tz[t.par][:, :], AT["gates"][:, G:2 * G], ACT.Tanh, scale=0.5, bias=half_bias[:, 3:4])\
              .then_inc(s["rz_copied"], 1)
            done(act, "rz_copied", t)
            nc.scalar.activation(zs[t.par][:, :], tz[t.par][:, :], ACT.Square, scale=0.5, bias=half_col[:, 0:1])\
              .then_inc(s["tz_done"], 1)

        def gate_exp(t):
            done(act, "gneg_done", t)
            reused(act, "gx_done", t)
            nc.scalar.activation(ge[t.par][:, :], gm[t.par][:, :], ACT.Exp, bias=gneg[t.par][:, 0:1])\
              .then_inc(s["ge_done"], 1)

        def values(t):
            done(act, "v_done", t)
            reused(act, "pv_done_", t)
            nc.scalar.activation(v17[t.par][:, :, 0:HD], AT["v"][0:G, 0:P].rearrange("p (h d) -> p h d", h=HEADS),
                                 ACT.Identity).then_inc(s["v_copied"], 1)

        pipeline(act, [
            (copy(kS, AT["k"][:, 0:G], "k_done", "kb_done", "k_copied", bias=col("bk1")), 3), (gates, 2),
            (exponentials, 4), (copy(x0T, AT["x0"][:, 0:G], "x0T_done", "yT_done", "x0T_copied"), 0), (gate_exp, 1),
            (copy(qT, AT["q"][:, 0:G], "q_done_", "s_done", "q_copied", scale=SCALE, bias=bq_scaled[:, 0:1]), 3),
            (values, 4), (copy(oT, AT["o"][:, 0:G], "oT_done_", "wo_done", "oT_copied_", bias=col("bv1")), 5),
            (highway(0, relu1, gate1, "x1_done"), 0),
            (copy(x2, AT["x2"][0:G, 0:P], "x2t_done", "att_done", "x2_copied"), 1),
            (copy(gpT, AT["gp"][0:G, 0:G], "gpT_done", "att_done", "gpT_copied"), 1), (copy_probs, 4),
            (copy(x4T, AT["x4"][:, 0:G], "x4T_done", "v_done", "x4T_copied"), 2),
            (copy(attT, AT["gather"][:, 0:G], "att_done", "rz_done", "att_copied"), 1),
            (highway(1, relu2, gate2, "x2_done"), 0),
            (copy(tT, AT["n"][:, 0:G], "nT_done", "logits_done", "tT_copied", scale=col("g"), bias=col("b")), 6)],
            GROUPS, *LOOP)
    @block.vector
    def _(dve):
        dve.wait_ge(weights1_in, 16)
        for i, name in enumerate(("cb0", "cb1", "frb", "ffb")):
            nc.vector.tensor_scalar(half_bias[:, i:i + 1], col(name), 0.5, None, ALU.mult).then_inc(s["halves"], 1)
        nc.vector.tensor_copy(member[:, :], V("member", rows_=IMG_G)).then_inc(s["consts"], 1)
        nc.vector.tensor_copy(apart[:, :], V("apart", rows_=IMG_G)).then_inc(s["consts"], 1)
        nc.vector.tensor_copy(sent[:, :, AT_TOKEN], V("token", rows_=G)).then_inc(s["halves"], 1)
        nc.vector.tensor_scalar(bq_scaled[:, :], col("bq1"), SCALE, None, ALU.mult).then_inc(s["halves"], 1)
        dve.wait_ge(s["consts"], 6)

        def moments(k, src, stats, mv, ve):
            def run(t):
                dve.drain()
                nc.vector.bn_stats(stats[t.par][:, :], src)
                dve.drain()
                nc.vector.bn_aggr(mv[t.par][:, :], stats[t.par][:, :]).then_inc(s[f"mv{k}_done"], 1)
                done(dve, f"mv{k}_done", t)
                reused(dve, f"rstd{k}_done", t)
                nc.vector.tensor_scalar(ve[t.par][:, :], mv[t.par][:, 1:2], EPS, None, ALU.add)\
                  .then_inc(s[f"ve{k}_done"], 1)
            return run

        def scale(out, src, k, mv, rstd, used, now):
            def stage(t):
                done(dve, f"rstd{k}_done", t)
                reused(dve, used, t)
                nc.vector.tensor_scalar(out[t.par][:, :], src(t), mv[t.par][:, 0:1], rstd[t.par][:, 0:1],
                                        ALU.subtract, ALU.mult).then_inc(s[now], 1)
            return stage

        def norm5(t):
            reused(dve, "nT_done", t)
            after(dve, kept[t.par], 16 * t.half)
            scale(nb, lambda t: y5[t.par][:, :], 5, mv5, rstd5, "nT_done", "nb_done")(t)

        def blend(k, mix, gate, mixb):
            def stage(t):
                done(dve, f"gate{k}_done", t)
                done(dve, f"mix{k}_done", t)
                after(dve, s[f"x{k}_done"], t.n)
                nc.vector.scalar_tensor_tensor(out=mixb[:, :], in0=gate[t.par][:, :], scalar=1.0, in1=mix[t.par][:, :],
                                               op0=ALU.add, op1=ALU.mult).then_inc(s[f"mixb{k}_done"], 1)
            return stage

        def highway(k, x, mixb, out, *used):
            def stage(t):
                done(dve, f"mixb{k}_done", t)
                for name in used:
                    reused(dve, name, t)
                nc.vector.scalar_tensor_tensor(out=out[t.par][:, :], in0=mixb[:, :], scalar=0.5, in1=x[t.par][:, :],
                                               op0=ALU.mult, op1=ALU.add).then_inc(s[f"x{k}_done"], 1)
            return stage

        def weigh(t):
            done(dve, "x2_done", t)
            reused(dve, "gram_done", t)
            nc.vector.tensor_scalar(aT[t.par][:, :], x2T[t.par][:, :], col("a3"), col("a2"), ALU.mult, ALU.add)\
              .then_inc(s["aT_done"], 1)

        def first_moments(t):
            dve.wait_ge(loaded, 16)
            if not isinstance(t.n, int) or t.n >= 2:
                dve.wait_ge(loaded, 32)
            moments(0, h_all[:, t.n, :], stats0, mv0, ve0)(t)

        def first_part(t):
            done(dve, "tz_done", t)
            after(dve, s["yT_done"], t.n)
            nc.vector.scalar_tensor_tensor(out=rx[:, :], in0=tr[t.par][:, :], scalar=1.0, in1=x0T[t.par][:, :],
                                           op0=ALU.add, op1=ALU.mult).then_inc(s["rx_done"], 1)

        def mix(t):
            done(dve, "rx_done", t)
            reused(dve, "y_done", t)
            nc.vector.scalar_tensor_tensor(out=yT[t.par][:, :], in0=rx[:, :], scalar=0.5, in1=zs[t.par][:, :],
                                           op0=ALU.mult, op1=ALU.add).then_inc(s["yT_done"], 1)

        def keep_logits(t):
            done(dve, "logits_done", t)
            nc.vector.tensor_tensor(lg_all[:, t.n, :], AT["logits"][0:G, 0:EXPERTS], row("gate_b", G), ALU.add)\
              .then_inc(s["logits_kept"], 1)

        o = T[0:G, 0, 0:HEADS * (HD + 1)].rearrange("p (h d) -> p h d", h=HEADS)

        def reciprocals(t):
            done(dve, "pv_done_", t)
            nc.vector.reciprocal(rs[t.par][:, :], o[:, :, HD]).then_inc(s["rs_done"], 1)

        def divide(t):
            done(dve, "rs_done", t)
            reused(dve, "oT_done_", t)
            nc.vector.tensor_tensor(on[t.par][:, :, :], o[:, :, 0:HD], over(rs[t.par][:, :], 2, HD, [G, HEADS, HD]),
                                    ALU.mult).then_inc(s["on_done"], 1)

        def third_residual(t):
            reused(dve, "x4_done", t)
            done(dve, "y_done", t)
            nc.vector.tensor_tensor(h_all[:, t.n, :], h_all[:, t.n, :], AT["y"][0:G, 0:P], ALU.add)\
              .then_inc(s["h3_done"], 1)
            moments(4, h_all[:, t.n, :], stats4, mv4, ve4)(t)

        def gate_scores(t):
            done(dve, "gram_done", t)
            reused(dve, "ge_done", t)
            nc.vector.tensor_scalar(gm[t.par][:, :], AT["gram"][0:G, 0:G], col("ab", G), 0.0, ALU.add, ALU.max)\
              .then_inc(s["gm_done"], 1)

        def gate_maxima(t):
            done(dve, "gm_done", t)
            nc.vector.tensor_reduce(gneg[t.par][:, :], gm[t.par][:, :], X, ALU.max, negate=True)\
              .then_inc(s["gneg_done"], 1)

        def gate_sums(t):
            done(dve, "ge_done", t)
            after(dve, s["gp_done"], t.n)
            nc.vector.tensor_tensor_reduce(out=gx[:, :], in0=ge[t.par][:, :], in1=V("same", rows_=G), scale=1.0, scalar=0.0,
                                           op0=ALU.mult, op1=ALU.add, accum_out=gsum[:, :]).then_inc(s["gx_done"], 1)

        def gate_reciprocals(t):
            done(dve, "gx_done", t)
            nc.vector.reciprocal(grec[:, :], gsum[:, :]).then_inc(s["grec_done"], 1)

        def gate_probs(t):
            done(dve, "grec_done", t)
            reused(dve, "gpT_done", t)
            nc.vector.tensor_scalar(gp[t.par][:, :], gx[:, :], grec[:, 0:1], None, ALU.mult).then_inc(s["gp_done"], 1)

        def scale4(t):
            reused(dve, "xb_done", t)
            scale(x4, lambda t: h_all[:, t.n, :], 4, mv4, rstd4, "x4T_done", "x4_done")(t)

        def fourth_residual(t):
            done(dve, "wo_done", t)
            reused(dve, "nb_done", t)
            dve.wait_ge(xb_kept[t.par], 16 * (t.half + 1))
            nc.vector.tensor_tensor(y5[t.par][:, :], AT["out"][0:G, 0:P], xb_all[:, t.n, :], ALU.add).then_inc(s["y5_done"], 1)
            moments(5, y5[t.par][:, :], stats5, mv5, ve5)(t)

        def maxima(t):
            done(dve, "s_done", t)
            reused(dve, "ex_done", t)
            nc.vector.tensor_reduce(less[t.par][:, :].rearrange("p (b h) -> p b h", b=2),
                                    S[0:G, :, 0:HALF * G].rearrange("p b (h j) -> p b h j", h=HALF), X, ALU.max,
                                    negate=True).then_inc(s["less_done"], 1)

        pipeline(dve, [
            (gate_sums, 3), (gate_reciprocals, 3), (gate_probs, 3), (norm5, 8), (scale4, 4), (fourth_residual, 7),
            (blend(1, mix1, gate1, mixb1), 2), (highway(1, x0T, mixb1, x1T, "hw2_done"), 2), (first_moments, 0),
            (maxima, 5), (scale(x0, lambda t: h_all[:, t.n, :], 0, mv0, rstd0, "x0T_done", "x0_done"), 0),
            (blend(2, mix2, gate2, mixb2), 2), (highway(2, x1T, mixb2, x2T, "gram_done", "x2t_done"), 2), (weigh, 2),
            (first_part, 3), (mix, 3), (reciprocals, 6), (divide, 6), (gate_scores, 2), (keep_logits, 8),
            (gate_maxima, 2), (third_residual, 3)],
            GROUPS, *LOOP)

def block2(nc, ctx, sem, banks, V, col, Wident, sent, lg_all, W1_sb, W2_sb, b2_sb, experts_in,
           sorted_dram, out, slots_empty, kept):
    def sb(name, shape, dt=F32):
        return ctx.enter_context(nc.sbuf_tensor(name, shape, dt))

    def pair(name, shape, dt=F32):
        return [sb(f"{name}{i}", shape, dt) for i in range(2)]

    NT, YB = banks[0:2], banks[2:4]
    HT = [banks[5][:, p, :] for p in range(2)]
    RB = banks[4][:, 0, :]
    GE = [G, GROUPS, EXPERTS]
    LASTG = TOKENS - (GROUPS - 1) * G

    top = sb("top", [G, GROUPS])
    less = sb("less", GE)
    expo = sb("expo", GE)
    esum = sb("esum", [G, GROUPS])
    table_warm = sb("table_warm", [G, 1])
    cand = sb("cand", GE)
    first = sb("first", [G, GROUPS])
    hot = sb("hot", GE)
    hotv = sb("hotv", GE)
    hotb = sb("hotb", GE, BF16)
    hot_sum, hot_sum_b = sb("hot_sum", [G, EXPERTS]), sb("hot_sum_b", [G, EXPERTS], BF16)
    before_b, ones_b = sb("before_b", [G, G], BF16), sb("ones_b", [G, G], BF16)
    over_t = sb("over_t", [G, EXPERTS, TILES])
    tiles_e = sb("tiles_e", [G, EXPERTS])
    sofar = sb("sofar", [G, EXPERTS, EXPERTS])
    start = sb("start", [G, EXPERTS])
    end = sb("end", [G, EXPERTS])
    slot_e = sb("slot_e", GE)
    slot_h = sb("slot_h", GE)
    slot_f = sb("slot_f", [G, GROUPS])
    slot = sb("slot", [G, GROUPS], I32)
    past = sb("past", [G, SLOT_TILES, EXPERTS])
    owner_f, owner_c = sb("owner_f", [G, SLOT_TILES]), sb("owner_c", [G, SLOT_TILES])
    owner = sb("owner", [G, SLOT_TILES], I32)
    nt = pair("nt", [P, P])
    tT = pair("t2T", [P, P])
    first_w = pair("first_w", [P, FIRST])
    hT = pair("hT", [P, FF])
    ye = pair("ye", [P, P])
    rest = pair("rest", [P, ROW - P])
    to = pair("to", [P, 1], I32)
    res = pair("res", [P, P])

    names = ("routed expo_done hot_ready ranks_done slots_done owners_done "
             "nT_done2 tT_done2 first_ready hid_done hT_ready y_done2 ye_done to_made res_done sending").split()
    s = {n: sem(n) for n in names}
    sorted_in = sem("sorted_in")
    nt_in = [sem("nt_in_even"), sem("nt_in_odd")]
    rest_in = [sem("rest_in_even"), sem("rest_in_odd")]
    out_done = [sem("out_done_even"), sem("out_done_odd")]
    LOOP = (3, (SLOT_TILES - 1) // 2)

    def done(eng, name, t):
        eng.wait_ge(s[name], t.n + 1)

    def reused(eng, name, t):
        after(eng, s[name], t.n - 1)

    block = ctx.enter_context(nc.Block())

    @block.gpsimd
    def _(pool):
        for q in kept:
            pool.wait_ge(q, 16 * GROUPS // 2)
        pool.wait_ge(slots_empty, 16)
        pool.wait_ge(s["slots_done"], 1)
        for g in range(GROUPS):
            rows = G if g < GROUPS - 1 else LASTG
            pool.indirect_dma_start(out=sorted_dram, out_offset=bass.IndirectOffsetOnAxis(ap=slot[0:rows, g:g + 1], axis=0),
                                    in_=sent[0:rows, g, :], in_offset=None).then_inc(sorted_in, 16)

        def send(t):
            done(pool, "res_done", t)
            pool.sem_inc(s["sending"], 1)
            pool.indirect_dma_start(out=out, out_offset=bass.IndirectOffsetOnAxis(ap=to[t.par][:, 0:1], axis=0),
                                    in_=res[t.par][:, :], in_offset=None).then_inc(out_done[t.par], 16)

        pipeline(pool, [(send, 4)], SLOT_TILES, *LOOP)
        for i, q in enumerate(out_done):
            pool.wait_ge(q, 16 * ((SLOT_TILES + 1 - i) // 2))

    @block.sync
    def _(sp):
        sp.wait_ge(sorted_in, 16 * GROUPS)

        in_tiles = sorted_dram.rearrange("(t p) e -> t p e", p=P)

        def load(t):
            reused(sp, "nT_done2", t)
            sp.dma_start(nt[t.par][:, :], in_tiles[t.n, :, 0:P]).then_inc(nt_in[t.par], 16)

        def load_rest(t):
            reused(sp, "res_done", t)
            sp.dma_start(rest[t.par][:, :], in_tiles[t.n, :, P:ROW]).then_inc(rest_in[t.par], 16)

        pipeline(sp, [(load, 0), (load_rest, 3)], SLOT_TILES, *LOOP)

    @block.tensor
    def _(pe):
        pe.wait_ge(s["hot_ready"], 3)
        R = RB[0:G, 0:GROUPS * EXPERTS]
        nc.tensor.matmul(R, before_b[:, :], hotb[:, :, :].rearrange("p g e -> p (g e)"), start=True, stop=False)
        for g in range(GROUPS - 1):
            later = GROUPS - 1 - g
            nc.tensor.matmul(R[:, (g + 1) * EXPERTS:], ones_b[:, :], over(hotb[:, g, :], 1, later, [G, later, EXPERTS]),
                             start=False, stop=(g == GROUPS - 2))
        pe.wait_ge(s["hot_ready"], 4)
        nc.tensor.matmul(RB[0:G, GROUPS * EXPERTS:(GROUPS + 1) * EXPERTS], ones_b[:, :], hot_sum_b[:, :],
                         start=True, stop=True).then_inc(s["ranks_done"], 1)
        pe.wait_ge(s["owners_done"], 1)
        pe.wait_ge(experts_in, 48)

        def turn_n(t):
            pe.wait_ge(nt_in[t.par], 16 * (t.half + 1))
            reused(pe, "tT_done2", t)
            nc.tensor.transpose(NT[t.par][:, 0:P], nt[t.par][:, :], Wident).then_inc(s["nT_done2"], 1)

        def hidden(t):
            done(pe, "tT_done2", t)
            done(pe, "first_ready", t)
            reused(pe, "hT_ready", t)
            for c in range(FC):
                mm = nc.tensor.matmul(HT[t.par][:, c * P:(c + 1) * P], first_w[t.par][:, c * P:(c + 1) * P],
                                      tT[t.par][:, :], start=True, stop=True)
            mm.then_inc(s["hid_done"], 1)

        expert = {}

        def read_expert(t):
            expert[t.par] = pe.value_load(owner[0:1, bass.ds(t.n, 1)], min_val=0, max_val=EXPERTS - 1)

        def expert_out(t):
            e = expert[t.par]
            done(pe, "hT_ready", t)
            reused(pe, "ye_done", t)
            for c in range(FC):
                mm = nc.tensor.matmul(YB[t.par][:, 0:P], hT[t.par][:, c * P:(c + 1) * P],
                                      W2_sb[:, bass.ds(e * FF + c * P, P)], start=(c == 0), stop=(c == FC - 1))
            mm.then_inc(s["y_done2"], 1)

        pipeline(pe, [(turn_n, 1), (hidden, 2), (read_expert, 3), (expert_out, 3)], SLOT_TILES, *LOOP)

    @block.scalar
    def _(act):
        act.wait_ge(s["routed"], 2)
        nc.scalar.activation(expo[:, :, :], less[:, :, :], ACT.Exp).then_inc(s["expo_done"], 1)
        act.wait_ge(s["expo_done"], 1)
        nc.scalar.activation(table_warm[:, :], expo[:, 0, 0:1], ACT.Gelu_apprx_tanh)

        def gain(t):
            done(act, "nT_done2", t)
            reused(act, "hid_done", t)
            nc.scalar.activation(tT[t.par][:, :], NT[t.par][:, 0:P], ACT.Identity, scale=col("g"), bias=col("b"))\
              .then_inc(s["tT_done2"], 1)

        def gelu(t):
            done(act, "hid_done", t)
            reused(act, "y_done2", t)
            for c in range(FC):
                g = nc.scalar.activation(hT[t.par][:, c * P:(c + 1) * P], HT[t.par][:, c * P:(c + 1) * P],
                                         ACT.Gelu_apprx_tanh, bias=first_w[t.par][:, FF + c:FF + c + 1])
            g.then_inc(s["hT_ready"], 1)

        pipeline(act, [(gain, 1), (gelu, 2)], SLOT_TILES, *LOOP)

    @block.vector
    def _(dve):
        k = [0]

        def chain(ins):
            k[0] += 1
            ins.then_inc(s["routed"], 1)
            dve.wait_ge(s["routed"], k[0])

        nc.vector.tensor_copy(before_b[:, :], V("before", rows_=G)).then_inc(s["hot_ready"], 1)
        nc.vector.tensor_copy(ones_b[:, :], V("ones", rows_=G)).then_inc(s["hot_ready"], 1)
        chain(nc.vector.tensor_reduce(top[:, :], lg_all[:, :, :], X, ALU.max))
        chain(nc.vector.tensor_tensor(less[:, :, :], lg_all[:, :, :], over(top[:, :], 2, EXPERTS, GE), ALU.subtract))
        chain(nc.vector.scalar_tensor_tensor(out=cand[:, :, :], in0=less[:, :, :], scalar=0.0,
                                             in1=over(V("rank_w", rows_=G), 1, GROUPS, GE), op0=ALU.is_ge, op1=ALU.mult))
        chain(nc.vector.tensor_reduce(first[:, :], cand[:, :, :], X, ALU.max))
        chain(nc.vector.tensor_tensor(hot[:, :, :], cand[:, :, :], over(first[:, :], 2, EXPERTS, GE), ALU.is_equal))
        nc.vector.tensor_tensor(hotb[:, :, :], hot[:, :, :], over(V("valid", rows_=G), 2, EXPERTS, GE), ALU.mult)\
          .then_inc(s["hot_ready"], 1)
        chain(nc.vector.tensor_tensor(hotv[:, :, :], hot[:, :, :], over(V("valid", rows_=G), 2, EXPERTS, GE), ALU.mult))
        chain(nc.vector.tensor_reduce(hot_sum[:, :], hotv[:, :, :].rearrange("p g e -> p e g"), X, ALU.add))
        nc.vector.tensor_copy(hot_sum_b[:, :], hot_sum[:, :]).then_inc(s["hot_ready"], 1)
        dve.wait_ge(s["expo_done"], 1)
        chain(nc.vector.tensor_reduce(esum[:, :], expo[:, :, :], X, ALU.add))
        chain(nc.vector.reciprocal(sent[:, :, AT_WEIGHT], esum[:, :]))
        dve.wait_ge(s["ranks_done"], 1)
        count = RB[0:G, GROUPS * EXPERTS:(GROUPS + 1) * EXPERTS]
        chain(nc.vector.tensor_tensor(over_t[:, :, :], over(count, 2, TILES, [G, EXPERTS, TILES]),
                                      over(V("tile_lo", rows_=G), 1, EXPERTS, [G, EXPERTS, TILES]), ALU.is_gt))
        chain(nc.vector.tensor_reduce(tiles_e[:, :], over_t[:, :, :], X, ALU.add))
        chain(nc.vector.tensor_tensor(sofar[:, :, :], over(tiles_e[:, :], 1, EXPERTS, [G, EXPERTS, EXPERTS]),
                                      V("lower", rows_=G).rearrange("p (a b) -> p a b", a=EXPERTS), ALU.mult))
        chain(nc.vector.tensor_reduce(start[:, :], sofar[:, :, :], X, ALU.add))
        chain(nc.vector.scalar_tensor_tensor(out=slot_e[:, :, :], in0=over(start[:, :], 1, GROUPS, GE), scalar=float(P),
                                             in1=RB[0:G, 0:GROUPS * EXPERTS].rearrange("p (g e) -> p g e", g=GROUPS),
                                             op0=ALU.mult, op1=ALU.add))
        chain(nc.vector.tensor_tensor(slot_h[:, :, :], slot_e[:, :, :], hotv[:, :, :], ALU.mult))
        chain(nc.vector.tensor_reduce(slot_f[:, :], slot_h[:, :, :], X, ALU.add))
        nc.vector.tensor_copy(slot[:, :], slot_f[:, :]).then_inc(s["slots_done"], 1)
        chain(nc.vector.tensor_tensor(end[:, :], start[:, :], tiles_e[:, :], ALU.add))
        chain(nc.vector.tensor_tensor(past[:, :, :], over(V("tile_no", rows_=G), 2, EXPERTS, [G, SLOT_TILES, EXPERTS]),
                                      over(end[:, :], 1, SLOT_TILES, [G, SLOT_TILES, EXPERTS]), ALU.is_ge))
        chain(nc.vector.tensor_reduce(owner_f[:, :], past[:, :, :], X, ALU.add))
        chain(nc.vector.tensor_scalar(owner_c[:, :], owner_f[:, :], float(EXPERTS - 1), None, ALU.min))
        nc.vector.tensor_copy(owner[:, :], owner_c[:, :]).then_inc(s["owners_done"], 1)
        dve.wait_ge(s["owners_done"], 1)
        dve.wait_ge(experts_in, 48)

        expert_first = [dve.alloc_register(f"expert_first{i}") for i in range(2)]
        expert_last = [dve.alloc_register(f"expert_last{i}") for i in range(2)]

        def read_expert(t):
            dve.reg_load(expert_first[t.par], owner[0:1, bass.ds(t.n, 1)])

        def hand_over_expert(t):
            dve.reg_mov(expert_last[t.par], expert_first[t.par])

        def fetch(t):
            e = dve.snap(expert_first[t.par], min_val=0, max_val=EXPERTS - 1)
            reused(dve, "hT_ready", t)
            nc.vector.tensor_copy(first_w[t.par][:, :], W1_sb[:, bass.ds(e * FIRST, FIRST)]).then_inc(s["first_ready"], 1)

        def bias2(t):
            e = dve.snap(expert_last[t.par], min_val=0, max_val=EXPERTS - 1)
            done(dve, "y_done2", t)
            nc.vector.tensor_tensor(ye[t.par][:, :], YB[t.par][:, 0:P], b2_sb[:, bass.ds(e * P, P)], ALU.add)\
              .then_inc(s["ye_done"], 1)

        def destinations(t):
            dve.wait_ge(rest_in[t.par], 16 * (t.half + 1))
            after(dve, out_done[t.par], 16 * t.half)
            nc.vector.tensor_copy(to[t.par][:, :], rest[t.par][:, AT_TOKEN - P:AT_TOKEN - P + 1])\
              .then_inc(s["to_made"], 1)

        def residual(t):
            done(dve, "ye_done", t)
            nc.vector.scalar_tensor_tensor(out=res[t.par][:, :], in0=ye[t.par][:, :],
                                           scalar=rest[t.par][:, AT_WEIGHT - P:AT_WEIGHT - P + 1],
                                           in1=rest[t.par][:, 0:P], op0=ALU.mult, op1=ALU.add)\
              .then_inc(s["res_done"], 1)

        pipeline(dve, [(fetch, 1), (bias2, 3), (hand_over_expert, 1), (read_expert, 0), (destinations, 3), (residual, 3)],
                 SLOT_TILES, *LOOP)


def layout(x, w):
    f = np.float32
    a = {k: np.asarray(v) for k, v in w.items()}
    x = np.asarray(x)
    pt = x.reshape(IMAGES, 3, 6, 16, 6, 16).transpose(2, 4, 1, 3, 5, 0)
    pt = pt.reshape(TILES, 2, CHUNKS, P, IMAGES).transpose(0, 3, 2, 1, 4).reshape(TILES, P, CHUNKS * P)

    ident = np.eye(P, dtype=f)
    fh = np.arange(P)[:, None] // HD == np.arange(HEADS)[None, :]
    parity = np.arange(P)[:, None] // IMAGES == np.arange(HEADS)[None, :] % 2
    parts = {
        "tok": a["L0_tok_w"].T.reshape(CHUNKS, P, P).transpose(1, 0, 2).reshape(P, CHUNKS * P),
        "in_proj": a["L0_attn_in_proj_w"].T, "out_proj": a["L0_attn_out_proj_w"].T,
        "pos_w": a["L0_attn_pos_w"].T, "pos": a["L0_attn_pos_emb"][0, 0:REL].T,
        "ident": ident, "head_mask": fh.astype(f), "half_mask": parity.astype(f)}
    weights = np.concatenate([parts[n] for n, _ in _WEIGHTS], 1)

    g = np.arange(G)

    def pad(m):
        return np.concatenate([m, np.zeros((P - m.shape[0], m.shape[1]), f)], 0)

    same = (g[:, None] // POSITIONS == g[None, :] // POSITIONS).astype(f)
    member = (np.arange(IMG_G)[:, None] == g[None, :] // POSITIONS).astype(f)
    apart = np.where(member > 0, f(0), f(FAR))
    token = np.arange(GROUPS)[None, :] * G + np.arange(P)[:, None]
    parts = {
        "tW": a["L1_attn_tW"].transpose(1, 0, 2).reshape(P, 2 * P),
        "cW": a["L1_attn_cW"].transpose(1, 0, 2).reshape(P, 2 * P),
        "ff": a["L1_attn_ffW"].reshape(2, P, P).transpose(1, 0, 2).reshape(P, 2 * P),
        "fr": a["L1_attn_frW"].reshape(2, P, P).transpose(1, 0, 2).reshape(P, 2 * P),
        "Wq": a["L1_ffn_Wq"], "Wk": a["L1_ffn_Wk"], "Wv": a["L1_ffn_Wv"], "Wo": a["L1_ffn_Wo"],
        "gate": a["L1_ffn_gate_W"], "same": pad(same),
        "before": pad((g[:, None] < g[None, :]).astype(f)), "ones": np.ones((P, G), f),
        "member": pad(member), "apart": pad(np.tile(apart, (1, 4))),
        "valid": ((token < TOKENS) & (np.arange(P)[:, None] < G)).astype(f),
        "rank_w": np.tile(np.arange(EXPERTS, 0, -1, dtype=f), (P, 1)),
        "tile_lo": np.tile(np.arange(TILES, dtype=f) * P, (P, 1)),
        "tile_no": np.tile(np.arange(SLOT_TILES, dtype=f), (P, 1)),
        "lower": np.tile(np.tril(np.ones((EXPERTS, EXPERTS), f), -1).reshape(1, -1), (P, 1)),
        "token": token.astype(f)}
    weights1 = np.concatenate([parts[n] for n, _ in _WEIGHTS1], 1)

    ipb, aw = a["L0_attn_in_proj_b"], a["L1_attn_aW"]
    columns = np.stack([
        ipb[0:P], ipb[P:2 * P], ipb[2 * P:], a["L0_attn_pos_bias_u"].reshape(P), a["L0_attn_pos_bias_v"].reshape(P),
        a["L1_attn_tb"][0], a["L1_attn_tb"][1], a["L1_attn_cb"][0], a["L1_attn_cb"][1], aw[0:P], aw[P:2 * P],
        aw[2 * P:], a["L1_attn_frb"], a["L1_attn_ffb"], a["L1_ffn_ln1_g"], a["L1_ffn_ln1_b"], a["L1_ffn_bq"],
        a["L1_ffn_bk"], a["L1_ffn_bv"], np.broadcast_to(a["L1_attn_ab"], (P,))], 1)
    rows = np.concatenate([a["L0_tok_b"], a["L0_attn_out_proj_b"], a["L1_ffn_bo"], a["L1_ffn_gate_b"]])
    rows = np.broadcast_to(rows[None, :], (P, WIDTH_R))
    empty = np.zeros((SLOTS, ROW), f)
    empty[:, AT_TOKEN] = TOKENS + np.arange(SLOTS)
    return {
        "patches": pt, "weights": weights, "weights1": weights1, "columns": columns, "rows": rows,
        "b2_rows": np.broadcast_to(a["L1_ffn_b2"].reshape(1, EXPERTS * P), (P, EXPERTS * P)),
        "W1": np.concatenate([a["L1_ffn_W1"].transpose(1, 0, 2),
                              a["L1_ffn_b1"].reshape(EXPERTS, FC, P).transpose(2, 0, 1)], 2).reshape(P, EXPERTS * FIRST),
        "W2": a["L1_ffn_W2"].reshape(EXPERTS, FC, P, P).transpose(2, 0, 1, 3).reshape(P, EXPERTS * FC * P),
        "zeros": np.zeros((P, P), f), "empty": empty}


def kernel(x, **inputs):
    import concourse.bacc as _bacc
    from concourse.bass_utils import run_bass_kernel_spmd as _run

    nc = _bacc.Bacc("TRN2", target_bir_lowering=False, num_devices=1)
    arrays, args = {}, []
    for name, a in layout(x, inputs).items():
        a = np.ascontiguousarray(a)
        arrays[name] = a
        args.append(nc.dram_tensor(name, a.shape, mybir.dt.from_np(a.dtype), kind="ExternalInput").ap())
    args.append(nc.dram_tensor("out", (TOKENS + SLOTS, P), F32, kind="ExternalOutput").ap())
    for name, shape in (("bd_dram", (2, P, HEADS * REL)), ("hs_dram", (GROUPS * G, P)),
                        ("sorted_dram", (SLOTS, ROW))):
        args.append(nc.dram_tensor(name, shape, F32, kind="Internal").ap())
    tower(nc, *args)
    r = _run(nc, [arrays], core_ids=[0])
    return r.results[0]["out"][0:TOKENS].reshape(IMAGES, POSITIONS, P)
```
